# Optimizing a Trainium2 kernel written in Bass

```python
import numpy as np
import jax
import jax.numpy as jnp

def _softmax(x, axis=-1):
    return jax.nn.softmax(x, axis=axis)

def _gelu(x):
    return jax.nn.gelu(x, approximate=True)

def _silu(x):
    return jax.nn.silu(x)

def _sigmoid(x):
    return jax.nn.sigmoid(x)

def _layernorm(x, axis=-1, eps=1e-05):
    m = jnp.mean(x, axis=axis, keepdims=True)
    v = jnp.var(x, axis=axis, keepdims=True)
    return (x - m) / jnp.sqrt(v + eps)

def _scatter_add(tgt, idx, src, axis=0):
    return tgt.at[idx].add(src)

def _segment_sum(src, seg, n):
    return jax.ops.segment_sum(src, seg, n)
kernel_name = 'mk_lm_tower_d4_tok_ids1024_r4_126c99'

def setup_inputs(seed: int=0):
    np.random.seed(seed)
    _w = jnp.asarray

    def _rec_inputs():
        import jax
        import jax.numpy as jnp
        _rk = jax.random.key(seed)
        x = jax.random.randint(jax.random.fold_in(_rk, 1), (8, 256), 0, 12564, jnp.int32)
        return x
    x = _rec_inputs()

    def _L0_tok_setup():
        import jax, jax.numpy as jnp
        import numpy as np
        VOCAB, HID, RANK, MAX_LEN = (50257, 256, 32, 512)
        B, S = (32, 512)
        key = jax.random.key(seed)
        k1, k2, k3, k4, k5 = jax.random.split(key, 5)
        input_ids = jax.random.randint(k1, (B, S), 0, VOCAB)
        E1 = jax.random.normal(k2, (VOCAB, RANK), dtype=jnp.float32)
        W2 = jax.random.normal(k3, (HID, RANK), dtype=jnp.float32) / np.sqrt(RANK)
        b2 = jax.random.normal(k4, (HID,), dtype=jnp.float32) * 0.01
        pos_emb = jax.random.normal(k5, (1, MAX_LEN, HID), dtype=jnp.float32)
        return {'input_ids': input_ids, 'E1': E1, 'W2': W2, 'b2': b2, 'pos_emb': pos_emb}
    _L0_tok_all = _L0_tok_setup()
    _L0_tok_in = {k: v for k, v in _L0_tok_all.items() if k in ('E1', 'W2', 'b2', 'pos_emb')}
    del _L0_tok_all

    def _L0_attn_setup():
        import jax, jax.numpy as jnp
        import numpy as np
        key = jax.random.key(seed)
        ks = jax.random.split(key, 5)
        B, T, D = (4, 1024, 256)
        x = jax.random.normal(ks[0], (B, T, D), dtype=jnp.float32)
        Wqkv = jax.random.normal(ks[1], (D, 3 * D), dtype=jnp.float32) * D ** (-0.5)
        bqkv = jax.random.normal(ks[2], (3 * D,), dtype=jnp.float32) * 0.02
        Wout = jax.random.normal(ks[3], (D, D), dtype=jnp.float32) * D ** (-0.5)
        bout = jax.random.normal(ks[4], (D,), dtype=jnp.float32) * 0.02
        return {'x': x, 'Wqkv': Wqkv, 'bqkv': bqkv, 'Wout': Wout, 'bout': bout}
    _L0_attn_all = _L0_attn_setup()
    _L0_attn_in = {k: v for k, v in _L0_attn_all.items() if k in ('Wqkv', 'bqkv', 'Wout', 'bout')}
    del _L0_attn_all

    def _L0_ffn_setup():
        import jax, jax.numpy as jnp
        import numpy as np
        import math
        D_IN = 256
        FEATURES = (1024, 1024, 256)
        BATCH, SEQ = (8, 512)

        def _conn_dense(kernel_bool, x):
            w = jnp.where(kernel_bool, jnp.float32(1.0), jnp.float32(-1.0))
            return x @ w
        key = jax.random.key(seed)
        kx, kk0, kk1, kk2 = jax.random.split(key, 4)
        x = jax.random.normal(kx, (BATCH, SEQ, D_IN), dtype=jnp.float32)
        k0 = jax.random.randint(kk0, (2 * D_IN, FEATURES[0]), 0, 2).astype(jnp.bool_)
        k1 = jax.random.randint(kk1, (FEATURES[0], FEATURES[1]), 0, 2).astype(jnp.bool_)
        k2 = jax.random.randint(kk2, (FEATURES[1], FEATURES[2]), 0, 2).astype(jnp.bool_)
        s0 = jnp.asarray(1.0 / math.sqrt(2 * D_IN), dtype=jnp.float32)
        s1 = jnp.asarray(1.0 / math.sqrt(FEATURES[0]), dtype=jnp.float32)
        s2 = jnp.asarray(1.0 / math.sqrt(FEATURES[1]), dtype=jnp.float32)
        return {'x': x, 'k0': k0, 'k1': k1, 'k2': k2, 's0': s0, 's1': s1, 's2': s2}
    _L0_ffn_all = _L0_ffn_setup()
    _L0_ffn_in = {k: v for k, v in _L0_ffn_all.items() if k in ('k0', 'k1', 'k2', 's0', 's1', 's2')}
    del _L0_ffn_all

    def _L1_attn_setup():
        import jax, jax.numpy as jnp
        import numpy as np
        HID = 256
        EXP = 1024

        def _min_gru(x_in, Wz, bz, Wh, bh):
            z = jax.nn.sigmoid(jnp.einsum('bse,ef->bsf', x_in, Wz) + bz)
            h_tilde = jnp.einsum('bse,ef->bsf', x_in, Wh) + bh
            a = 1.0 - z
            b = z * h_tilde

            def combine(c1, c2):
                a1, b1 = c1
                a2, b2 = c2
                return (a2 * a1, a2 * b1 + b2)
            _, h = jax.lax.associative_scan(combine, (a, b), axis=1)
            return h
        key = jax.random.key(seed)
        ks = jax.random.split(key, 11)
        s = lambda fan_in: 1.0 / np.sqrt(fan_in)
        return {'x': jax.random.normal(ks[0], (4, 512, HID), dtype=jnp.float32), 'W1': jax.random.uniform(ks[1], (HID, EXP), jnp.float32, -s(HID), s(HID)), 'b1': jax.random.uniform(ks[2], (EXP,), jnp.float32, -s(HID), s(HID)), 'W2': jax.random.uniform(ks[3], (HID, EXP), jnp.float32, -s(HID), s(HID)), 'b2': jax.random.uniform(ks[4], (EXP,), jnp.float32, -s(HID), s(HID)), 'Wz': jax.random.uniform(ks[5], (EXP, EXP), jnp.float32, -s(EXP), s(EXP)), 'bz': jax.random.uniform(ks[6], (EXP,), jnp.float32, -s(EXP), s(EXP)), 'Wh': jax.random.uniform(ks[7], (EXP, EXP), jnp.float32, -s(EXP), s(EXP)), 'bh': jax.random.uniform(ks[8], (EXP,), jnp.float32, -s(EXP), s(EXP)), 'Wo': jax.random.uniform(ks[9], (EXP, HID), jnp.float32, -s(EXP), s(EXP)), 'bo': jax.random.uniform(ks[10], (HID,), jnp.float32, -s(EXP), s(EXP))}
    _L1_attn_all = _L1_attn_setup()
    _L1_attn_in = {k: v for k, v in _L1_attn_all.items() if k in ('W1', 'b1', 'W2', 'b2', 'Wz', 'bz', 'Wh', 'bh', 'Wo', 'bo')}
    del _L1_attn_all

    def _L1_ffn_setup():
        import jax, jax.numpy as jnp
        import numpy as np
        B, S, D = (1, 512, 256)
        F = 352
        E = 16
        K = 2
        CAP_FACTOR = 1.25

        def _mlp(h, wg, wu, wd):
            return jax.nn.silu(h @ wg) * (h @ wu) @ wd
        key = jax.random.key(seed)
        ks = jax.random.split(key, 10)
        sd = 0.02
        return {'x': jax.random.normal(ks[0], (B, S, D), jnp.float32), 'router_w': jax.random.normal(ks[1], (D, E), jnp.float32) * sd, 'router_b': jnp.zeros((E,), jnp.float32), 'w_gate': jax.random.normal(ks[2], (E, D, F), jnp.float32) * sd, 'w_up': jax.random.normal(ks[3], (E, D, F), jnp.float32) * sd, 'w_down': jax.random.normal(ks[4], (E, F, D), jnp.float32) * sd, 'sw_gate': jax.random.normal(ks[5], (D, F), jnp.float32) * sd, 'sw_up': jax.random.normal(ks[6], (D, F), jnp.float32) * sd, 'sw_down': jax.random.normal(ks[7], (F, D), jnp.float32) * sd}
    _L1_ffn_all = _L1_ffn_setup()
    _L1_ffn_in = {k: v for k, v in _L1_ffn_all.items() if k in ('router_w', 'router_b', 'w_gate', 'w_up', 'w_down', 'sw_gate', 'sw_up', 'sw_down')}
    del _L1_ffn_all

    def _L2_attn_setup():
        import jax, jax.numpy as jnp
        import numpy as np
        SEQ, BATCH, HIDDEN = (512, 2, 256)
        NUM_HEADS, HEAD_DIM = (16, 64)
        LN_EPS = 1e-06
        NEG_INF = -10000000000.0
        key = jax.random.key(seed)
        k1, k2, k3 = jax.random.split(key, 3)
        inputs_q = jax.random.normal(k1, (SEQ, BATCH, HIDDEN), dtype=jnp.float32)
        ln_scale = jnp.ones((HIDDEN,), dtype=jnp.float32)
        ln_bias = jnp.zeros((HIDDEN,), dtype=jnp.float32)
        qkv_kernel = jax.random.normal(k2, (HIDDEN, 3, NUM_HEADS * HEAD_DIM), dtype=jnp.float32) / np.sqrt(HIDDEN).astype(np.float32)
        out_kernel = jax.random.normal(k3, (NUM_HEADS * HEAD_DIM, HIDDEN), dtype=jnp.float32) / np.sqrt(NUM_HEADS * HEAD_DIM).astype(np.float32)
        return {'inputs_q': inputs_q, 'ln_scale': ln_scale, 'ln_bias': ln_bias, 'qkv_kernel': qkv_kernel, 'out_kernel': out_kernel}
    _L2_attn_all = _L2_attn_setup()
    _L2_attn_in = {k: v for k, v in _L2_attn_all.items() if k in ('ln_scale', 'ln_bias', 'qkv_kernel', 'out_kernel')}
    del _L2_attn_all

    def _L2_ffn_setup():
        import jax, jax.numpy as jnp
        import numpy as np
        B, S, DIM, FFN, E = (4, 512, 256, 1024, 8)
        key = jax.random.key(seed)
        k0, k1, k2, k3 = jax.random.split(key, 4)
        scale = 0.02
        return {'hidden_states': jax.random.normal(k0, (B, S, DIM), jnp.float32), 'router_w': jax.random.normal(k1, (DIM, E), jnp.float32) * scale, 'router_b': jnp.zeros((E,), jnp.float32), 'w1': jax.random.normal(k2, (E, DIM, 2 * FFN), jnp.float32) * scale, 'w2': jax.random.normal(k3, (E, FFN, DIM), jnp.float32) * scale}
    _L2_ffn_all = _L2_ffn_setup()
    _L2_ffn_in = {k: v for k, v in _L2_ffn_all.items() if k in ('router_w', 'router_b', 'w1', 'w2')}
    del _L2_ffn_all

    def _L3_attn_setup():
        import jax, jax.numpy as jnp
        import numpy as np
        DIM = 256
        NUM_HEADS = 16
        HEAD_DIM = DIM // NUM_HEADS
        SCALE = 1.0 / float(np.sqrt(HEAD_DIM))
        key = jax.random.key(seed)
        kx, kw1, kb1, kw2, kb2 = jax.random.split(key, 5)
        b, l = (2, 512)
        s = 1.0 / np.sqrt(DIM)
        return {'x': jax.random.normal(kx, (b, l, DIM), dtype=jnp.float32), 'w_qkv': jax.random.uniform(kw1, (DIM, 3 * DIM), jnp.float32, -s, s), 'b_qkv': jax.random.uniform(kb1, (3 * DIM,), jnp.float32, -s, s), 'w_proj': jax.random.uniform(kw2, (DIM, DIM), jnp.float32, -s, s), 'b_proj': jax.random.uniform(kb2, (DIM,), jnp.float32, -s, s)}
    _L3_attn_all = _L3_attn_setup()
    _L3_attn_in = {k: v for k, v in _L3_attn_all.items() if k in ('w_qkv', 'b_qkv', 'w_proj', 'b_proj')}
    del _L3_attn_all

    def _L3_ffn_setup():
        import jax, jax.numpy as jnp
        import numpy as np
        DIM = 256
        HIDDEN = 768
        SCALE = 1.0 / 127.0

        def _dequant(w_int, dtype):
            return w_int.astype(dtype) * jnp.asarray(SCALE, dtype)
        key = jax.random.key(seed)
        k_x, k_g, k_u, k_d = jax.random.split(key, 4)
        x = jax.random.normal(k_x, (4, 512, DIM), dtype=jnp.float32)
        w_gate = jax.random.randint(k_g, (HIDDEN, DIM), -127, 128, dtype=jnp.int32)
        w_up = jax.random.randint(k_u, (HIDDEN, DIM), -127, 128, dtype=jnp.int32)
        w_down = jax.random.randint(k_d, (DIM, HIDDEN), -127, 128, dtype=jnp.int32)
        return {'x': x, 'w_gate': w_gate, 'w_up': w_up, 'w_down': w_down}
    _L3_ffn_all = _L3_ffn_setup()
    _L3_ffn_in = {k: v for k, v in _L3_ffn_all.items() if k in ('w_gate', 'w_up', 'w_down')}
    del _L3_ffn_all
    return {'x': x, 'L0_tok_E1': _L0_tok_in['E1'], 'L0_tok_W2': _L0_tok_in['W2'], 'L0_tok_b2': _L0_tok_in['b2'], 'L0_tok_pos_emb': _L0_tok_in['pos_emb'], 'L0_attn_Wqkv': _L0_attn_in['Wqkv'], 'L0_attn_bqkv': _L0_attn_in['bqkv'], 'L0_attn_Wout': _L0_attn_in['Wout'], 'L0_attn_bout': _L0_attn_in['bout'], 'L0_ffn_k0': _L0_ffn_in['k0'], 'L0_ffn_k1': _L0_ffn_in['k1'], 'L0_ffn_k2': _L0_ffn_in['k2'], 'L0_ffn_s0': _L0_ffn_in['s0'], 'L0_ffn_s1': _L0_ffn_in['s1'], 'L0_ffn_s2': _L0_ffn_in['s2'], 'L1_attn_W1': _L1_attn_in['W1'], 'L1_attn_b1': _L1_attn_in['b1'], 'L1_attn_W2': _L1_attn_in['W2'], 'L1_attn_b2': _L1_attn_in['b2'], 'L1_attn_Wz': _L1_attn_in['Wz'], 'L1_attn_bz': _L1_attn_in['bz'], 'L1_attn_Wh': _L1_attn_in['Wh'], 'L1_attn_bh': _L1_attn_in['bh'], 'L1_attn_Wo': _L1_attn_in['Wo'], 'L1_attn_bo': _L1_attn_in['bo'], 'L1_ffn_router_w': _L1_ffn_in['router_w'], 'L1_ffn_router_b': _L1_ffn_in['router_b'], 'L1_ffn_w_gate': _L1_ffn_in['w_gate'], 'L1_ffn_w_up': _L1_ffn_in['w_up'], 'L1_ffn_w_down': _L1_ffn_in['w_down'], 'L1_ffn_sw_gate': _L1_ffn_in['sw_gate'], 'L1_ffn_sw_up': _L1_ffn_in['sw_up'], 'L1_ffn_sw_down': _L1_ffn_in['sw_down'], 'L2_attn_ln_scale': _L2_attn_in['ln_scale'], 'L2_attn_ln_bias': _L2_attn_in['ln_bias'], 'L2_attn_qkv_kernel': _L2_attn_in['qkv_kernel'], 'L2_attn_out_kernel': _L2_attn_in['out_kernel'], 'L2_ffn_router_w': _L2_ffn_in['router_w'], 'L2_ffn_router_b': _L2_ffn_in['router_b'], 'L2_ffn_w1': _L2_ffn_in['w1'], 'L2_ffn_w2': _L2_ffn_in['w2'], 'L3_attn_w_qkv': _L3_attn_in['w_qkv'], 'L3_attn_b_qkv': _L3_attn_in['b_qkv'], 'L3_attn_w_proj': _L3_attn_in['w_proj'], 'L3_attn_b_proj': _L3_attn_in['b_proj'], 'L3_ffn_w_gate': _L3_ffn_in['w_gate'], 'L3_ffn_w_up': _L3_ffn_in['w_up'], 'L3_ffn_w_down': _L3_ffn_in['w_down']}

def reference(x, L0_tok_E1, L0_tok_W2, L0_tok_b2, L0_tok_pos_emb, L0_attn_Wqkv, L0_attn_bqkv, L0_attn_Wout, L0_attn_bout, L0_ffn_k0, L0_ffn_k1, L0_ffn_k2, L0_ffn_s0, L0_ffn_s1, L0_ffn_s2, L1_attn_W1, L1_attn_b1, L1_attn_W2, L1_attn_b2, L1_attn_Wz, L1_attn_bz, L1_attn_Wh, L1_attn_bh, L1_attn_Wo, L1_attn_bo, L1_ffn_router_w, L1_ffn_router_b, L1_ffn_w_gate, L1_ffn_w_up, L1_ffn_w_down, L1_ffn_sw_gate, L1_ffn_sw_up, L1_ffn_sw_down, L2_attn_ln_scale, L2_attn_ln_bias, L2_attn_qkv_kernel, L2_attn_out_kernel, L2_ffn_router_w, L2_ffn_router_b, L2_ffn_w1, L2_ffn_w2, L3_attn_w_qkv, L3_attn_b_qkv, L3_attn_w_proj, L3_attn_b_proj, L3_ffn_w_gate, L3_ffn_w_up, L3_ffn_w_down):
    import jax
    import jax.numpy as jnp

    def _L0_tok_ref(input_ids, E1, W2, b2, pos_emb):
        import jax, jax.numpy as jnp
        import numpy as np
        VOCAB, HID, RANK, MAX_LEN = (50257, 256, 32, 512)
        B, S = (32, 512)
        x = E1[input_ids]
        x = jnp.einsum('bsr,hr->bsh', x, W2) + b2
        S_ = input_ids.shape[1]
        return x + pos_emb[:, :S_]

    def _L0_attn_ref(x, Wqkv, bqkv, Wout, bout):
        import jax, jax.numpy as jnp
        import numpy as np
        qkv = jnp.einsum('btd,de->bte', x, Wqkv) + bqkv
        q, k, v = jnp.split(qkv, 3, axis=-1)
        q = q / jnp.linalg.norm(q, axis=-1, keepdims=True)
        k = k / jnp.linalg.norm(k, axis=-1, keepdims=True)
        kv = jnp.sum(k * v, axis=-2, keepdims=True)
        out = q * kv
        return jnp.einsum('btd,de->bte', out, Wout) + bout

    def _L0_ffn_ref(x, k0, k1, k2, s0, s1, s2):
        import jax, jax.numpy as jnp
        import numpy as np
        import math
        D_IN = 256
        FEATURES = (1024, 1024, 256)
        BATCH, SEQ = (8, 512)

        def _conn_dense(kernel_bool, x):
            w = jnp.where(kernel_bool, jnp.float32(1.0), jnp.float32(-1.0))
            return x @ w
        h = jnp.concatenate([x, -x], axis=-1)
        h = s0 * _conn_dense(k0, h)
        h = jax.nn.relu(h) * 2
        h = s1 * _conn_dense(k1, h)
        h = jax.nn.relu(h) * 2
        h = s2 * _conn_dense(k2, h)
        return h

    def _L1_attn_ref(x, W1, b1, W2, b2, Wz, bz, Wh, bh, Wo, bo):
        import jax, jax.numpy as jnp
        import numpy as np
        HID = 256
        EXP = 1024

        def _min_gru(x_in, Wz, bz, Wh, bh):
            z = jax.nn.sigmoid(jnp.einsum('bse,ef->bsf', x_in, Wz) + bz)
            h_tilde = jnp.einsum('bse,ef->bsf', x_in, Wh) + bh
            a = 1.0 - z
            b = z * h_tilde

            def combine(c1, c2):
                a1, b1 = c1
                a2, b2 = c2
                return (a2 * a1, a2 * b1 + b2)
            _, h = jax.lax.associative_scan(combine, (a, b), axis=1)
            return h
        x_in = jax.nn.silu(jnp.einsum('bsd,de->bse', x, W1) + b1)
        x_skip = jax.nn.silu(jnp.einsum('bsd,de->bse', x, W2) + b2)
        h = _min_gru(x_in, Wz, bz, Wh, bh)
        return jnp.einsum('bse,ed->bsd', x_skip + h, Wo) + bo

    def _L1_ffn_ref(x, router_w, router_b, w_gate, w_up, w_down, sw_gate, sw_up, sw_down):
        import jax, jax.numpy as jnp
        import numpy as np
        B, S, D = (1, 512, 256)
        F = 352
        E = 16
        K = 2
        CAP_FACTOR = 1.25

        def _mlp(h, wg, wu, wd):
            return jax.nn.silu(h @ wg) * (h @ wu) @ wd
        b, s, d = x.shape
        N = b * s
        NK = N * K
        C = int(np.ceil(CAP_FACTOR * NK / E))
        x_tokens = x.reshape(N, d)
        logits = x_tokens @ router_w + router_b
        probs = jax.nn.softmax(logits, axis=-1)
        vals, idx = jax.lax.top_k(probs, K)
        vals = vals / (jnp.sum(vals, axis=-1, keepdims=True) + 1e-09)
        idx_flat = idx.reshape(NK)
        vals_flat = vals.reshape(NK)
        oh_e = jax.nn.one_hot(idx_flat, E, dtype=x.dtype)
        pos = (jnp.cumsum(oh_e, axis=0) * oh_e).sum(axis=1) - 1
        within = (pos < C).astype(x.dtype)
        pos_c = jnp.clip(pos, 0, C - 1).astype(jnp.int32)
        token_ids = jnp.arange(NK) // K
        x_pair = x_tokens[token_ids] * within[:, None]
        expert_inputs = jnp.zeros((E, C, d), x.dtype).at[idx_flat, pos_c].add(x_pair)
        expert_outputs = jax.vmap(_mlp)(expert_inputs, w_gate, w_up, w_down)
        gathered = expert_outputs[idx_flat, pos_c] * (vals_flat * within)[:, None]
        output_tokens = gathered.reshape(N, K, d).sum(axis=1)
        return x + _mlp(x, sw_gate, sw_up, sw_down) + output_tokens.reshape(b, s, d)

    def _L2_attn_ref(inputs_q, ln_scale, ln_bias, qkv_kernel, out_kernel):
        import jax, jax.numpy as jnp
        import numpy as np
        SEQ, BATCH, HIDDEN = (512, 2, 256)
        NUM_HEADS, HEAD_DIM = (16, 64)
        LN_EPS = 1e-06
        NEG_INF = -10000000000.0
        s, b, h = inputs_q.shape
        mu = jnp.mean(inputs_q, axis=-1, keepdims=True)
        var = jnp.mean(jnp.square(inputs_q - mu), axis=-1, keepdims=True)
        ln_out = (inputs_q - mu) * jax.lax.rsqrt(var + LN_EPS) * ln_scale + ln_bias
        qkv = jnp.einsum('sbh,htk->stbk', ln_out, qkv_kernel)
        q = qkv[:, 0].reshape(s, b, NUM_HEADS, HEAD_DIM)
        k = qkv[:, 1].reshape(s, b, NUM_HEADS, HEAD_DIM)
        v = qkv[:, 2].reshape(s, b, NUM_HEADS, HEAD_DIM)
        scale = 1.0 / np.sqrt(HEAD_DIM).astype(np.float32)
        logits = jnp.einsum('qbhd,kbhd->bhqk', q, k) * scale
        causal = jnp.tril(jnp.ones((s, s), dtype=bool))
        logits = jnp.where(causal[None, None], logits, jnp.asarray(NEG_INF, logits.dtype))
        attn = jax.nn.softmax(logits, axis=-1)
        ctx = jnp.einsum('bhqk,kbhd->qbhd', attn, v).reshape(s, b, NUM_HEADS * HEAD_DIM)
        return jnp.einsum('sbk,kh->sbh', ctx, out_kernel)

    def _L2_ffn_ref(hidden_states, router_w, router_b, w1, w2):
        import jax, jax.numpy as jnp
        import numpy as np
        B, S, DIM, FFN, E = (4, 512, 256, 1024, 8)
        b, s, d = hidden_states.shape
        x = hidden_states.reshape(-1, d)
        logits = x @ router_w + router_b
        route = jax.nn.softmax(logits, axis=1)
        max_prob = jnp.max(route, axis=1, keepdims=True)
        max_ind = jnp.argmax(route, axis=1)
        out = jnp.zeros_like(x)
        num_experts = w1.shape[0]
        for e in range(num_experts):
            h = x @ w1[e]
            a, g = jnp.split(h, 2, axis=1)
            y = jax.nn.silu(a) * g @ w2[e]
            out = jnp.where((max_ind == e)[:, None], y, out)
        out = out * max_prob
        return out.reshape(b, s, d)

    def _L3_attn_ref(x, w_qkv, b_qkv, w_proj, b_proj):
        import jax, jax.numpy as jnp
        import numpy as np
        DIM = 256
        NUM_HEADS = 16
        HEAD_DIM = DIM // NUM_HEADS
        SCALE = 1.0 / float(np.sqrt(HEAD_DIM))
        b, l, c = x.shape
        n, d = (NUM_HEADS, HEAD_DIM)
        qkv = x @ w_qkv + b_qkv
        qkv = qkv.reshape(b, l, 3 * n, d)
        q, k, v = (qkv[:, :, :n], qkv[:, :, n:2 * n], qkv[:, :, 2 * n:])
        attn = SCALE * jnp.einsum('binc,bjnc->bnij', q, k)
        attn = jax.nn.softmax(attn.astype(jnp.float32), axis=-1).astype(q.dtype)
        out = jnp.einsum('bnij,bjnc->binc', attn, v)
        out = out.reshape(b, l, c)
        return out @ w_proj + b_proj

    def _L3_ffn_ref(x, w_gate, w_up, w_down):
        import jax, jax.numpy as jnp
        import numpy as np
        DIM = 256
        HIDDEN = 768
        SCALE = 1.0 / 127.0

        def _dequant(w_int, dtype):
            return w_int.astype(dtype) * jnp.asarray(SCALE, dtype)
        wg = _dequant(w_gate, x.dtype)
        wu = _dequant(w_up, x.dtype)
        wd = _dequant(w_down, x.dtype)
        gate = jnp.einsum('bsd,hd->bsh', x, wg)
        up = jnp.einsum('bsd,hd->bsh', x, wu)
        h = jax.nn.silu(gate) * up
        return jnp.einsum('bsh,dh->bsd', h, wd)
    h = _L0_tok_ref(x, L0_tok_E1, L0_tok_W2, L0_tok_b2, L0_tok_pos_emb)
    h = h + _L0_attn_ref(_layernorm(h, axis=-1), L0_attn_Wqkv, L0_attn_bqkv, L0_attn_Wout, L0_attn_bout)
    h = h + _L0_ffn_ref(_layernorm(h, axis=-1), L0_ffn_k0, L0_ffn_k1, L0_ffn_k2, L0_ffn_s0, L0_ffn_s1, L0_ffn_s2)
    h = h + _L1_attn_ref(_layernorm(h, axis=-1), L1_attn_W1, L1_attn_b1, L1_attn_W2, L1_attn_b2, L1_attn_Wz, L1_attn_bz, L1_attn_Wh, L1_attn_bh, L1_attn_Wo, L1_attn_bo)
    h = h + _L1_ffn_ref(_layernorm(h, axis=-1), L1_ffn_router_w, L1_ffn_router_b, L1_ffn_w_gate, L1_ffn_w_up, L1_ffn_w_down, L1_ffn_sw_gate, L1_ffn_sw_up, L1_ffn_sw_down)
    h = h + _L2_attn_ref(_layernorm(h, axis=-1), L2_attn_ln_scale, L2_attn_ln_bias, L2_attn_qkv_kernel, L2_attn_out_kernel)
    h = h + _L2_ffn_ref(_layernorm(h, axis=-1), L2_ffn_router_w, L2_ffn_router_b, L2_ffn_w1, L2_ffn_w2)
    h = h + _L3_attn_ref(_layernorm(h, axis=-1), L3_attn_w_qkv, L3_attn_b_qkv, L3_attn_w_proj, L3_attn_b_proj)
    h = h + _L3_ffn_ref(_layernorm(h, axis=-1), L3_ffn_w_gate, L3_ffn_w_up, L3_ffn_w_down)
    return h

_drawn_inputs = setup_inputs


def setup_inputs(seed=0):
    import zlib

    import numpy as np

    out = dict(_drawn_inputs(seed))
    spreads = {'L1_ffn_router_b': (0.0, 0.8),
     'L2_attn_ln_scale': (1.0, 0.2),
     'L2_attn_ln_bias': (0.0, 0.1),
     'L2_ffn_router_b': (0.0, 0.8)}
    factors = {'L0_tok_b2': 5.922,
     'L0_attn_bqkv': 8.0,
     'L0_attn_bout': 2.872,
     'L1_attn_b1': 8.0,
     'L1_attn_b2': 8.0,
     'L1_attn_Wz': 8.0,
     'L1_attn_bz': 8.0,
     'L1_attn_bh': 8.0,
     'L1_attn_bo': 4.758,
     'L1_ffn_router_w': 8.0,
     'L1_ffn_w_gate': 8.0,
     'L1_ffn_w_up': 8.0,
     'L1_ffn_w_down': 8.0,
     'L1_ffn_sw_gate': 7.134,
     'L1_ffn_sw_up': 6.945,
     'L1_ffn_sw_down': 6.981,
     'L2_ffn_router_w': 8.0,
     'L2_ffn_w1': 8.0,
     'L2_ffn_w2': 8.0,
     'L3_attn_b_qkv': 29.298,
     'L3_attn_b_proj': 19.278,
     'L3_attn_w_qkv': 8.0,
     'L3_attn_w_proj': 4.463}
    for name, (base, spread) in spreads.items():
        noise = np.random.default_rng([zlib.crc32(name.encode()), seed]).standard_normal(out[name].shape)
        drawn = base * np.exp(spread * noise) if base else spread * noise
        out[name] = jnp.asarray(drawn.astype(out[name].dtype))
    for name, factor in factors.items():
        out[name] = (out[name] * factor).astype(out[name].dtype)
    return out
```

```python
from contextlib import ExitStack

import numpy as np

import concourse.bass as bass
from concourse import mybir

ALU = mybir.AluOpType
ACT = mybir.ActivationFunctionType
AX_X = mybir.AxisListType.X
F32 = mybir.dt.float32
BF16 = mybir.dt.bfloat16
F32R = mybir.dt.float32r
I32 = mybir.dt.int32
U8 = mybir.dt.uint8
ds = bass.ds

P = 128
BATCH, SEQ, D = 8, 256, 256
N = BATCH * SEQ
TILES = N // P
TPB = SEQ // P
DC = D // P
RANK = 32
LN_EPS = 1e-5


class Scope:

    def __init__(self, nc, ctx, prefix, stage=None):
        self.nc, self.ctx, self.prefix = nc, ctx, prefix
        self.sems = [] if stage is None else stage.sems

    def sb(self, name, shape, dt=F32):
        return self.ctx.enter_context(self.nc.sbuf_tensor(f"{self.prefix}_{name}", shape, dt))

    def sem(self, name):
        self.sems.append(self.ctx.enter_context(self.nc.semaphore(f"{self.prefix}_{name}")))
        return self.sems[-1]

    def clear(self):
        with self.nc.Block() as block:
            @block.gpsimd
            def _(pool):
                for sem in self.sems:
                    pool.sem_clear(sem)


class Chain:

    def __init__(self, eng, sem, base=0):
        self.eng, self.sem, self.base, self.steps = eng, sem, base, 0

    def __call__(self, ins):
        self.steps += 1
        ins.then_inc(self.sem, 1)
        self.eng.wait_ge(self.sem, self.base + self.steps)


class Core:

    def __init__(self, nc, ctx):
        s = Scope(nc, ctx, "core")
        self.pool_dma = Scope(nc, ctx, "pool_dma")
        self.h = s.sb("h", [P, TILES + TPB, D])
        self.xr = s.sb("xr", [P, TPB, D])
        self.xT = s.sb("xT", [P, DC, SEQ])
        self.ident = s.sb("ident", [P, P])
        self.ones = s.sb("ones", [P, P])
        self.neg_half = s.sb("neg_half", [P, TILES])
        self.ps = ctx.enter_context(nc.psum_tensor("ps", [P, 8, 512], F32))


class RowNorm:

    BANK = 7
    STEPS = 8

    def __init__(self, nc, core, s, eps=LN_EPS, again=None, affine=None):
        self.core, self.again, self.affine = core, again, affine
        self.eps = [eps] if again is None else [eps, again]
        self.stats = s.sb("norm_stats", [P, TPB, 6])
        self.mean = s.sb("norm_mean", [P, TPB])
        self.diff = s.sb("norm_diff", [P, TPB])
        self.var_eps = s.sb("norm_var_eps", [P, TPB])
        self.rstd = s.sb("norm_rstd", [P, TPB])
        self.step = s.sem("norm_step")
        self.var_ready = s.sem("norm_var_ready")
        self.rstd_ready = s.sem("norm_rstd_ready")
        self.row_normed = s.sem("norm_row_normed")
        self.turned = s.sem("norm_turned")
        self.xT_ready = s.sem("norm_xT_ready")
        self.low_ready = s.sem("norm_low_ready")

    def norm(self, dve, r, first=False):
        n = len(self.eps)
        xr = self.core.xr
        stats, mean, diff, var = self.stats, self.mean, self.diff, self.var_eps
        step = Chain(dve, self.step, r * self.STEPS * n)
        for k, eps in enumerate(self.eps):
            src = self.core.h[:, ds(r * TPB, TPB), :] if k == 0 else xr[:, :, :]
            for t in range(TPB):
                ins = dve.bn_stats(stats[:, t, :], src[:, t, :])
                if t == 0:
                    ins.then_inc(self.step, 1)
            step.steps += 1
            step(ins)
            dve.tensor_tensor(mean[:, :], stats[:, :, 1], stats[:, :, 4], ALU.add).then_inc(self.step, 1)
            dve.tensor_tensor(var[:, :], stats[:, :, 2], stats[:, :, 5], ALU.add).then_inc(self.step, 1)
            step.steps += 2
            step(dve.tensor_tensor(diff[:, :], stats[:, :, 1], stats[:, :, 4], ALU.subtract))
            dve.tensor_scalar(mean[:, :], mean[:, :], 0.5, None, ALU.mult).then_inc(self.step, 1)
            step.steps += 1
            step(dve.scalar_tensor_tensor(out=diff[:, :], in0=diff[:, :], scalar=D / 4.0, in1=diff[:, :],
                                          op0=ALU.mult, op1=ALU.mult))
            step(dve.tensor_tensor(var[:, :], var[:, :], diff[:, :], ALU.add))
            dve.tensor_scalar(var[:, :], var[:, :], 1.0 / D, eps, ALU.mult, ALU.add).then_inc(self.var_ready, 1)
            dve.wait_ge(self.rstd_ready, r * n + k + 1)
            if k == 0 and not first:
                dve.wait_ge(self.turned, r)
            for t in range(TPB):
                ins = dve.tensor_scalar(xr[:, t, :], src[:, t, :], mean[:, t:t + 1], self.rstd[:, t:t + 1],
                                        ALU.subtract, ALU.mult).then_inc(self.row_normed, 1)
            if k < n - 1:
                dve.wait_ge(self.row_normed, (r * n + k + 1) * TPB)
        assert step.steps == self.STEPS * n

    def root(self, pool, r):
        n = len(self.eps)
        for k in range(n):
            pool.wait_ge(self.var_ready, r * n + k + 1)
            pool.tensor_tensor(self.rstd[:, :], self.var_eps[:, :], self.core.neg_half[:, 0:TPB],
                               ALU.pow).then_inc(self.rstd_ready, 1)

    def turn(self, pe, r):
        pe.wait_ge(self.row_normed, (r + 1) * (TPB * len(self.eps)))
        for c in range(DC):
            for t in range(TPB):
                last = pe.transpose(self.core.ps[:, self.BANK, c * SEQ + t * P:c * SEQ + (t + 1) * P],
                                    self.core.xr[:, t, c * P:(c + 1) * P], self.core.ident[:, :])
        last.then_inc(self.turned, 1)

    def evacuate(self, act, r, out=None):
        out = self.core.xT[:, :, :] if out is None else out
        turned = self.core.ps[:, self.BANK, :].rearrange("p (c n) -> p c n", c=DC)
        act.wait_ge(self.turned, r + 1)
        if self.affine is None:
            act.activation(out, turned, ACT.Copy).then_inc(self.xT_ready, 1)
        else:
            gain, shift = self.affine
            act.activation(out[:, 0, :], turned[:, 0, :], ACT.Identity, bias=shift[:, 0:1], scale=gain[:, 0:1])
            act.activation(out[:, 1, :], turned[:, 1, :], ACT.Identity, bias=shift[:, 1:2],
                           scale=gain[:, 1:2]).then_inc(self.xT_ready, 1)


    def low(self, dve, r, high, low):
        dve.wait_ge(self.xT_ready, r + 1)
        dve.tensor_tensor(low[:, :, :], self.core.ps[:, self.BANK, :].rearrange("p (c n) -> p c n", c=DC),
                          high[:, :, :].bitcast(F32), ALU.subtract).then_inc(self.low_ready, 1)


def constants(nc, core):
    with ExitStack() as ctx:
        s = Scope(nc, ctx, "const")
        ident_zero = s.sem("ident_zero")
        made = s.sem("made")
        with nc.Block() as block:
            @block.gpsimd
            def _(pool):
                pool.memset(core.ident[:, :], 0.0).then_inc(ident_zero, 1)
                pool.memset(core.ones[:, :], 1.0).then_inc(made, 1)
                pool.memset(core.neg_half[:, :], -0.5).then_inc(made, 1)
                pool.memset(core.h[:, TILES:TILES + TPB, :], 0.0).then_inc(made, 1)
                pool.wait_ge(ident_zero, 1)
                pool.affine_select(out=core.ident[:, :], in_=core.ident[:, :], compare_op=ALU.not_equal,
                                   fill=1.0, base=0, pattern=[[-1, P]], channel_multiplier=1).then_inc(made, 1)
                pool.wait_ge(made, 4)
        s.clear()


def embed(nc, core, ids_d, E1_d, W2T_d, b2_d, pos_d):
    ps = core.ps
    with ExitStack() as ctx:
        s = Scope(nc, ctx, "tok")
        ids = s.sb("ids", [P, TILES], I32)
        rows = s.sb("rows", [P, TILES, RANK])
        rowsT = s.sb("rowsT", [RANK, N])
        W2T = s.sb("W2T", [RANK, D])
        b2 = s.sb("b2", [P, D])
        pos = s.sb("pos", [P, TPB, D])
        ids_in = s.sem("ids_in")
        params_in = s.sem("params_in")
        rows_in = core.pool_dma.sem("table_rows_in")
        rows_turned = s.sem("rows_turned")
        rowsT_ready = s.sem("rowsT_ready")
        pos_ready = s.sem("pos_ready")
        bank_full = s.sem("bank_full")
        bank_free = s.sem("bank_free")

        with nc.Block() as block:
            @block.sync
            def _(sp):
                sp.dma_start(ids[:, :], ids_d).then_inc(ids_in, 16)
                sp.dma_start(W2T[:, :], W2T_d).then_inc(params_in, 16)
                sp.dma_start(pos[:, :, :], pos_d[0, 0:SEQ, :].rearrange("(t p) d -> p t d", p=P)).then_inc(params_in, 16)
                sp.dma_start(b2[:, :], b2_d.partition_broadcast(P)).then_inc(params_in, 16)

            @block.gpsimd
            def _(pool):
                pool.wait_ge(ids_in, 16)
                for t in range(TILES):
                    pool.indirect_dma_start(rows[:, t, :], None, E1_d,
                                            bass.IndirectOffsetOnAxis(ap=ids[:, t:t + 1], axis=0)).then_inc(rows_in, 16)

            @block.tensor
            def _(pe):
                pe.wait_ge(rows_in, 16 * TILES)
                for t in range(TILES):
                    last = pe.transpose(ps[0:RANK, t // 4, t % 4 * P:(t % 4 + 1) * P], rows[:, t, :], core.ident[:, :])
                last.then_inc(rows_turned, 1)
                pe.wait_ge(params_in, 48)
                pe.wait_ge(rowsT_ready, 1)
                for b in range(BATCH):
                    if b >= 4:
                        pe.wait_ge(bank_free, b - 3)
                    for t in range(TPB):
                        last = pe.matmul(ps[:, 4 + b % 4, t * D:(t + 1) * D],
                                         rowsT[:, (b * TPB + t) * P:(b * TPB + t + 1) * P], W2T[:, :],
                                         start=True, stop=True)
                    last.then_inc(bank_full, 1)

            @block.scalar
            def _(act):
                act.wait_ge(rows_turned, 1)
                act.activation(rowsT[:, :].rearrange("r (k n) -> r k n", k=4), ps[0:RANK, 0:4, :],
                               ACT.Copy).then_inc(rowsT_ready, 1)

            @block.vector
            def _(dve):
                dve.wait_ge(params_in, 48)
                dve.tensor_tensor(pos[:, :, :], pos[:, :, :], b2[:, :].unsqueeze(1).broadcast_to([P, TPB, D]),
                                  ALU.add).then_inc(pos_ready, 1)
                dve.wait_ge(pos_ready, 1)
                for b in range(BATCH):
                    dve.wait_ge(bank_full, b + 1)
                    dve.tensor_tensor(core.h[:, b * TPB:(b + 1) * TPB, :],
                                      ps[:, 4 + b % 4, :].rearrange("p (t d) -> p t d", t=TPB),
                                      pos[:, :, :], ALU.add).then_inc(bank_free, 1)
        s.clear()


def linear_attention(nc, core, Wqkv_d, bq_d, bkv_d, Wout_d, bout_d):
    ps, xT, h = core.ps, core.xT, core.h
    with ExitStack() as ctx:
        s = Scope(nc, ctx, "lattn")
        Wqkv = s.sb("Wqkv", [P, DC, 3 * D])
        Wout = s.sb("Wout", [P, DC, D])
        bq = s.sb("bq", [P, DC])
        bkv = s.sb("bkv", [P, 2 * D])
        bout = s.sb("bout", [P, D])
        qT = s.sb("qT", [P, DC, SEQ])
        q_sq = s.sb("q_sq", [P, DC, SEQ])
        kv = s.sb("kv", [P, TPB, 2 * D])
        k_sq = s.sb("k_sq", [P, D])
        k_ss = s.sb("k_ss", [P, TPB])
        rk = s.sb("rk", [P, TPB])
        k_by_v = s.sb("k_by_v", [P, TPB, D])
        sums = s.sb("sums", [P, DC + TPB])
        rq = s.sb("rq", [P, TPB])
        W_row = s.sb("W_row", [P, DC, D])
        weights_in = s.sem("weights_in")
        q_full = s.sem("q_full")
        kv_full = s.sem("kv_full")
        qT_ready = s.sem("qT_ready")
        kv_ready = s.sem("kv_ready")
        k_ss_ready = s.sem("k_ss_ready")
        k_by_v_ready = s.sem("k_by_v_ready")
        rk_ready = s.sem("rk_ready")
        sums_full = s.sem("sums_full")
        sums_ready = s.sem("sums_ready")
        rq_ready = s.sem("rq_ready")
        W_row_ready = s.sem("W_row_ready")
        out_full = s.sem("out_full")
        scaled = s.sem("scaled")
        row_added = s.sem("row_added")
        row = RowNorm(nc, core, s)

        with nc.Block() as block:
            @block.sync
            def _(sp):
                sp.dma_start(Wqkv[:, :, :], Wqkv_d.rearrange("(c p) n -> p c n", p=P)).then_inc(weights_in, 16)
                sp.dma_start(bq[:, :], bq_d).then_inc(weights_in, 16)
                sp.dma_start(bkv[:, :], bkv_d.partition_broadcast(P)).then_inc(weights_in, 16)
                sp.dma_start(Wout[:, :, :], Wout_d.rearrange("(c p) n -> p c n", p=P)).then_inc(weights_in, 16)
                sp.dma_start(bout[:, :], bout_d.partition_broadcast(P)).then_inc(weights_in, 16)

            @block.tensor
            def _(pe):
                pe.wait_ge(weights_in, 80)
                row.turn(pe, 0)
                with pe.Fori(0, BATCH) as b:
                    pe.wait_ge(row.xT_ready, b + 1)
                    pe.wait_ge(qT_ready, b * 2 + 2)
                    for m in range(DC):
                        for c in range(DC):
                            last = pe.matmul(ps[:, 0, m * SEQ:(m + 1) * SEQ], Wqkv[:, c, m * P:(m + 1) * P],
                                             xT[:, c, :], start=(c == 0), stop=(c == DC - 1))
                    last.then_inc(q_full, 1)
                    pe.wait_ge(kv_ready, b * 2 + 2)
                    for t in range(TPB):
                        for c in range(DC):
                            last = pe.matmul(ps[:, 1 + t, :], xT[:, c, t * P:(t + 1) * P],
                                             Wqkv[:, c, D:3 * D], start=(c == 0), stop=(c == DC - 1))
                        last.then_inc(kv_full, 1)
                    row.turn(pe, b + 1)
                    pe.wait_ge(k_by_v_ready, b * 2 + 2)
                    pe.wait_ge(rk_ready, b + 1)
                    pe.wait_ge(sums_ready, b + 1)
                    for c in range(DC):
                        for t in range(TPB):
                            pe.matmul(ps[:, 3, c:c + 1], k_by_v[:, t, c * P:(c + 1) * P], rk[:, t:t + 1],
                                      start=(t == 0), stop=(t == TPB - 1))
                    pe.wait_ge(qT_ready, b * 2 + 4)
                    for t in range(TPB):
                        for c in range(DC):
                            last = pe.matmul(ps[:, 3, DC + t:DC + t + 1], q_sq[:, c, t * P:(t + 1) * P],
                                             core.ones[:, 0:1], start=(c == 0), stop=(c == DC - 1))
                    last.then_inc(sums_full, 1)
                    pe.wait_ge(W_row_ready, b + 1)
                    pe.wait_ge(row_added, b + 1)
                    for t in range(TPB):
                        for c in range(DC):
                            last = pe.matmul(ps[:, 4, t * D:(t + 1) * D], qT[:, c, t * P:(t + 1) * P], W_row[:, c, :],
                                             start=(c == 0), stop=(c == DC - 1))
                    last.then_inc(out_full, 1)

            @block.scalar
            def _(act):
                act.sem_inc(qT_ready, 2)
                act.wait_ge(weights_in, 80)
                row.evacuate(act, 0)
                with act.Fori(0, BATCH) as b:
                    act.wait_ge(q_full, b + 1)
                    for m in range(DC):
                        act.activation(q_sq[:, m, :], ps[:, 0, m * SEQ:(m + 1) * SEQ], ACT.Square, bias=bq[:, m:m + 1])
                    act.wait_ge(row_added, b + 1)
                    for m in range(DC):
                        act.activation(qT[:, m, :], ps[:, 0, m * SEQ:(m + 1) * SEQ], ACT.Identity,
                                       bias=bq[:, m:m + 1]).then_inc(qT_ready, 1)
                    row.evacuate(act, b + 1)

            @block.gpsimd
            def _(pool):
                row.root(pool, 0)
                with pool.Fori(0, BATCH) as b:
                    row.root(pool, b + 1)
                    pool.wait_ge(k_ss_ready, b * 2 + 2)
                    pool.tensor_tensor(rk[:, :], k_ss[:, :], core.neg_half[:, 0:TPB], ALU.pow).then_inc(rk_ready, 1)
                    pool.wait_ge(sums_ready, b + 2)
                    pool.tensor_tensor(rq[:, :], sums[:, DC:DC + TPB], core.neg_half[:, 0:TPB],
                                       ALU.pow).then_inc(rq_ready, 1)

            @block.vector
            def _(dve):
                dve.sem_inc(kv_ready, 2)
                dve.sem_inc(sums_ready, 1)
                dve.sem_inc(row_added, 1)
                dve.wait_ge(weights_in, 80)
                row.norm(dve, 0, first=True)
                with dve.Fori(0, BATCH) as b:
                    row.norm(dve, b + 1)
                    for t in range(TPB):
                        dve.wait_ge(kv_full, b * 2 + t + 1)
                        dve.tensor_tensor(kv[:, t, :], ps[:, 1 + t, :], bkv[:, :], ALU.add).then_inc(kv_ready, 1)
                        dve.wait_ge(kv_ready, b * 2 + t + 3)
                        dve.tensor_tensor_reduce(out=k_sq[:, :], in0=kv[:, t, 0:D], in1=kv[:, t, 0:D], scale=1.0,
                                                 scalar=0.0, op0=ALU.mult, op1=ALU.add,
                                                 accum_out=k_ss[:, t:t + 1]).then_inc(k_ss_ready, 1)
                        dve.tensor_tensor(k_by_v[:, t, :], kv[:, t, 0:D], kv[:, t, D:2 * D],
                                          ALU.mult).then_inc(k_by_v_ready, 1)
                    dve.wait_ge(sums_full, b + 1)
                    dve.tensor_copy(sums[:, :], ps[:, 3, 0:DC + TPB]).then_inc(sums_ready, 1)
                    dve.wait_ge(sums_ready, b + 2)
                    dve.tensor_scalar(W_row[:, 0, :], Wout[:, 0, :], sums[:, 0:1], None, ALU.mult)
                    dve.tensor_scalar(W_row[:, 1, :], Wout[:, 1, :], sums[:, 1:2], None,
                                      ALU.mult).then_inc(W_row_ready, 1)
                    dve.wait_ge(out_full, b + 1)
                    dve.wait_ge(rq_ready, b + 1)
                    for t in range(TPB):
                        dve.scalar_tensor_tensor(out=h[:, ds(b * 2 + t, 1), :], in0=ps[:, 4, t * D:(t + 1) * D],
                                                 scalar=rq[:, t:t + 1], in1=h[:, ds(b * 2 + t, 1), :],
                                                 op0=ALU.mult, op1=ALU.add).then_inc(scaled, 1)
                    dve.wait_ge(scaled, b * 2 + 2)
                    dve.tensor_tensor(h[:, ds(b * 2, TPB), :], h[:, ds(b * 2, TPB), :],
                                      bout[:, :].unsqueeze(1).broadcast_to([P, TPB, D]), ALU.add).then_inc(row_added, 1)
        s.clear()


def sign_ffn(nc, core, k0_d, k1_d, k2_d, s_d):
    ps, xT, h = core.ps, core.xT, core.h
    F = k1_d.shape[0]
    FC = F // P
    G1_BANKS, G2_BANKS = (0, 1, 2), (3, 4, 5)
    JOBS = FC // 2
    with ExitStack() as ctx:
        s = Scope(nc, ctx, "sffn")
        k0_words = s.sb("k0", [P, 2 * DC, F // 4], I32)
        k1_words = s.sb("k1", [P, FC, F // 4], I32)
        k2_words = s.sb("k2", [P, FC, D // 4], I32)
        k0, k1, k2 = (k[:, :, :].bitcast(U8) for k in (k0_words, k1_words, k2_words))
        W0 = s.sb("W0", [P, DC, F], F32R)
        W1 = s.sb("W1", [P, FC, F], F32R)
        W2 = s.sb("W2", [P, FC, D], F32R)
        x_parts = [s.sb(f"x_{n}", [P, DC, SEQ], F32R) for n in ("high", "low")]
        sc = s.sb("sc", [P, 3])
        gain = s.sb("gain", [P, 2])
        hidden = s.sb("hidden", [P, 2, 2, SEQ])
        h1_parts, h2_parts = ([s.sb(f"{h}_{n}", [P, FC, SEQ], F32R) for n in ("high", "low")] for h in ("h1", "h2"))
        bits_in = s.sem("bits_in")
        W0_ready = s.sem("W0_ready")
        W1_ready = s.sem("W1_ready")
        W2_ready = s.sem("W2_ready")
        gain_ready = s.sem("gain_ready")
        hidden_full = s.sem("hidden_full")
        hidden_ready = s.sem("hidden_ready")
        high_ready = s.sem("high_ready")
        parts_ready = s.sem("parts_ready")
        out_full = s.sem("out_full")
        row_added = s.sem("row_added")
        row = RowNorm(nc, core, s)

        with nc.Block() as block:
            @block.sync
            def _(sp):
                sp.dma_start(k0_words[:, :, :], k0_d.rearrange("(c p) n -> p c n", p=P)).then_inc(bits_in, 16)
                sp.dma_start(sc[:, :], s_d.partition_broadcast(P)).then_inc(bits_in, 16)
                sp.dma_start(k1_words[:, :, :], k1_d.rearrange("(c p) n -> p c n", p=P)).then_inc(bits_in, 16)
                sp.dma_start(k2_words[:, :, :], k2_d.rearrange("(c p) n -> p c n", p=P)).then_inc(bits_in, 16)

            @block.tensor
            def _(pe):
                row.turn(pe, 0)
                pe.wait_ge(W0_ready, 1)
                with pe.Fori(0, BATCH) as b:
                    done = b * (2 * JOBS)
                    pe.wait_ge(row.low_ready, b + 1)
                    for j in range(JOBS):
                        pe.wait_ge(hidden_ready, done + (JOBS if j < 3 else 2 * JOBS + j - 2))
                        for m in range(2):
                            for c in range(DC):
                                for i, x in enumerate(x_parts):
                                    last = pe.matmul(ps[:, G1_BANKS[j % 3], m * SEQ:(m + 1) * SEQ],
                                                     W0[:, c, (2 * j + m) * P:(2 * j + m + 1) * P], x[:, c, :],
                                                     start=(c + i == 0), stop=(c + i == DC))
                        last.then_inc(hidden_full, 1)
                    pe.wait_ge(W1_ready, 1)
                    for j in range(JOBS):
                        if j == 2:
                            row.turn(pe, b + 1)
                        if j >= 3:
                            pe.wait_ge(hidden_ready, done + 3 * JOBS + j - 2)
                        for m in range(2):
                            for c in range(FC):
                                if j == 0 and m == 0 and c % 2 == 0:
                                    pe.wait_ge(parts_ready, done + c // 2 + 3)
                                for i, h1 in enumerate(h1_parts):
                                    last = pe.matmul(ps[:, G2_BANKS[j % 3], m * SEQ:(m + 1) * SEQ],
                                                     W1[:, c, (2 * j + m) * P:(2 * j + m + 1) * P], h1[:, c, :],
                                                     start=(c + i == 0), stop=(c + i == FC))
                        last.then_inc(hidden_full, 1)
                    pe.wait_ge(W2_ready, 1)
                    pe.wait_ge(row_added, b + 1)
                    for t in range(TPB):
                        for c in range(FC):
                            if t == 0 and c % 2 == 0:
                                pe.wait_ge(parts_ready, done + JOBS + c // 2 + 3)
                            for i, h2 in enumerate(h2_parts):
                                last = pe.matmul(ps[:, 6, t * D:(t + 1) * D], h2[:, c, t * P:(t + 1) * P], W2[:, c, :],
                                                 start=(c + i == 0), stop=(c + i == FC))
                    last.then_inc(out_full, 1)

            @block.scalar
            def _(act):
                def relu(n, j, bank, k):
                    act.wait_ge(hidden_full, n + 1)
                    act.wait_ge(parts_ready, n + 1)
                    act.activation(hidden[:, j % 2, :, :], ps[:, bank, :].rearrange("p (m n) -> p m n", m=2),
                                   ACT.Relu, scale=gain[:, k:k + 1]).then_inc(hidden_ready, 1)

                act.sem_inc(hidden_ready, 2 * JOBS)
                row.evacuate(act, 0, x_parts[0][:, :, :])
                act.wait_ge(gain_ready, 2)
                with act.Fori(0, BATCH) as b:
                    for j in range(JOBS):
                        relu(b * (2 * JOBS) + j, j, G1_BANKS[j % 3], 0)
                    for j in range(JOBS):
                        if j == 2:
                            row.evacuate(act, b + 1, x_parts[0][:, :, :])
                        relu(b * (2 * JOBS) + JOBS + j, j, G2_BANKS[j % 3], 1)

            @block.gpsimd
            def _(pool):
                row.root(pool, 0)
                with pool.Fori(0, BATCH) as b:
                    row.root(pool, b + 1)

            @block.vector
            def _(dve):
                def split(n, j, parts):
                    high, low = (p[:, 2 * j:2 * j + 2, :] for p in parts)
                    dve.wait_ge(hidden_ready, n + 2 * JOBS + 1)
                    dve.tensor_copy(high, hidden[:, j % 2, :, :]).then_inc(high_ready, 1)
                    dve.wait_ge(high_ready, n + 1)
                    dve.tensor_tensor(low, hidden[:, j % 2, :, :], high.bitcast(F32), ALU.subtract).then_inc(parts_ready, 1)

                row.norm(dve, 0, first=True)
                dve.sem_inc(row_added, 1)
                dve.sem_inc(parts_ready, 2)
                dve.wait_ge(bits_in, 64)
                dve.tensor_scalar(gain[:, 0:1], sc[:, 0:1], 4.0, None, ALU.mult).then_inc(gain_ready, 1)
                dve.tensor_scalar(gain[:, 1:2], sc[:, 1:2], 2.0, None, ALU.mult).then_inc(gain_ready, 1)
                dve.tensor_tensor(W0[:, :, :], k0[:, 0:DC, :], k0[:, DC:2 * DC, :], ALU.subtract).then_inc(W0_ready, 1)
                dve.tensor_scalar(W1[:, :, :], k1[:, :, :], 2.0, -1.0, ALU.mult, ALU.add).then_inc(W1_ready, 1)
                dve.tensor_scalar(W2[:, :, :], k2[:, :, :], 2.0, -1.0, ALU.mult, ALU.add).then_inc(W2_ready, 1)
                row.low(dve, 0, *x_parts)
                with dve.Fori(0, BATCH) as b:
                    for j in range(JOBS):
                        split(b * (2 * JOBS) + j, j, h1_parts)
                    row.norm(dve, b + 1)
                    for j in range(JOBS):
                        if j == 2:
                            row.low(dve, b + 1, *x_parts)
                        split(b * (2 * JOBS) + JOBS + j, j, h2_parts)
                    dve.wait_ge(out_full, b + 1)
                    dve.scalar_tensor_tensor(out=h[:, ds(b * TPB, TPB), :],
                                             in0=ps[:, 6, :].rearrange("p (t d) -> p t d", t=TPB), scalar=sc[:, 2:3],
                                             in1=h[:, ds(b * TPB, TPB), :], op0=ALU.mult,
                                             op1=ALU.add).then_inc(row_added, 1)
        s.clear()


def min_gru(nc, core, W1_d, b1_d, W2_d, b2_d, Wz_d, bz_d, Wh_d, bh_d, Wo_d, bo_d):
    ps, xT, h = core.ps, core.xT, core.h
    F = Wz_d.shape[0]
    FC = F // P
    with ExitStack() as ctx:
        s = Scope(nc, ctx, "gru")
        W1 = s.sb("W1", [P, DC, F])
        W2 = s.sb("W2", [P, DC, F])
        Wz = s.sb("Wz", [P, FC, F])
        Wh = s.sb("Wh", [P, FC, F])
        Wo = s.sb("Wo", [P, FC, D])
        b1, b2, bz, bh = (s.sb(n, [P, FC]) for n in ("b1", "b2", "bz", "bh"))
        neg_bz = s.sb("neg_bz", [P, FC])
        bo = s.sb("bo", [P, D])
        sg = s.sb("sg", [P, 2, SEQ])
        u = s.sb("u", [P, FC, SEQ])
        skip = s.sb("skip", [P, FC, SEQ])
        keep = s.sb("keep", [P, 2, SEQ])
        z = s.sb("z", [P, 2, SEQ])
        drive = s.sb("drive", [P, 2, SEQ])
        state = s.sb("state", [P, 2, SEQ])
        W1_in, W2_in, gates_in, Wo_in = (s.sem(n) for n in ("W1_in", "W2_in", "gates_in", "Wo_in"))
        neg_bz_ready = s.sem("neg_bz_ready")
        silu_full = s.sem("silu_full")
        sg_ready = s.sem("sg_ready")
        silu_ready = s.sem("silu_ready")
        gate_full = s.sem("gate_full")
        gate_ready = s.sem("gate_ready")
        drive_ready = s.sem("drive_ready")
        state_ready = s.sem("state_ready")
        sum_ready = s.sem("sum_ready")
        out_full = s.sem("out_full")
        product_added = s.sem("product_added")
        row_added = s.sem("row_added")
        row = RowNorm(nc, core, s)

        with nc.Block() as block:
            @block.sync
            def _(sp):
                sp.dma_start(W1[:, :, :], W1_d.rearrange("(c p) n -> p c n", p=P)).then_inc(W1_in, 16)
                sp.dma_start(b1[:, :], b1_d).then_inc(W1_in, 16)
                sp.dma_start(W2[:, :, :], W2_d.rearrange("(c p) n -> p c n", p=P)).then_inc(W2_in, 16)
                sp.dma_start(b2[:, :], b2_d).then_inc(W2_in, 16)
                sp.dma_start(Wz[:, :, :], Wz_d.rearrange("(c p) n -> p c n", p=P)).then_inc(gates_in, 16)
                sp.dma_start(bz[:, :], bz_d).then_inc(gates_in, 16)
                sp.dma_start(Wh[:, :, :], Wh_d.rearrange("(c p) n -> p c n", p=P)).then_inc(gates_in, 16)
                sp.dma_start(bh[:, :], bh_d).then_inc(gates_in, 16)
                sp.dma_start(Wo[:, :, :], Wo_d.rearrange("(c p) n -> p c n", p=P)).then_inc(Wo_in, 16)
                sp.dma_start(bo[:, :], bo_d.partition_broadcast(P)).then_inc(Wo_in, 16)

            @block.tensor
            def _(pe):
                row.turn(pe, 0)
                pe.wait_ge(W1_in, 32)
                pe.wait_ge(W2_in, 32)
                with pe.Fori(0, BATCH) as b:
                    pe.wait_ge(row.xT_ready, b + 1)
                    for j in range(2 * FC):
                        W, m = (W1, j) if j < FC else (W2, j - FC)
                        bank = 2 * (j // FC) + j % 2
                        if j not in (FC, FC + 1):
                            pe.wait_ge(silu_ready, b * (2 * FC) + j + 1)
                        for c in range(DC):
                            last = pe.matmul(ps[:, bank, 0:SEQ], W[:, c, m * P:(m + 1) * P], xT[:, c, :],
                                             start=(c == 0), stop=(c == DC - 1))
                        last.then_inc(silu_full, 1)
                    row.turn(pe, b + 1)
                    pe.wait_ge(gates_in, 64)
                    pe.wait_ge(silu_ready, b * (2 * FC) + FC + 2)
                    for m in range(FC):
                        pe.wait_ge(gate_ready, b * FC + m + 1)
                        pe.wait_ge(drive_ready, b * FC + m + 1)
                        for half, W in ((0, Wz), (1, Wh)):
                            for c in range(FC):
                                last = pe.matmul(ps[:, 4 + m % 2, half * SEQ:(half + 1) * SEQ],
                                                 W[:, c, m * P:(m + 1) * P], u[:, c, :],
                                                 start=(c == 0), stop=(c == FC - 1))
                        last.then_inc(gate_full, 1)
                    pe.wait_ge(Wo_in, 32)
                    pe.wait_ge(sum_ready, b * FC + FC)
                    pe.wait_ge(product_added, b + 1)
                    for t in range(TPB):
                        for c in range(FC):
                            last = pe.matmul(ps[:, 6, t * D:(t + 1) * D], skip[:, c, t * P:(t + 1) * P], Wo[:, c, :],
                                             start=(c == 0), stop=(c == FC - 1))
                    last.then_inc(out_full, 1)

            @block.scalar
            def _(act):
                row.evacuate(act, 0)
                act.sem_inc(gate_ready, 2)
                act.wait_ge(W1_in, 32)
                act.wait_ge(W2_in, 32)
                act.wait_ge(gates_in, 64)
                act.wait_ge(neg_bz_ready, 1)
                with act.Fori(0, BATCH) as b:
                    for j in range(2 * FC):
                        bias, m = (b1, j) if j < FC else (b2, j - FC)
                        bank = 2 * (j // FC) + j % 2
                        act.wait_ge(silu_full, b * (2 * FC) + j + 1)
                        act.wait_ge(silu_ready, b * (2 * FC) + j + 1)
                        act.activation(sg[:, j % 2, :], ps[:, bank, 0:SEQ], ACT.Sigmoid,
                                       bias=bias[:, m:m + 1]).then_inc(sg_ready, 1)
                    row.evacuate(act, b + 1)
                    for m in range(FC):
                        act.wait_ge(gate_full, b * FC + m + 1)
                        act.wait_ge(state_ready, b * FC + m + 1)
                        act.activation(keep[:, m % 2, :], ps[:, 4 + m % 2, 0:SEQ], ACT.Sigmoid,
                                       bias=neg_bz[:, m:m + 1], scale=-1.0)
                        act.activation(z[:, m % 2, :], ps[:, 4 + m % 2, 0:SEQ], ACT.Sigmoid,
                                       bias=bz[:, m:m + 1]).then_inc(gate_ready, 1)

            @block.gpsimd
            def _(pool):
                row.root(pool, 0)
                with pool.Fori(0, BATCH) as b:
                    row.root(pool, b + 1)

            @block.vector
            def _(dve):
                row.norm(dve, 0, first=True)
                dve.sem_inc(silu_ready, 2)
                dve.sem_inc(drive_ready, 2)
                dve.sem_inc(state_ready, 2)
                dve.sem_inc(product_added, 1)
                dve.wait_ge(gates_in, 64)
                dve.tensor_scalar(neg_bz[:, :], bz[:, :], -1.0, None, ALU.mult).then_inc(neg_bz_ready, 1)
                dve.wait_ge(W1_in, 32)
                dve.wait_ge(W2_in, 32)
                dve.wait_ge(Wo_in, 32)
                with dve.Fori(0, BATCH) as b:
                    for j in range(2 * FC):
                        bias, out, m = (b1, u, j) if j < FC else (b2, skip, j - FC)
                        bank = 2 * (j // FC) + j % 2
                        dve.wait_ge(sg_ready, b * (2 * FC) + j + 1)
                        dve.scalar_tensor_tensor(out=out[:, m, :], in0=ps[:, bank, 0:SEQ], scalar=bias[:, m:m + 1],
                                                 in1=sg[:, j % 2, :], op0=ALU.add,
                                                 op1=ALU.mult).then_inc(silu_ready, 1)
                    row.norm(dve, b + 1)
                    for m in range(FC):
                        dve.wait_ge(gate_ready, b * FC + m + 3)
                        dve.scalar_tensor_tensor(out=drive[:, m % 2, :], in0=ps[:, 4 + m % 2, SEQ:2 * SEQ],
                                                 scalar=bh[:, m:m + 1], in1=z[:, m % 2, :], op0=ALU.add,
                                                 op1=ALU.mult).then_inc(drive_ready, 1)
                        dve.wait_ge(drive_ready, b * FC + m + 3)
                        dve.tensor_tensor_scan(out=state[:, m % 2, :], data0=keep[:, m % 2, :],
                                               data1=drive[:, m % 2, :], initial=0.0, op0=ALU.mult,
                                               op1=ALU.add).then_inc(state_ready, 1)
                        dve.wait_ge(state_ready, b * FC + m + 3)
                        dve.tensor_tensor(skip[:, m, :], skip[:, m, :], state[:, m % 2, :],
                                          ALU.add).then_inc(sum_ready, 1)
                    dve.wait_ge(out_full, b + 1)
                    dve.tensor_tensor(h[:, ds(b * TPB, TPB), :], ps[:, 6, :].rearrange("p (t d) -> p t d", t=TPB),
                                      h[:, ds(b * TPB, TPB), :], ALU.add).then_inc(product_added, 1)
                    dve.wait_ge(product_added, b + 2)
                    dve.tensor_tensor(h[:, ds(b * TPB, TPB), :], h[:, ds(b * TPB, TPB), :],
                                      bo[:, :].unsqueeze(1).broadcast_to([P, TPB, D]), ALU.add).then_inc(row_added, 1)
        s.clear()


class Router:

    def __init__(self, nc, core, s, E, K):
        self.core, self.E, self.K = core, E, K
        T = TILES
        self.logits = s.sb("logits", [P, T, E])
        self.peak = s.sb("peak", [P, T])
        self.probs = s.sb("probs", [P, T, E])
        self.total = s.sb("total", [P, T])
        self.index = s.sb("index", [P, T, E])
        self.before = s.sb("before", [P, P])
        self.cand = s.sb("cand", [P, T, E])
        self.top = [s.sb(f"top{k}", [P, T]) for k in range(K)]
        self.best = [s.sb(f"best{k}", [P, T]) for k in range(K)]
        self.hot = [s.sb(f"hot{k}", [P, T, E]) for k in range(K)]
        self.chosen = s.sb("chosen", [P, T, E]) if K > 1 else self.hot[0]
        self.count = [s.sb(f"count{k}", [P, T, E]) for k in range(2)]
        self.pos = s.sb("pos", [P, T, E])
        self.made = s.sem("route_made")
        self.before_one = s.sem("route_before_one")
        self.shifted = s.sem("route_shifted")
        self.exped = s.sem("route_exped")
        self.chosen_ready = s.sem("route_chosen_ready")
        self.counted = s.sem("route_counted")
        self.step = s.sem("route_step")

    def wide(self, column):
        return column[:, :].unsqueeze(2).broadcast_to([P, TILES, self.E])

    def tables(self, pool):
        pool.iota(self.index[:, :, :], pattern=[[0, TILES], [1, self.E]], base=0, channel_multiplier=0,
                  allow_small_or_imprecise_dtypes=True).then_inc(self.made, 1)
        pool.memset(self.before[:, :], 1.0).then_inc(self.before_one, 1)
        pool.wait_ge(self.before_one, 1)
        pool.affine_select(out=self.before[:, :], in_=self.before[:, :], compare_op=ALU.is_ge, fill=0.0, base=-1,
                           pattern=[[1, P]], channel_multiplier=-1).then_inc(self.made, 1)

    def exp(self, act):
        act.wait_ge(self.shifted, 1)
        act.activation(self.probs[:, :, :], self.cand[:, :, :], ACT.Exp).then_inc(self.exped, 1)

    def count_before(self, pe):
        pe.wait_ge(self.made, 2)
        pe.wait_ge(self.chosen_ready, 1)
        n = TILES * self.E
        flat = self.chosen[:, :, :].rearrange("p t e -> p (t e)")
        pe.matmul(self.core.ps[:, 0, 0:n], self.before[:, :], flat, start=True, stop=True)
        pe.matmul(self.core.ps[:, 1, 0:n], self.core.ones[:, :], flat, start=True, stop=True).then_inc(self.counted, 1)

    def route(self, dve):
        T, E, n = TILES, self.E, TILES * self.E
        step = Chain(dve, self.step)
        step(dve.tensor_reduce(self.peak[:, :], self.logits[:, :, :], AX_X, ALU.max))
        dve.tensor_tensor(self.cand[:, :, :], self.logits[:, :, :], self.wide(self.peak),
                          ALU.subtract).then_inc(self.shifted, 1)
        dve.wait_ge(self.exped, 1)
        step(dve.tensor_reduce(self.total[:, :], self.probs[:, :, :], AX_X, ALU.add))
        step(dve.reciprocal(self.total[:, :], self.total[:, :]))
        step(dve.tensor_tensor(self.probs[:, :, :], self.probs[:, :, :], self.wide(self.total), ALU.mult))
        dve.wait_ge(self.made, 2)
        for k in range(self.K):
            step(dve.tensor_reduce(self.top[k][:, :], self.probs[:, :, :], AX_X, ALU.max))
            step(dve.tensor_tensor(self.cand[:, :, :], self.probs[:, :, :], self.wide(self.top[k]), ALU.is_equal))
            step(dve.scalar_tensor_tensor(out=self.cand[:, :, :], in0=self.cand[:, :, :], scalar=-float(E),
                                          in1=self.index[:, :, :], op0=ALU.mult, op1=ALU.add))
            step(dve.tensor_reduce(self.best[k][:, :], self.cand[:, :, :], AX_X, ALU.min))
            step(dve.tensor_tensor(self.hot[k][:, :, :], self.cand[:, :, :], self.wide(self.best[k]), ALU.is_equal))
            if k < self.K - 1:
                step(dve.scalar_tensor_tensor(out=self.probs[:, :, :], in0=self.hot[k][:, :, :], scalar=-2.0,
                                              in1=self.probs[:, :, :], op0=ALU.mult, op1=ALU.add))
        if self.K > 1:
            step(dve.tensor_tensor(self.chosen[:, :, :], self.hot[0][:, :, :], self.hot[1][:, :, :], ALU.add))
        dve.sem_inc(self.chosen_ready, 1)
        dve.wait_ge(self.counted, 1)
        in_tile = self.core.ps[:, 0, 0:n].rearrange("p (t e) -> p t e", e=E)
        of_tile = self.core.ps[:, 1, 0:n].rearrange("p (t e) -> p t e", e=E)
        a, b = self.count
        step(dve.tensor_copy(a[:, :, :], of_tile))
        d = 1
        while d < T:
            step(dve.tensor_copy(b[:, 0:d, :], a[:, 0:d, :]))
            step(dve.tensor_tensor(b[:, d:T, :], a[:, d:T, :], a[:, 0:T - d, :], ALU.add))
            a, b = b, a
            d *= 2
        step(dve.tensor_tensor(self.pos[:, :, :], a[:, :, :], of_tile, ALU.subtract))
        step(dve.tensor_tensor(self.pos[:, :, :], self.pos[:, :, :], in_tile, ALU.add))
        return step, a[:, T - 1, :], b


def capacity(E):
    return -(-N * 2 * 5 // 4 // E)


def spare_rows(E, C):
    return -(-(E + 1) * C // (4 * P)) * 4 * P


def capacity_moe(nc, core, router_w_d, router_b_d, gate_d, up_d, down_d, sgate_d, sup_d, sdown_d, ROWS, OUTS):
    ps, xT, xr, h = core.ps, core.xT, core.xr, core.h
    E, _, F = gate_d.shape
    C = capacity(E)
    SPARE = spare_rows(E, C)
    CHUNKS = [(c, min(P, F - c * P)) for c in range(-(-F // P))]
    SLOTS = [(t, min(P, C - t * P)) for t in range(-(-C // P))]
    NF, NS = len(CHUNKS), len(SLOTS)
    ZERO = SPARE * D // P // 4
    with ExitStack() as ctx:
        s = Scope(nc, ctx, "cmoe")
        xn = s.sb("xn", [P, TILES, D])
        r = Router(nc, core, s, E, 2)
        slot = [s.sb(f"slot{k}", [P, TILES]) for k in range(2)]
        place = [s.sb(f"place{k}", [P, TILES]) for k in range(2)]
        kept = [s.sb(f"kept{k}", [P, TILES]) for k in range(2)]
        spare = [s.sb(f"spare{k}", [P, TILES]) for k in range(2)]
        weight = [s.sb(f"weight{k}", [P, TILES]) for k in range(2)]
        to_row = [s.sb(f"to_row{k}", [P, TILES], I32) for k in range(2)]
        from_row = [s.sb(f"from_row{k}", [P, TILES], I32) for k in range(2)]
        zeros_done = s.sem("zeros_done")

        with ExitStack() as ctx_a:
            sa = Scope(nc, ctx_a, "cmoe_shared", s)
            Wr = sa.sb("Wr", [P, DC, E])
            br = sa.sb("br", [P, E])
            Wg = sa.sb("Wg", [P, DC, F])
            Wu = sa.sb("Wu", [P, DC, F])
            Wd = sa.sb("Wd", [P, NF, D])
            zeros = sa.sb("zeros", [P, ZERO])
            sg = sa.sb("sg", [P, 2, SEQ])
            act_ = sa.sb("act", [P, NF, SEQ])
            zeros_made = sa.sem("zeros_made")
            weights_in = sa.sem("weights_in")
            logits_full = sa.sem("logits_full")
            logits_ready = sa.sem("logits_ready")
            gated_full = sa.sem("gated_full")
            sg_ready = sa.sem("sg_ready")
            swish_ready = sa.sem("swish_ready")
            act_ready = sa.sem("act_ready")
            out_full = sa.sem("out_full")
            product_added = sa.sem("product_added")
            xn_ready = sa.sem("xn_ready")
            row_added = sa.sem("row_added")
            row = RowNorm(nc, core, sa)

            with nc.Block() as block:
                @block.sync
                def _(sp):
                    sp.dma_start(Wr[:, :, :], router_w_d.rearrange("(c p) n -> p c n", p=P)).then_inc(weights_in, 16)
                    sp.dma_start(br[:, :], router_b_d.partition_broadcast(P)).then_inc(weights_in, 16)
                    sp.dma_start(Wg[:, :, :], sgate_d.rearrange("(c p) n -> p c n", p=P)).then_inc(weights_in, 16)
                    sp.dma_start(Wu[:, :, :], sup_d.rearrange("(c p) n -> p c n", p=P)).then_inc(weights_in, 16)
                    sp.dma_start(Wd[:, :, :], sdown_d.rearrange("(c p) n -> p c n", p=P)).then_inc(weights_in, 16)
                    sp.wait_ge(zeros_made, 1)
                    rows = ROWS[0:SPARE, :].rearrange("(q a) d -> q (a d)", q=4 * P)
                    for q in range(4):
                        sp.dma_start(rows[q * P:(q + 1) * P, :], zeros[:, :]).then_inc(zeros_done, 16)
                    sp.wait_ge(zeros_done, 64)

                @block.tensor
                def _(pe):
                    row.turn(pe, 0)
                    pe.wait_ge(weights_in, 80)
                    with pe.Fori(0, BATCH) as b:
                        pe.wait_ge(row.xT_ready, b + 1)
                        pe.wait_ge(logits_ready, b + 1)
                        for t in range(TPB):
                            for c in range(DC):
                                last = pe.matmul(ps[:, 4, t * E:(t + 1) * E], xT[:, c, t * P:(t + 1) * P], Wr[:, c, :],
                                                 start=(c == 0), stop=(c == DC - 1))
                        last.then_inc(logits_full, 1)
                        for m, w in CHUNKS:
                            pe.wait_ge(act_ready, b * NF + m + 1)
                            for half, W in ((0, Wg), (1, Wu)):
                                for c in range(DC):
                                    last = pe.matmul(ps[0:w, m, half * SEQ:(half + 1) * SEQ],
                                                     W[:, c, m * P:m * P + w], xT[:, c, :],
                                                     start=(c == 0), stop=(c == DC - 1))
                            last.then_inc(gated_full, 1)
                        row.turn(pe, b + 1)
                        pe.wait_ge(product_added, b + 1)
                        for t in range(TPB):
                            for m, w in CHUNKS:
                                pe.wait_ge(act_ready, b * NF + NF + m + 1)
                                last = pe.matmul(ps[:, 3, t * D:(t + 1) * D], act_[0:w, m, t * P:(t + 1) * P],
                                                 Wd[0:w, m, :], start=(m == 0), stop=(m == NF - 1))
                        last.then_inc(out_full, 1)

                @block.scalar
                def _(act):
                    row.evacuate(act, 0)
                    with act.Fori(0, BATCH) as b:
                        for m, w in CHUNKS:
                            act.wait_ge(gated_full, b * NF + m + 1)
                            act.wait_ge(act_ready, b * NF + NF + m // 2)
                            act.activation(sg[0:w, m % 2, :], ps[0:w, m, 0:SEQ], ACT.Sigmoid).then_inc(sg_ready, 1)
                        row.evacuate(act, b + 1)

                @block.gpsimd
                def _(pool):
                    pool.memset(zeros[:, :], 0.0).then_inc(zeros_made, 1)
                    row.root(pool, 0)
                    with pool.Fori(0, BATCH) as b:
                        row.root(pool, b + 1)
                    r.tables(pool)
                    for k in range(2):
                        pool.iota(spare[k][:, :], pattern=[[P, TILES]], base=SPARE + k * N, channel_multiplier=1,
                                  allow_small_or_imprecise_dtypes=True).then_inc(r.made, 1)
                    pool.wait_ge(r.made, 4)

                @block.vector
                def _(dve):
                    dve.sem_inc(logits_ready, 1)
                    dve.sem_inc(act_ready, NF)
                    dve.sem_inc(product_added, 1)
                    row.norm(dve, 0, first=True)
                    dve.wait_ge(weights_in, 80)
                    with dve.Fori(0, BATCH) as b:
                        dve.wait_ge(row.row_normed, b * TPB + TPB)
                        dve.tensor_tensor(xn[:, ds(b * TPB, TPB), :], xr[:, :, :], xr[:, :, :],
                                          ALU.max).then_inc(xn_ready, 1)
                        row.norm(dve, b + 1)
                        dve.wait_ge(logits_full, b + 1)
                        dve.tensor_tensor(r.logits[:, ds(b * TPB, TPB), :],
                                          ps[:, 4, 0:TPB * E].rearrange("p (t e) -> p t e", e=E),
                                          br[:, :].unsqueeze(1).broadcast_to([P, TPB, E]),
                                          ALU.add).then_inc(logits_ready, 1)
                        for m, w in CHUNKS:
                            dve.wait_ge(sg_ready, b * NF + m + 1)
                            dve.tensor_tensor(sg[0:w, m % 2, :], sg[0:w, m % 2, :], ps[0:w, m, 0:SEQ],
                                              ALU.mult).then_inc(swish_ready, 1)
                            dve.wait_ge(swish_ready, b * NF + m + 1)
                            dve.tensor_tensor(act_[0:w, m, :], sg[0:w, m % 2, :], ps[0:w, m, SEQ:2 * SEQ],
                                              ALU.mult).then_inc(act_ready, 1)
                        dve.wait_ge(out_full, b + 1)
                        dve.tensor_tensor(h[:, ds(b * TPB, TPB), :], ps[:, 3, :].rearrange("p (t d) -> p t d", t=TPB),
                                          h[:, ds(b * TPB, TPB), :], ALU.add).then_inc(product_added, 1)
                        dve.wait_ge(product_added, b + 2)
                        dve.tensor_tensor(h[:, ds(b * TPB, TPB), :], h[:, ds(b * TPB, TPB), :],
                                          xn[:, ds(b * TPB, TPB), :], ALU.add).then_inc(row_added, 1)
                    dve.wait_ge(row_added, BATCH)
                    dve.wait_ge(xn_ready, BATCH)
                    dve.wait_ge(logits_ready, BATCH + 1)

        with ExitStack() as ctx_b:
            sb_ = Scope(nc, ctx_b, "cmoe_route", s)
            rows_ready = sb_.sem("rows_ready")
            scattered = core.pool_dma.sem("cmoe_scattered")
            with nc.Block() as block:
                @block.scalar
                def _(act):
                    r.exp(act)

                @block.tensor
                def _(pe):
                    r.count_before(pe)

                @block.vector
                def _(dve):
                    step, _, tmp = r.route(dve)
                    for k in range(2):
                        step(dve.tensor_tensor(tmp[:, :, :], r.hot[k][:, :, :], r.pos[:, :, :], ALU.mult))
                        step(dve.tensor_reduce(place[k][:, :], tmp[:, :, :], AX_X, ALU.add))
                        step(dve.tensor_scalar(kept[k][:, :], place[k][:, :], float(C), None, ALU.is_lt))
                        step(dve.tensor_scalar(place[k][:, :], place[k][:, :], float(C - 1), None, ALU.min))
                        step(dve.tensor_scalar(slot[k][:, :], r.best[k][:, :], float(E), float(C), ALU.add, ALU.mult))
                        step(dve.tensor_tensor(slot[k][:, :], slot[k][:, :], place[k][:, :], ALU.add))
                        step(dve.tensor_copy(from_row[k][:, :], slot[k][:, :]))
                        step(dve.tensor_tensor(slot[k][:, :], slot[k][:, :], spare[k][:, :], ALU.subtract))
                        step(dve.tensor_tensor(slot[k][:, :], slot[k][:, :], kept[k][:, :], ALU.mult))
                        step(dve.tensor_tensor(slot[k][:, :], slot[k][:, :], spare[k][:, :], ALU.add))
                        dve.tensor_copy(to_row[k][:, :], slot[k][:, :]).then_inc(rows_ready, 1)
                    total = r.total
                    step(dve.tensor_tensor(total[:, :], r.top[0][:, :], r.top[1][:, :], ALU.add))
                    step(dve.tensor_scalar(total[:, :], total[:, :], 1e-9, None, ALU.add))
                    step(dve.reciprocal(total[:, :], total[:, :]))
                    for k in range(2):
                        step(dve.tensor_tensor(weight[k][:, :], r.top[k][:, :], total[:, :], ALU.mult))
                        step(dve.tensor_tensor(weight[k][:, :], weight[k][:, :], kept[k][:, :], ALU.mult))

                @block.gpsimd
                def _(pool):
                    for k in range(2):
                        pool.wait_ge(rows_ready, k + 1)
                        for t in range(TILES):
                            pool.indirect_dma_start(ROWS, bass.IndirectOffsetOnAxis(ap=to_row[k][:, t:t + 1], axis=0),
                                                    xn[:, t, :], None).then_inc(scattered, 16)
                    pool.wait_ge(scattered, 16 * 2 * TILES)

        with ExitStack() as ctx_c:
            sc = Scope(nc, ctx_c, "cmoe_experts", s)
            Wg = sc.sb("Wg", [P, 2, DC, F])
            Wu = sc.sb("Wu", [P, 2, DC, F])
            Wd = sc.sb("Wd", [P, 2, NF, D])
            xe = sc.sb("xe", [P, 2, NS, D])
            xeT = sc.sb("xeT", [P, DC, C])
            sg = sc.sb("sg", [P, 2, C])
            act_ = sc.sb("act", [P, NF, C])
            ye = sc.sb("ye", [P, 2, NS, D])
            weights_in = [sc.sem(f"weights_in{u}") for u in range(2)]
            rows_in = [sc.sem(f"rows_in{u}") for u in range(2)]
            turned = sc.sem("turned")
            xeT_ready = sc.sem("xeT_ready")
            gated_full = sc.sem("gated_full")
            sg_ready = sc.sem("sg_ready")
            swish_ready = sc.sem("swish_ready")
            act_ready = sc.sem("act_ready")
            out_full = sc.sem("out_full")
            ye_ready = sc.sem("ye_ready")
            stored = [sc.sem(f"stored{u}") for u in range(2)]

            with nc.Block() as block:
                @block.sync
                def _(sp):
                    def rows(e, u, first):
                        if not first:
                            sp.wait_ge(turned, e - 1)
                        sp.dma_start(xe[:, u, 0:NS - 1, :],
                                     ROWS[ds(e * C, (NS - 1) * P), :].rearrange("(t p) d -> p t d", p=P)
                                     ).then_inc(rows_in[u], 16)
                        sp.dma_start(xe[0:SLOTS[-1][1], u, NS - 1, :],
                                     ROWS[ds(e * C + (NS - 1) * P, SLOTS[-1][1]), :]).then_inc(rows_in[u], 16)

                    def weights(e, u, first):
                        if not first:
                            sp.wait_ge(out_full, e - 1)
                        for W, W_d in ((Wg, gate_d), (Wu, up_d), (Wd, down_d)):
                            sp.dma_start(W[:, u, :, :], W_d[ds(e, 1), :, :].rearrange("e (c p) n -> p (e c) n", p=P)
                                         ).then_inc(weights_in[u], 16)

                    for u in range(2):
                        rows(u, u, True)
                        weights(u, u, True)
                    with sp.Fori(1, E // 2) as i:
                        for u in range(2):
                            rows(i * 2 + u, u, False)
                            weights(i * 2 + u, u, False)
                    rows(E, 0, False)

                @block.tensor
                def _(pe):
                    def turn(e, i, u):
                        pe.wait_ge(rows_in[u], i * 32 + 32)
                        for c in range(DC):
                            for t, n in SLOTS:
                                last = pe.transpose(ps[:, 6 + c, t * P:t * P + n], xe[0:n, u, t, c * P:(c + 1) * P],
                                                    core.ident[0:n, 0:n])
                        last.then_inc(turned, 1)

                    turn(0, 0, 0)
                    with pe.Fori(0, E // 2) as i:
                        for u in range(2):
                            e = i * 2 + u
                            pe.wait_ge(xeT_ready, e + 1)
                            pe.wait_ge(weights_in[u], i * 48 + 48)
                            for m, w in CHUNKS:
                                pe.wait_ge(act_ready, e * NF + 1 + m // 2)
                                for half, W in ((0, Wg), (1, Wu)):
                                    for c in range(DC):
                                        last = pe.matmul(ps[0:w, 2 * (m % 2) + half, 0:C], W[:, u, c, m * P:m * P + w],
                                                         xeT[:, c, :], start=(c == 0), stop=(c == DC - 1))
                                last.then_inc(gated_full, 1)
                            turn(e + 1, i + u, 1 - u)
                            pe.wait_ge(act_ready, e * NF + NF + 1)
                            pe.wait_ge(ye_ready, e + 1)
                            for t, n in SLOTS:
                                for m, w in CHUNKS:
                                    last = pe.matmul(ps[0:n, 4 + t // 2, t % 2 * D:(t % 2 + 1) * D],
                                                     act_[0:w, m, t * P:t * P + n], Wd[0:w, u, m, :],
                                                     start=(m == 0), stop=(m == NF - 1))
                            last.then_inc(out_full, 1)

                @block.scalar
                def _(act):
                    def evacuate(e):
                        act.wait_ge(turned, e + 1)
                        act.activation(xeT[:, :, :], ps[:, 6:8, 0:C], ACT.Copy).then_inc(xeT_ready, 1)

                    act.sem_inc(ye_ready, 1)
                    for u in range(2):
                        act.sem_inc(stored[u], 32)
                    evacuate(0)
                    with act.Fori(0, E // 2) as i:
                        for u in range(2):
                            e = i * 2 + u
                            for m, w in CHUNKS:
                                act.wait_ge(gated_full, e * NF + m + 1)
                                act.wait_ge(act_ready, e * NF + 1 + m // 2)
                                act.activation(sg[0:w, m % 2, :], ps[0:w, 2 * (m % 2), 0:C],
                                               ACT.Sigmoid).then_inc(sg_ready, 1)
                            evacuate(e + 1)
                            act.wait_ge(out_full, e + 1)
                            act.wait_ge(stored[u], i * 32 + 32)
                            act.activation(ye[:, u, 0:2, :], ps[:, 4, :].rearrange("p (t d) -> p t d", t=2), ACT.Copy)
                            n = SLOTS[-1][1]
                            act.activation(ye[0:n, u, 2, :], ps[0:n, 5, 0:D], ACT.Copy).then_inc(ye_ready, 1)
                            act.wait_ge(ye_ready, e + 2)
                            act.dma_start(OUTS[ds(e * C, 2 * P), :].rearrange("(t p) d -> p t d", p=P),
                                          ye[:, u, 0:2, :]).then_inc(stored[u], 16)
                            act.dma_start(OUTS[ds(e * C + 2 * P, n), :], ye[0:n, u, 2, :]).then_inc(stored[u], 16)
                    for u in range(2):
                        act.wait_ge(stored[u], 32 + E // 2 * 32)

                @block.vector
                def _(dve):
                    dve.sem_inc(act_ready, 1)
                    with dve.Fori(0, E // 2) as i:
                        for u in range(2):
                            e = i * 2 + u
                            for m, w in CHUNKS:
                                dve.wait_ge(sg_ready, e * NF + m + 1)
                                dve.tensor_tensor(sg[0:w, m % 2, :], sg[0:w, m % 2, :], ps[0:w, 2 * (m % 2), 0:C],
                                                  ALU.mult).then_inc(swish_ready, 1)
                                dve.wait_ge(swish_ready, e * NF + m + 1)
                                dve.tensor_tensor(act_[0:w, m, :], sg[0:w, m % 2, :], ps[0:w, 2 * (m % 2) + 1, 0:C],
                                                  ALU.mult).then_inc(act_ready, 1)

        with ExitStack() as ctx_d:
            sd = Scope(nc, ctx_d, "cmoe_combine", s)
            y = [sd.sb(f"y{k}", [P, TILES, D]) for k in range(2)]
            y_in = [core.pool_dma.sem(f"cmoe_y_in{t}") for t in range(4)]
            added = sd.sem("added")
            with nc.Block() as block:
                @block.gpsimd
                def _(pool):
                    for t in range(TILES):
                        for k in range(2):
                            pool.indirect_dma_start(y[k][:, t, :], None, OUTS,
                                                    bass.IndirectOffsetOnAxis(ap=from_row[k][:, t:t + 1], axis=0)
                                                    ).then_inc(y_in[t // 4], 16)

                @block.vector
                def _(dve):
                    for g in range(4):
                        dve.wait_ge(y_in[g], 16 * 8)
                        for k in range(2):
                            for t in range(4 * g, 4 * g + 4):
                                dve.scalar_tensor_tensor(out=h[:, t, :], in0=y[k][:, t, :],
                                                         scalar=weight[k][:, t:t + 1], in1=h[:, t, :],
                                                         op0=ALU.mult, op1=ALU.add).then_inc(added, 1)
                            dve.wait_ge(added, 8 * g + 4 * k + 4)
        s.clear()


def column_attention(nc, core, ln_d, Wqkv_d, Wout_d):
    ps, h = core.ps, core.h
    HD = 64
    H = Wqkv_d.shape[1] // 3 // HD
    HC = H * HD // P
    GROUP, HALF = 32, 16
    GROUPS = SEQ // GROUP
    UH = 8
    UNITS = 2 * H // UH
    MASKED = -1e30
    SCALE = 1.0 / float(np.sqrt(HD))
    with ExitStack() as ctx:
        s = Scope(nc, ctx, "cattn")
        xT_all = s.sb("xT_all", [P, DC, N + GROUP])
        ctxT = s.sb("ctxT", [P, HC, N])
        Wout = s.sb("Wout", [P, HC, D])
        Wqkv = s.sb("Wqkv", [P, DC, 3 * H * HD])
        weights_in = s.sem("weights_in")
        Wout_in = s.sem("Wout_in")

        with ExitStack() as ctx_a:
            sa = Scope(nc, ctx_a, "cattn_norm", s)
            affine = sa.sb("affine", [P, 2, DC])
            affine_in = sa.sem("affine_in")
            pad_zero = sa.sem("pad_zero")
            row = RowNorm(nc, core, sa, LN_EPS, again=1e-6, affine=(affine[:, 0, :], affine[:, 1, :]))
            with nc.Block() as block:
                @block.sync
                def _(sp):
                    sp.dma_start(affine[:, :, :], ln_d).then_inc(affine_in, 16)
                    sp.dma_start(Wqkv[:, :, :], Wqkv_d.rearrange("(c p) n -> p c n", p=P)).then_inc(weights_in, 16)
                    sp.dma_start(Wout[:, :, :], Wout_d.rearrange("(c p) n -> p c n", p=P)).then_inc(Wout_in, 16)

                @block.tensor
                def _(pe):
                    row.turn(pe, 0)
                    with pe.Fori(1, BATCH) as b:
                        pe.wait_ge(row.xT_ready, b)
                        row.turn(pe, b)

                @block.scalar
                def _(act):
                    act.wait_ge(affine_in, 16)
                    with act.Fori(0, BATCH) as b:
                        row.evacuate(act, b, xT_all[:, :, ds(b * SEQ, SEQ)])

                @block.gpsimd
                def _(pool):
                    pool.memset(xT_all[:, :, N:N + GROUP], 0.0).then_inc(pad_zero, 1)
                    with pool.Fori(0, BATCH) as b:
                        row.root(pool, b)
                    pool.wait_ge(pad_zero, 1)

                @block.vector
                def _(dve):
                    row.norm(dve, 0, first=True)
                    with dve.Fori(1, BATCH) as b:
                        row.norm(dve, b)

        with ExitStack() as ctx_b:
            sb_ = Scope(nc, ctx_b, "cattn_heads", s)
            ident16 = sb_.sb("ident16", [P, P], BF16)
            mask = sb_.sb("mask", [P, 4, P], BF16)
            xg = sb_.sb("xg", [P, DC, 2 * P])
            qkT = sb_.sb("qkT", [P, 2 * HC, 2 * P])
            v = sb_.sb("v", [P, 2, H * HD])
            probs = sb_.sb("probs", [P, 4, UH, P])
            probsT = sb_.sb("probsT", [P, 2, UH, P])
            peak = sb_.sb("peak", [P, 2, UH])
            total = sb_.sb("total", [P, 2, UH])
            mask_step = sb_.sem("mask_step")
            xg_ready = sb_.sem("xg_ready")
            scores_full = sb_.sem("scores_full")
            peak_ready = sb_.sem("peak_ready")
            shifted = sb_.sem("shifted")
            exped = sb_.sem("exped")
            total_ready = sb_.sem("total_ready")
            inverse_ready = sb_.sem("inverse_ready")
            probs_ready = sb_.sem("probs_ready")
            turned = sb_.sem("turned")
            probsT_ready = sb_.sem("probsT_ready")
            job_full = sb_.sem("job_full")
            job_read = sb_.sem("job_read")
            JOBS = ["ctx0", "qk0", "qk1", "ctx1", "qk2", "qk3", "ctx2", "qk4", "qk5", "qk6", "qk7", "ctx3",
                    "v0", "v1", "v2", "v3"]
            NJ = len(JOBS)

            with nc.Block() as block:
                @block.gpsimd
                def _(pool):
                    step = Chain(pool, mask_step)
                    step(pool.memset(mask[:, :, :], MASKED))
                    for b in range(BATCH):
                        step(pool.affine_select(out=mask[:, :, :], in_=mask[:, :, :], compare_op=ALU.not_equal,
                                                fill=0.0, base=-b * HALF, pattern=[[0, 4], [-1, P]],
                                                channel_multiplier=1))
                    step(pool.tensor_copy(ident16[:, :], core.ident[:, :]))

                @block.tensor
                def _(pe):
                    def job(name, base):
                        q = JOBS.index(name)
                        pe.wait_ge(job_read, base + q + 1)
                        return 6 + q % 2

                    def qk(j, base):
                        bank = job(f"qk{j}", base)
                        for half in range(2):
                            col = (2 * j + half) * P
                            for c in range(DC):
                                last = pe.matmul(ps[:, bank, half * 2 * P:(half + 1) * 2 * P],
                                                 Wqkv[:, c, col:col + P], xg[:, c, :],
                                                 start=(c == 0), stop=(c == DC - 1))
                        last.then_inc(job_full, 1)

                    def values(i, base):
                        u, half = i // 2, i % 2
                        bank = job(f"v{i}", base)
                        col = (2 * H * HD) + half * 512
                        for c in range(DC):
                            last = pe.matmul(ps[:, bank, :], xg[:, c, u * P:(u + 1) * P],
                                             Wqkv[:, c, col:col + 512], start=(c == 0), stop=(c == DC - 1))
                        last.then_inc(job_full, 1)

                    def scores(k, g):
                        u, m0, bank = k // 2, k % 2 * 4, 2 * (k % 2)
                        pe.wait_ge(shifted, g * UNITS + k + 1)
                        for odd in range(2):
                            pe.matmul(ps[:, bank + odd, :], ident16[:, :], mask[:, :, :].rearrange("p r k -> p (r k)"),
                                      start=True, stop=False, skip_group_check=True)
                        for j in range(4):
                            for odd in range(2):
                                rows = slice(odd * HD, (odd + 1) * HD)
                                last = pe.matmul(ps[:, bank + odd, j * P:(j + 1) * P],
                                                 qkT[rows, m0 + j, u * P:(u + 1) * P],
                                                 qkT[rows, HC + m0 + j, u * P:(u + 1) * P],
                                                 start=False, stop=(j == 3), skip_group_check=True)
                        last.then_inc(scores_full, 1)

                    def turn(k, g):
                        pe.wait_ge(probs_ready, g * UNITS + k + 1)
                        pe.wait_ge(probsT_ready, g * UNITS + k + 1)
                        for i in range(UH):
                            last = pe.transpose(ps[:, 4 + i // 4, i % 4 * P:(i % 4 + 1) * P], probs[:, k, i, :],
                                                core.ident[:, :])
                        last.then_inc(turned, 1)

                    def mix(k, base, g):
                        u, m0 = k // 2, k % 2 * 4
                        bank = job(f"ctx{k}", base)
                        pe.wait_ge(probsT_ready, g * UNITS + k + 2)
                        for j in range(4):
                            for odd in range(2):
                                head = 2 * (m0 + j) + odd
                                last = pe.matmul(ps[odd * HD:(odd + 1) * HD, bank, j * P:(j + 1) * P],
                                                 v[:, u, head * HD:(head + 1) * HD], probsT[:, k % 2, odd * 4 + j, :],
                                                 start=True, stop=True, skip_group_check=True)
                        last.then_inc(job_full, 1)

                    pe.wait_ge(weights_in, 16)
                    pe.wait_ge(mask_step, BATCH + 2)
                    pe.wait_ge(xg_ready, 1)
                    first = 0
                    for j in range(HC):
                        if first >= 2:
                            pe.wait_ge(job_read, 2 + first - 1)
                        for half in range(2):
                            col = (2 * j + half) * P
                            for c in range(DC):
                                last = pe.matmul(ps[:, 6 + first % 2, half * 2 * P:(half + 1) * 2 * P],
                                                 Wqkv[:, c, col:col + P], xg[:, c, :],
                                                 start=(c == 0), stop=(c == DC - 1))
                        last.then_inc(job_full, 1)
                        first += 1
                    for u in range(2):
                        for half in range(2):
                            pe.wait_ge(job_read, 2 + first - 1)
                            col = (2 * H * HD) + half * 512
                            for c in range(DC):
                                last = pe.matmul(ps[:, 6 + first % 2, :], xg[:, c, u * P:(u + 1) * P],
                                                 Wqkv[:, c, col:col + 512], start=(c == 0), stop=(c == DC - 1))
                            last.then_inc(job_full, 1)
                            first += 1
                    assert first == HC + 4 and first % 2 == 0

                    pe.wait_ge(job_read, 2 + HC)
                    scores(0, 0)
                    scores(1, 0)
                    with pe.Fori(0, GROUPS) as g:
                        base = g * NJ + first
                        scores(2, g)
                        turn(0, g)
                        scores(3, g)
                        turn(1, g)
                        pe.wait_ge(job_read, base + 2)
                        mix(0, base, g)
                        pe.wait_ge(xg_ready, g + 2)
                        qk(0, base)
                        qk(1, base)
                        turn(2, g)
                        mix(1, base, g)
                        qk(2, base)
                        qk(3, base)
                        turn(3, g)
                        mix(2, base, g)
                        for j in range(4, HC):
                            qk(j, base)
                        mix(3, base, g)
                        values(0, base)
                        pe.wait_ge(job_read, base + 2 + JOBS.index("qk7") + 1)
                        scores(0, g + 1)
                        values(1, base)
                        scores(1, g + 1)
                        values(2, base)
                        values(3, base)

                @block.scalar
                def _(act):
                    def read(n, out, src):
                        act.wait_ge(job_full, n + 1)
                        act.activation(out, src, ACT.Copy).then_inc(job_read, 1)

                    def read_qk(n, j, bank):
                        read(n, qkT[:, 2 * j:2 * j + 2, :], ps[:, bank, :].rearrange("p (m n) -> p m n", m=2))

                    def read_v(n, u, half, bank):
                        read(n, v[:, u, half * 512:(half + 1) * 512], ps[:, bank, :])

                    def read_ctx(n, k, g, bank):
                        u, m0 = k // 2, k % 2 * 4
                        out = ctxT[:, m0:m0 + 4, :].rearrange("p m (b s) -> p m b s", s=SEQ)
                        act.wait_ge(job_full, n + 1)
                        for j in range(4):
                            ins = act.activation(out[:, j, :, ds(g * GROUP + u * HALF, HALF)],
                                                 ps[:, bank, j * P:(j + 1) * P].rearrange("p (b s) -> p b s", s=HALF),
                                                 ACT.Copy)
                        ins.then_inc(job_read, 1)

                    def exp(k, g):
                        act.wait_ge(shifted, g * UNITS + k + 3)
                        act.activation(probs[:, k, :, :], probs[:, k, :, :], ACT.Exp,
                                       scale=SCALE).then_inc(exped, 1)

                    def read_probsT(k, g):
                        act.wait_ge(turned, g * UNITS + k + 1)
                        act.activation(probsT[:, k % 2, :, :].rearrange("p (x i) n -> p x (i n)", x=2), ps[:, 4:6, :],
                                       ACT.Copy).then_inc(probsT_ready, 1)

                    act.sem_inc(job_read, 2)
                    act.sem_inc(probsT_ready, 1)
                    for j in range(HC):
                        read_qk(j, j, 6 + j % 2)
                    for i in range(4):
                        read_v(HC + i, i // 2, i % 2, 6 + (HC + i) % 2)
                    first = HC + 4
                    exp(0, 0)
                    exp(1, 0)
                    with act.Fori(0, GROUPS) as g:
                        base = g * NJ + first

                        def next_qk(j):
                            q = JOBS.index(f"qk{j}")
                            read_qk(base + q, j, 6 + q % 2)

                        def next_v(i):
                            q = JOBS.index(f"v{i}")
                            read_v(base + q, i // 2, i % 2, 6 + q % 2)

                        def mixed(k):
                            q = JOBS.index(f"ctx{k}")
                            read_ctx(base + q, k, g, 6 + q % 2)

                        read_probsT(0, g)
                        exp(2, g)
                        read_probsT(1, g)
                        mixed(0)
                        exp(3, g)
                        next_qk(0)
                        next_qk(1)
                        read_probsT(2, g)
                        mixed(1)
                        next_qk(2)
                        next_qk(3)
                        read_probsT(3, g)
                        mixed(2)
                        for j in range(4, HC):
                            next_qk(j)
                        mixed(3)
                        next_v(0)
                        exp(0, g + 1)
                        next_v(1)
                        exp(1, g + 1)
                        next_v(2)
                        next_v(3)

                @block.vector
                def _(dve):
                    columns_of = xT_all[:, :, 0:N].rearrange("p c (b s) -> p c b s", s=SEQ)
                    tail = xT_all[:, :, GROUP:N + GROUP].rearrange("p c (b s) -> p c b s", s=SEQ)

                    def group_columns(first):
                        for u in range(2):
                            for c in range(DC):
                                if first is None:
                                    src = columns_of[:, c, :, u * HALF:(u + 1) * HALF]
                                else:
                                    src = tail[:, c, :, ds(first * GROUP + u * HALF, HALF)]
                                ins = dve.tensor_copy(xg[:, c, u * P:(u + 1) * P].rearrange("p (b s) -> p b s", s=HALF),
                                                      src)
                        ins.then_inc(xg_ready, 1)

                    def softmax(k, g):
                        n = g * UNITS + k
                        bank, x = 2 * (k % 2), k % 2
                        scores = ps[:, bank:bank + 2, :].rearrange("p x (i n) -> p (x i) n", i=4)
                        dve.wait_ge(scores_full, n + 1)
                        dve.tensor_reduce(peak[:, x, :], scores, AX_X, ALU.max).then_inc(peak_ready, 1)
                        dve.wait_ge(peak_ready, n + 1)
                        dve.tensor_tensor(probs[:, k, :, :], scores,
                                          peak[:, x, :].unsqueeze(2).broadcast_to([P, UH, P]),
                                          ALU.subtract).then_inc(shifted, 1)

                    def normalise(k, g):
                        n = g * UNITS + k
                        x = k % 2
                        dve.wait_ge(exped, n + 1)
                        dve.tensor_reduce(total[:, x, :], probs[:, k, :, :], AX_X, ALU.add).then_inc(total_ready, 1)
                        dve.wait_ge(total_ready, n + 1)
                        dve.reciprocal(total[:, x, :], total[:, x, :]).then_inc(inverse_ready, 1)
                        dve.wait_ge(inverse_ready, n + 1)
                        dve.tensor_tensor(probs[:, k, :, :], probs[:, k, :, :],
                                          total[:, x, :].unsqueeze(2).broadcast_to([P, UH, P]),
                                          ALU.mult).then_inc(probs_ready, 1)

                    dve.sem_inc(shifted, 2)
                    group_columns(None)
                    softmax(0, 0)
                    softmax(1, 0)
                    normalise(0, 0)
                    normalise(1, 0)
                    with dve.Fori(0, GROUPS) as g:
                        softmax(2, g)
                        dve.wait_ge(job_full, g * NJ + HC + 4)
                        group_columns(g)
                        softmax(3, g)
                        normalise(2, g)
                        normalise(3, g)
                        softmax(0, g + 1)
                        softmax(1, g + 1)
                        normalise(0, g + 1)
                        normalise(1, g + 1)

        with ExitStack() as ctx_c:
            sc = Scope(nc, ctx_c, "cattn_out", s)
            rowT = sc.sb("rowT", [P, 2, HC, SEQ])
            rowT_ready = sc.sem("rowT_ready")
            out_full = sc.sem("out_full")
            row_added = sc.sem("row_added")
            with nc.Block() as block:
                @block.tensor
                def _(pe):
                    pe.wait_ge(Wout_in, 16)
                    with pe.Fori(0, BATCH // 2) as i:
                        for u in range(2):
                            pe.wait_ge(rowT_ready, i * 2 + u + 1)
                            pe.wait_ge(row_added, i * 2 + u + 1)
                            for t in range(TPB):
                                for c in range(HC):
                                    last = pe.matmul(ps[:, u, t * D:(t + 1) * D], rowT[:, u, c, t * P:(t + 1) * P],
                                                     Wout[:, c, :], start=(c == 0), stop=(c == HC - 1))
                            last.then_inc(out_full, 1)

                @block.scalar
                def _(act):
                    for u in range(2):
                        act.activation(rowT[:, u, :, :], ctxT[:, :, u * SEQ:(u + 1) * SEQ],
                                       ACT.Copy).then_inc(rowT_ready, 1)
                    with act.Fori(1, BATCH // 2) as i:
                        for u in range(2):
                            act.wait_ge(out_full, i * 2 + u - 1)
                            act.activation(rowT[:, u, :, :], ctxT[:, :, ds(i * (2 * SEQ) + u * SEQ, SEQ)],
                                           ACT.Copy).then_inc(rowT_ready, 1)

                @block.vector
                def _(dve):
                    dve.sem_inc(row_added, 2)
                    with dve.Fori(0, BATCH // 2) as i:
                        for u in range(2):
                            dve.wait_ge(out_full, i * 2 + u + 1)
                            dve.tensor_tensor(h[:, ds(i * 4 + 2 * u, TPB), :],
                                              ps[:, u, :].rearrange("p (t d) -> p t d", t=TPB),
                                              h[:, ds(i * 4 + 2 * u, TPB), :], ALU.add).then_inc(row_added, 1)
        s.clear()


def top1_blocks(E):
    return (N - E) // BLOCK + E


BLOCK = 256


def top1_moe(nc, core, router_w_d, router_b_d, w1_d, w2_d, ROWS, OUTS):
    ps, xT, xr, h = core.ps, core.xT, core.xr, core.h
    E, _, F2 = w1_d.shape
    F = F2 // 2
    FC = F // P
    NB = top1_blocks(E)
    TB = BLOCK // P
    ZERO = (NB + 1) * BLOCK * D // P // 4
    with ExitStack() as ctx:
        s = Scope(nc, ctx, "tmoe")
        xn = s.sb("xn", [P, TILES, D])
        r = Router(nc, core, s, E, 1)
        blocks = s.sb("blocks", [P, E])
        ends = [s.sb(f"ends{k}", [P, E]) for k in range(2)]
        block_no = s.sb("block_no", [P, NB, E])
        passed = s.sb("passed", [P, NB, E])
        block_expert_f = s.sb("block_expert_f", [P, NB])
        block_expert = s.sb("block_expert", [P, NB], I32)
        slot = s.sb("slot", [P, TILES])
        row_of = s.sb("row_of", [P, TILES], I32)
        zeros_done = s.sem("zeros_done")

        with ExitStack() as ctx_a:
            sa = Scope(nc, ctx_a, "tmoe_norm", s)
            Wr = sa.sb("Wr", [P, DC, E])
            br = sa.sb("br", [P, E])
            zeros = sa.sb("zeros", [P, ZERO])
            zeros_made = sa.sem("zeros_made")
            weights_in = sa.sem("weights_in")
            logits_full = sa.sem("logits_full")
            logits_ready = sa.sem("logits_ready")
            xn_ready = sa.sem("xn_ready")
            row = RowNorm(nc, core, sa)

            with nc.Block() as block:
                @block.sync
                def _(sp):
                    sp.dma_start(Wr[:, :, :], router_w_d.rearrange("(c p) n -> p c n", p=P)).then_inc(weights_in, 16)
                    sp.dma_start(br[:, :], router_b_d.partition_broadcast(P)).then_inc(weights_in, 16)
                    sp.wait_ge(zeros_made, 1)
                    rows = ROWS.rearrange("(q a) d -> q (a d)", q=4 * P)
                    for q in range(4):
                        sp.dma_start(rows[q * P:(q + 1) * P, :], zeros[:, :]).then_inc(zeros_done, 16)
                    sp.wait_ge(zeros_done, 64)

                @block.tensor
                def _(pe):
                    row.turn(pe, 0)
                    pe.wait_ge(weights_in, 32)
                    with pe.Fori(0, BATCH) as b:
                        pe.wait_ge(row.xT_ready, b + 1)
                        pe.wait_ge(logits_ready, b + 1)
                        for t in range(TPB):
                            for c in range(DC):
                                last = pe.matmul(ps[:, 4, t * E:(t + 1) * E], xT[:, c, t * P:(t + 1) * P], Wr[:, c, :],
                                                 start=(c == 0), stop=(c == DC - 1))
                        last.then_inc(logits_full, 1)
                        row.turn(pe, b + 1)

                @block.scalar
                def _(act):
                    row.evacuate(act, 0)
                    with act.Fori(0, BATCH) as b:
                        row.evacuate(act, b + 1)

                @block.gpsimd
                def _(pool):
                    pool.memset(zeros[:, :], 0.0).then_inc(zeros_made, 1)
                    row.root(pool, 0)
                    with pool.Fori(0, BATCH) as b:
                        row.root(pool, b + 1)
                    r.tables(pool)
                    pool.iota(block_no[:, :, :], pattern=[[1, NB], [0, E]], base=0, channel_multiplier=0,
                              allow_small_or_imprecise_dtypes=True).then_inc(r.made, 1)
                    pool.wait_ge(r.made, 3)

                @block.vector
                def _(dve):
                    dve.sem_inc(logits_ready, 1)
                    row.norm(dve, 0, first=True)
                    dve.wait_ge(weights_in, 32)
                    with dve.Fori(0, BATCH) as b:
                        dve.wait_ge(row.row_normed, b * TPB + TPB)
                        dve.tensor_tensor(xn[:, ds(b * TPB, TPB), :], xr[:, :, :], xr[:, :, :],
                                          ALU.max).then_inc(xn_ready, 1)
                        row.norm(dve, b + 1)
                        dve.wait_ge(logits_full, b + 1)
                        dve.tensor_tensor(r.logits[:, ds(b * TPB, TPB), :],
                                          ps[:, 4, 0:TPB * E].rearrange("p (t e) -> p t e", e=E),
                                          br[:, :].unsqueeze(1).broadcast_to([P, TPB, E]),
                                          ALU.add).then_inc(logits_ready, 1)
                    dve.wait_ge(xn_ready, BATCH)
                    dve.wait_ge(logits_ready, BATCH + 1)

        with ExitStack() as ctx_b:
            sb_ = Scope(nc, ctx_b, "tmoe_route", s)
            rows_ready = sb_.sem("rows_ready")
            scattered = core.pool_dma.sem("tmoe_scattered")
            with nc.Block() as block:
                @block.scalar
                def _(act):
                    r.exp(act)

                @block.tensor
                def _(pe):
                    r.count_before(pe)

                @block.vector
                def _(dve):
                    step, count, tmp = r.route(dve)
                    step(dve.tensor_scalar(blocks[:, :], count, 0.0, None, ALU.is_gt))
                    for k in range(1, N // BLOCK):
                        step(dve.scalar_tensor_tensor(out=blocks[:, :], in0=count, scalar=float(k * BLOCK),
                                                      in1=blocks[:, :], op0=ALU.is_gt, op1=ALU.add))
                    a, b = ends
                    step(dve.tensor_copy(a[:, :], blocks[:, :]))
                    d = 1
                    while d < E:
                        step(dve.tensor_copy(b[:, 0:d], a[:, 0:d]))
                        step(dve.tensor_tensor(b[:, d:E], a[:, d:E], a[:, 0:E - d], ALU.add))
                        a, b = b, a
                        d *= 2
                    step(dve.tensor_tensor(b[:, :], a[:, :], blocks[:, :], ALU.subtract))
                    step(dve.tensor_scalar(b[:, :], b[:, :], float(BLOCK), None, ALU.mult))
                    step(dve.tensor_tensor(r.pos[:, :, :], r.pos[:, :, :],
                                           b[:, :].unsqueeze(1).broadcast_to([P, TILES, E]), ALU.add))
                    step(dve.tensor_tensor(tmp[:, :, :], r.hot[0][:, :, :], r.pos[:, :, :], ALU.mult))
                    step(dve.tensor_reduce(slot[:, :], tmp[:, :, :], AX_X, ALU.add))
                    dve.tensor_copy(row_of[:, :], slot[:, :]).then_inc(rows_ready, 1)
                    step(dve.tensor_tensor(passed[:, :, :], block_no[:, :, :],
                                           a[:, :].unsqueeze(1).broadcast_to([P, NB, E]), ALU.is_ge))
                    step(dve.tensor_reduce(block_expert_f[:, :], passed[:, :, :], AX_X, ALU.add))
                    step(dve.tensor_scalar(block_expert_f[:, :], block_expert_f[:, :], float(E - 1), None, ALU.min))
                    step(dve.tensor_copy(block_expert[:, :], block_expert_f[:, :]))

                @block.gpsimd
                def _(pool):
                    pool.wait_ge(rows_ready, 1)
                    for t in range(TILES):
                        pool.indirect_dma_start(ROWS, bass.IndirectOffsetOnAxis(ap=row_of[:, t:t + 1], axis=0),
                                                xn[:, t, :], None).then_inc(scattered, 16)
                    pool.wait_ge(scattered, 16 * TILES)

        with ExitStack() as ctx_c:
            sc = Scope(nc, ctx_c, "tmoe_blocks", s)
            W1 = sc.sb("W1", [P, 2, DC, F2])
            W2 = sc.sb("W2", [P, 2, FC, D])
            xe = sc.sb("xe", [P, 2, TB, D])
            xeT = sc.sb("xeT", [P, DC, BLOCK])
            sg = sc.sb("sg", [P, 2, BLOCK])
            act_ = sc.sb("act", [P, FC, BLOCK])
            ye = sc.sb("ye", [P, 2, TB, D])
            weights_in = [sc.sem(f"weights_in{u}") for u in range(2)]
            rows_in = [sc.sem(f"rows_in{u}") for u in range(2)]
            turned = sc.sem("turned")
            xeT_ready = sc.sem("xeT_ready")
            gated_full = sc.sem("gated_full")
            sg_ready = sc.sem("sg_ready")
            swish_ready = sc.sem("swish_ready")
            act_ready = sc.sem("act_ready")
            out_full = sc.sem("out_full")
            ye_ready = sc.sem("ye_ready")
            stored = [sc.sem(f"stored{u}") for u in range(2)]
            PAIRS = NB // 2
            assert NB % 2 == 1

            with nc.Block() as block:
                @block.sync
                def _(sp):
                    def rows(j, u, first):
                        if not first:
                            sp.wait_ge(turned, j - 1)
                        sp.dma_start(xe[:, u, :, :], ROWS[ds(j * BLOCK, BLOCK), :].rearrange("(t p) d -> p t d", p=P)
                                     ).then_inc(rows_in[u], 16)

                    def weights(j, u, first):
                        e = sp.value_load(block_expert[0:1, ds(j, 1)], min_val=0, max_val=E - 1)
                        if not first:
                            sp.wait_ge(out_full, j - 1)
                        sp.dma_start(W1[:, u, :, :], w1_d[ds(e, 1), :, :].rearrange("e (c p) n -> p (e c) n", p=P)
                                     ).then_inc(weights_in[u], 16)
                        sp.dma_start(W2[:, u, :, :], w2_d[ds(e, 1), :, :].rearrange("e (c p) n -> p (e c) n", p=P)
                                     ).then_inc(weights_in[u], 16)

                    for u in range(2):
                        rows(u, u, True)
                        weights(u, u, True)
                    with sp.Fori(1, PAIRS) as i:
                        for u in range(2):
                            rows(i * 2 + u, u, False)
                            weights(i * 2 + u, u, False)
                    rows(NB - 1, 0, False)
                    weights(NB - 1, 0, False)
                    rows(NB, 1, False)
                    sp.wait_ge(rows_in[1], 16 * (NB + 1) // 2)

                @block.tensor
                def _(pe):
                    def turn(j, i, u):
                        pe.wait_ge(rows_in[u], i * 16 + 16)
                        for c in range(DC):
                            for t in range(TB):
                                last = pe.transpose(ps[:, 7, c * BLOCK + t * P:c * BLOCK + (t + 1) * P],
                                                    xe[:, u, t, c * P:(c + 1) * P], core.ident[:, :])
                        last.then_inc(turned, 1)

                    def mlp(j, i, u):
                        pe.wait_ge(xeT_ready, j + 1)
                        pe.wait_ge(weights_in[u], i * 32 + 32)
                        for m in range(FC):
                            pe.wait_ge(act_ready, j * FC + m + 1)
                            for half in range(2):
                                for c in range(DC):
                                    last = pe.matmul(ps[:, m % 4, half * BLOCK:(half + 1) * BLOCK],
                                                     W1[:, u, c, half * F + m * P:half * F + (m + 1) * P],
                                                     xeT[:, c, :], start=(c == 0), stop=(c == DC - 1))
                            last.then_inc(gated_full, 1)
                        turn(j + 1, i + u, 1 - u)
                        pe.wait_ge(ye_ready, j + 1)
                        pe.wait_ge(act_ready, j * FC + FC + 4)
                        for t in range(TB):
                            for m in range(FC):
                                last = pe.matmul(ps[:, 5, t * D:(t + 1) * D], act_[:, m, t * P:(t + 1) * P],
                                                 W2[:, u, m, :], start=(m == 0), stop=(m == FC - 1))
                        last.then_inc(out_full, 1)

                    turn(0, 0, 0)
                    with pe.Fori(0, PAIRS) as i:
                        for u in range(2):
                            mlp(i * 2 + u, i, u)
                    mlp(NB - 1, PAIRS, 0)

                @block.scalar
                def _(act):
                    def evacuate(j):
                        act.wait_ge(turned, j + 1)
                        act.activation(xeT[:, :, :], ps[:, 7, :].rearrange("p (c n) -> p c n", c=DC),
                                       ACT.Copy).then_inc(xeT_ready, 1)

                    def mlp(j, i, u):
                        for m in range(FC):
                            act.wait_ge(gated_full, j * FC + m + 1)
                            act.wait_ge(act_ready, j * FC + m + 3)
                            act.activation(sg[:, m % 2, :], ps[:, m % 4, 0:BLOCK], ACT.Sigmoid).then_inc(sg_ready, 1)
                        evacuate(j + 1)
                        act.wait_ge(out_full, j + 1)
                        act.wait_ge(stored[u], i * 16 + 16)
                        act.activation(ye[:, u, :, :], ps[:, 5, :].rearrange("p (t d) -> p t d", t=TB),
                                       ACT.Copy).then_inc(ye_ready, 1)
                        act.wait_ge(ye_ready, j + 2)
                        act.dma_start(OUTS[ds(j * BLOCK, BLOCK), :].rearrange("(t p) d -> p t d", p=P),
                                      ye[:, u, :, :]).then_inc(stored[u], 16)

                    act.sem_inc(ye_ready, 1)
                    for u in range(2):
                        act.sem_inc(stored[u], 16)
                    evacuate(0)
                    with act.Fori(0, PAIRS) as i:
                        for u in range(2):
                            mlp(i * 2 + u, i, u)
                    mlp(NB - 1, PAIRS, 0)
                    act.wait_ge(stored[0], 16 + 16 * (PAIRS + 1))
                    act.wait_ge(stored[1], 16 + 16 * PAIRS)

                @block.vector
                def _(dve):
                    def mlp(j):
                        for m in range(FC):
                            dve.wait_ge(sg_ready, j * FC + m + 1)
                            dve.tensor_tensor(sg[:, m % 2, :], sg[:, m % 2, :], ps[:, m % 4, 0:BLOCK],
                                              ALU.mult).then_inc(swish_ready, 1)
                            dve.wait_ge(swish_ready, j * FC + m + 1)
                            dve.tensor_tensor(act_[:, m, :], sg[:, m % 2, :], ps[:, m % 4, BLOCK:2 * BLOCK],
                                              ALU.mult).then_inc(act_ready, 1)

                    dve.sem_inc(act_ready, 4)
                    with dve.Fori(0, NB) as j:
                        mlp(j)

        with ExitStack() as ctx_d:
            sd = Scope(nc, ctx_d, "tmoe_combine", s)
            y = sd.sb("y", [P, TILES, D])
            y_in = [core.pool_dma.sem(f"tmoe_y_in{t}") for t in range(4)]
            added = sd.sem("added")
            with nc.Block() as block:
                @block.gpsimd
                def _(pool):
                    for t in range(TILES):
                        pool.indirect_dma_start(y[:, t, :], None, OUTS,
                                                bass.IndirectOffsetOnAxis(ap=row_of[:, t:t + 1], axis=0)
                                                ).then_inc(y_in[t // 4], 16)

                @block.vector
                def _(dve):
                    for g in range(4):
                        dve.wait_ge(y_in[g], 16 * 4)
                        for t in range(4 * g, 4 * g + 4):
                            dve.scalar_tensor_tensor(out=h[:, t, :], in0=y[:, t, :], scalar=r.top[0][:, t:t + 1],
                                                     in1=h[:, t, :], op0=ALU.mult, op1=ALU.add).then_inc(added, 1)
        s.clear()


def row_attention(nc, core, Wqkv_d, bq_d, bk_d, bv_d, Wproj_d, bproj_d):
    ps, xT, h = core.ps, core.xT, core.h
    H, HD = 16, 16
    UH = 4
    UNITS = TPB * H // UH
    PER_CHUNK = P // HD
    SCALE = 1.0 / float(np.sqrt(HD))
    JOBS = ["mix0", "mix1", "mix2", "mix3", "mix4", "outT0", "q", "k0", "k1", "proj0", "mix5", "mix6", "mix7", "v",
            "outT1", "proj1"]
    BY_ACT = [j for j in JOBS if j[0] in "okq"]
    BY_DVE = [j for j in JOBS if j not in BY_ACT]
    with ExitStack() as ctx:
        s = Scope(nc, ctx, "rattn")
        Wqkv = s.sb("Wqkv", [P, DC, 3 * D])
        Wproj = s.sb("Wproj", [P, DC, D])
        bq = s.sb("bq", [P, DC])
        bk = s.sb("bk", [P, DC])
        bv = s.sb("bv", [P, D])
        bproj = s.sb("bproj", [P, D])
        mask = s.sb("mask", [P, PER_CHUNK])
        qT = s.sb("qT", [P, DC, SEQ])
        kT = s.sb("kT", [P, DC, SEQ])
        keys = s.sb("keys", [P, H, SEQ])
        v = s.sb("v", [P, TPB, H, HD + 1])
        probs = s.sb("probs", [P, 4, UH, SEQ])
        probsT = s.sb("probsT", [P, 2, UH * TPB, P])
        peak = s.sb("peak", [P, 2, UH])
        inverse = s.sb("inverse", [P, 2, UH])
        out = s.sb("out", [P, TPB, D])
        outT = s.sb("outT", [P, TPB, DC, P])
        weights_in = s.sem("weights_in")
        mask_step = s.sem("mask_step")
        keys_ready = s.sem("keys_ready")
        ones_set = s.sem("ones_set")
        scores_full = s.sem("scores_full")
        peak_ready = s.sem("peak_ready")
        shifted = s.sem("shifted")
        exped = s.sem("exped")
        turned = s.sem("turned")
        probsT_ready = s.sem("probsT_ready")
        inverse_ready = s.sem("inverse_ready")
        job_full = s.sem("job_full")
        act_read = s.sem("act_read")
        dve_read = s.sem("dve_read")
        product_added = s.sem("product_added")
        row = RowNorm(nc, core, s)

        def bank(name):
            return 6 + JOBS.index(name) % 2

        def full(name, b):
            return b * len(JOBS) + (4 + JOBS.index(name) + 1)

        def act_count(name, b):
            return b * len(BY_ACT) + (len(BY_ACT) + BY_ACT.index(name) + 1)

        def dve_count(name, b):
            return b * len(BY_DVE) + (len(BY_DVE) + BY_DVE.index(name) + 1)

        with nc.Block() as block:
            @block.sync
            def _(sp):
                sp.dma_start(Wqkv[:, :, :], Wqkv_d.rearrange("(c p) n -> p c n", p=P)).then_inc(weights_in, 16)
                sp.dma_start(bq[:, :], bq_d).then_inc(weights_in, 16)
                sp.dma_start(bk[:, :], bk_d).then_inc(weights_in, 16)
                sp.dma_start(bv[:, :], bv_d.partition_broadcast(P)).then_inc(weights_in, 16)
                sp.dma_start(bproj[:, :], bproj_d.partition_broadcast(P)).then_inc(weights_in, 16)
                sp.dma_start(Wproj[:, :, :], Wproj_d.rearrange("(c p) n -> p c n", p=P)).then_inc(weights_in, 16)

            @block.gpsimd
            def _(pool):
                step = Chain(pool, mask_step)
                step(pool.memset(mask[:, :], 1.0))
                step(pool.affine_select(out=mask[:, :], in_=mask[:, :], compare_op=ALU.is_ge, fill=0.0, base=0,
                                        pattern=[[-HD, PER_CHUNK]], channel_multiplier=1))
                step(pool.affine_select(out=mask[:, :], in_=mask[:, :], compare_op=ALU.is_ge, fill=0.0, base=HD - 1,
                                        pattern=[[HD, PER_CHUNK]], channel_multiplier=-1))
                pool.memset(v[:, :, :, HD:HD + 1], 1.0).then_inc(ones_set, 1)

                def spread_keys(b):
                    for m in range(DC):
                        pool.wait_ge(act_read, act_count(f"k{m}", b))
                        pool.tensor_tensor(keys[:, m * PER_CHUNK:(m + 1) * PER_CHUNK, :],
                                           kT[:, m, :].unsqueeze(1).broadcast_to([P, PER_CHUNK, SEQ]),
                                           mask[:, :].unsqueeze(2).broadcast_to([P, PER_CHUNK, SEQ]),
                                           ALU.mult).then_inc(keys_ready, 1)

                row.root(pool, 0)
                pool.wait_ge(mask_step, 3)
                spread_keys(-1)
                with pool.Fori(0, BATCH) as b:
                    row.root(pool, b + 1)
                    spread_keys(b)

            @block.tensor
            def _(pe):
                def bank_free(name, b):
                    q = JOBS.index(name)
                    before = JOBS[q - 2]
                    if q < 2:
                        b = b - 1
                    if before in BY_ACT:
                        pe.wait_ge(act_read, act_count(before, b))
                    else:
                        pe.wait_ge(dve_read, dve_count(before, b))

                def scores(k, b):
                    u, c, x = k // (H // UH), k % (H // UH) // 2, 2 * (k % 2)
                    pe.wait_ge(shifted, b * UNITS + k + 1)
                    for i in range(2):
                        head = k % (H // UH) * UH + 2 * i
                        last = pe.matmul(ps[:, x + i, :], qT[:, c, u * P:(u + 1) * P],
                                         keys[:, head:head + 2, :].rearrange("p h n -> p (h n)"),
                                         start=True, stop=True)
                    last.then_inc(scores_full, 1)

                def turn_probs(k, b):
                    pe.wait_ge(exped, b * UNITS + k + 1)
                    pe.wait_ge(probsT_ready, b * UNITS + k + 1)
                    for i in range(UH):
                        for t in range(TPB):
                            n = i * TPB + t
                            last = pe.transpose(ps[:, 4 + n // 4, n % 4 * P:(n % 4 + 1) * P],
                                                probs[:, k % 4, i, t * P:(t + 1) * P], core.ident[:, :])
                    last.then_inc(turned, 1)

                def mix(k, b):
                    bank_free(f"mix{k}", b)
                    pe.wait_ge(probsT_ready, b * UNITS + k + 2)
                    for i in range(UH):
                        head = k % (H // UH) * UH + i
                        for t in range(TPB):
                            last = pe.matmul(ps[:, bank(f"mix{k}"), i * (HD + 1):(i + 1) * (HD + 1)],
                                             probsT[:, k % 2, i * TPB + t, :], v[:, t, head, :],
                                             start=(t == 0), stop=(t == TPB - 1))
                    last.then_inc(job_full, 1)

                def out_turn(u, b):
                    pe.wait_ge(dve_read, dve_count(f"mix{4 * u + 3}", b))
                    bank_free(f"outT{u}", b)
                    for c in range(DC):
                        last = pe.transpose(ps[:, bank(f"outT{u}"), c * P:(c + 1) * P], out[:, u, c * P:(c + 1) * P],
                                            core.ident[:, :])
                    last.then_inc(job_full, 1)

                def project(u, b):
                    pe.wait_ge(act_read, act_count(f"outT{u}", b))
                    bank_free(f"proj{u}", b)
                    for c in range(DC):
                        last = pe.matmul(ps[:, bank(f"proj{u}"), 0:D], outT[:, u, c, :], Wproj[:, c, :],
                                         start=(c == 0), stop=(c == DC - 1))
                    last.then_inc(job_full, 1)

                def queries():
                    for m in range(DC):
                        for c in range(DC):
                            last = pe.matmul(ps[:, bank("q"), m * SEQ:(m + 1) * SEQ], Wqkv[:, c, m * P:(m + 1) * P],
                                             xT[:, c, :], start=(c == 0), stop=(c == DC - 1))
                    last.then_inc(job_full, 1)

                def key_chunk(m):
                    for c in range(DC):
                        last = pe.matmul(ps[:, bank(f"k{m}"), 0:SEQ], Wqkv[:, c, D + m * P:D + (m + 1) * P],
                                         xT[:, c, :], start=(c == 0), stop=(c == DC - 1))
                    last.then_inc(job_full, 1)

                def values():
                    for t in range(TPB):
                        for c in range(DC):
                            last = pe.matmul(ps[:, bank("v"), t * D:(t + 1) * D], xT[:, c, t * P:(t + 1) * P],
                                             Wqkv[:, c, 2 * D:3 * D], start=(c == 0), stop=(c == DC - 1))
                    last.then_inc(job_full, 1)

                row.turn(pe, 0)
                pe.wait_ge(weights_in, 96)
                pe.wait_ge(row.xT_ready, 1)
                queries()
                key_chunk(0)
                pe.wait_ge(act_read, act_count("q", -1))
                key_chunk(1)
                pe.wait_ge(act_read, act_count("k0", -1))
                values()
                pe.wait_ge(ones_set, 1)
                pe.wait_ge(keys_ready, DC)
                scores(0, 0)
                scores(1, 0)
                with pe.Fori(0, BATCH) as b:
                    scores(2, b)
                    turn_probs(0, b)
                    scores(3, b)
                    turn_probs(1, b)
                    pe.wait_ge(dve_read, dve_count("v", b - 1))
                    mix(0, b)
                    row.turn(pe, b + 1)
                    scores(4, b)
                    turn_probs(2, b)
                    pe.wait_ge(row.xT_ready, b + 2)
                    mix(1, b)
                    for k in range(3, 6):
                        scores(k + 2, b)
                        turn_probs(k, b)
                        mix(k - 1, b)
                    out_turn(0, b)
                    bank_free("q", b)
                    queries()
                    for m in range(DC):
                        bank_free(f"k{m}", b)
                        key_chunk(m)
                    turn_probs(6, b)
                    project(0, b)
                    mix(5, b)
                    turn_probs(7, b)
                    mix(6, b)
                    pe.wait_ge(keys_ready, (b + 2) * DC)
                    scores(0, b + 1)
                    mix(7, b)
                    scores(1, b + 1)
                    bank_free("v", b)
                    values()
                    out_turn(1, b)
                    project(1, b)

            @block.scalar
            def _(act):
                def read_q(b):
                    act.wait_ge(job_full, full("q", b))
                    for m in range(DC):
                        ins = act.activation(qT[:, m, :], ps[:, bank("q"), m * SEQ:(m + 1) * SEQ], ACT.Identity,
                                             bias=bq[:, m:m + 1])
                    ins.then_inc(act_read, 1)

                def read_k(m, b):
                    act.wait_ge(job_full, full(f"k{m}", b))
                    act.activation(kT[:, m, :], ps[:, bank(f"k{m}"), 0:SEQ], ACT.Identity,
                                   bias=bk[:, m:m + 1]).then_inc(act_read, 1)

                def exp(k, b):
                    act.wait_ge(shifted, b * UNITS + k + 3)
                    act.activation(probs[:, k % 4, :, :], probs[:, k % 4, :, :], ACT.Exp, scale=SCALE).then_inc(exped, 1)

                def read_probsT(k, b):
                    act.wait_ge(turned, b * UNITS + k + 1)
                    act.activation(probsT[:, k % 2, :, :].rearrange("p (x i) n -> p x (i n)", x=2), ps[:, 4:6, :],
                                   ACT.Copy).then_inc(probsT_ready, 1)

                def read_outT(u, b):
                    act.wait_ge(job_full, full(f"outT{u}", b))
                    act.activation(outT[:, u, :, :], ps[:, bank(f"outT{u}"), 0:D].rearrange("p (c n) -> p c n", c=DC),
                                   ACT.Copy).then_inc(act_read, 1)

                act.sem_inc(act_read, BY_ACT.index("q"))
                act.sem_inc(probsT_ready, 1)
                row.evacuate(act, 0)
                act.wait_ge(weights_in, 96)
                act.wait_ge(job_full, 1)
                for m in range(DC):
                    ins = act.activation(qT[:, m, :], ps[:, bank("q"), m * SEQ:(m + 1) * SEQ], ACT.Identity,
                                         bias=bq[:, m:m + 1])
                ins.then_inc(act_read, 1)
                for m in range(DC):
                    act.wait_ge(job_full, 2 + m)
                    act.activation(kT[:, m, :], ps[:, bank(f"k{m}"), 0:SEQ], ACT.Identity,
                                   bias=bk[:, m:m + 1]).then_inc(act_read, 1)
                act.wait_ge(act_read, act_count("k1", -1))
                act.sem_inc(act_read, 1)
                exp(0, 0)
                exp(1, 0)
                with act.Fori(0, BATCH) as b:
                    for k in range(2):
                        read_probsT(k, b)
                        exp(k + 2, b)
                    row.evacuate(act, b + 1)
                    for k in range(2, 6):
                        read_probsT(k, b)
                        exp(k + 2, b)
                    read_outT(0, b)
                    read_q(b)
                    for m in range(DC):
                        read_k(m, b)
                    read_probsT(6, b)
                    read_probsT(7, b)
                    exp(0, b + 1)
                    exp(1, b + 1)
                    read_outT(1, b)

            @block.vector
            def _(dve):
                def shift(k, b):
                    n = b * UNITS + k
                    x = k % 2
                    scores = ps[:, 2 * x:2 * x + 2, :].rearrange("p x (i n) -> p (x i) n", i=2)
                    dve.wait_ge(scores_full, n + 1)
                    dve.tensor_reduce(peak[:, x, :], scores, AX_X, ALU.max).then_inc(peak_ready, 1)
                    dve.wait_ge(peak_ready, n + 1)
                    dve.tensor_tensor(probs[:, k % 4, :, :], scores, peak[:, x, :].unsqueeze(2).broadcast_to([P, UH, SEQ]),
                                      ALU.subtract).then_inc(shifted, 1)

                def read_mix(k, b):
                    u, first = k // (H // UH), k % (H // UH) * UH
                    dve.wait_ge(job_full, full(f"mix{k}", b))
                    mixed = ps[:, bank(f"mix{k}"), 0:UH * (HD + 1)].rearrange("p (h d) -> p h d", d=HD + 1)
                    dve.reciprocal(inverse[:, k % 2, :], mixed[:, :, HD]).then_inc(inverse_ready, 1)
                    dve.wait_ge(inverse_ready, b * UNITS + k + 1)
                    dve.tensor_tensor(out[:, u, first * HD:(first + UH) * HD].rearrange("p (h d) -> p h d", d=HD),
                                      mixed[:, :, 0:HD], inverse[:, k % 2, :].unsqueeze(2).broadcast_to([P, UH, HD]),
                                      ALU.mult).then_inc(dve_read, 1)

                def read_v(ready):
                    dve.wait_ge(job_full, ready)
                    for t in range(TPB):
                        ins = dve.tensor_tensor(v[:, t, :, 0:HD],
                                                ps[:, bank("v"), t * D:(t + 1) * D].rearrange("p (h d) -> p h d", d=HD),
                                                bv[:, :].rearrange("p (h d) -> p h d", d=HD), ALU.add)
                    ins.then_inc(dve_read, 1)

                def add(u, b):
                    dve.wait_ge(job_full, full(f"proj{u}", b))
                    dve.tensor_tensor(h[:, ds(b * TPB + u, 1), :], ps[:, bank(f"proj{u}"), 0:D],
                                      h[:, ds(b * TPB + u, 1), :], ALU.add).then_inc(dve_read, 1)
                    dve.wait_ge(dve_read, dve_count(f"proj{u}", b))
                    dve.tensor_tensor(h[:, ds(b * TPB + u, 1), :], h[:, ds(b * TPB + u, 1), :], bproj[:, :],
                                      ALU.add).then_inc(product_added, 1)

                dve.sem_inc(shifted, 2)
                dve.sem_inc(dve_read, BY_DVE.index("v"))
                row.norm(dve, 0, first=True)
                dve.wait_ge(weights_in, 96)
                read_v(4)
                dve.wait_ge(dve_read, dve_count("v", -1))
                dve.sem_inc(dve_read, 1)
                shift(0, 0)
                shift(1, 0)
                with dve.Fori(0, BATCH) as b:
                    shift(2, b)
                    row.norm(dve, b + 1)
                    shift(3, b)
                    for k in range(4):
                        read_mix(k, b)
                        shift(k + 4, b)
                    read_mix(4, b)
                    add(0, b)
                    read_mix(5, b)
                    read_mix(6, b)
                    shift(0, b + 1)
                    read_mix(7, b)
                    shift(1, b + 1)
                    read_v(full("v", b))
                    add(1, b)
        s.clear()


def swiglu(nc, core, Wg_d, Wu_d, Wd_d, out_d):
    ps, xT, h = core.ps, core.xT, core.h
    F = Wg_d.shape[1]
    FC = F // P
    SCALE = float(np.float32(1.0 / 127.0))
    with ExitStack() as ctx:
        s = Scope(nc, ctx, "swi")
        Wg_int = s.sb("Wg_int", [P, DC, F], I32)
        Wu_int = s.sb("Wu_int", [P, DC, F], I32)
        Wd_int = s.sb("Wd_int", [P, FC, D], I32)
        Wg = s.sb("Wg", [P, DC, F])
        Wu = s.sb("Wu", [P, DC, F])
        Wd = s.sb("Wd", [P, FC, D])
        sg = s.sb("sg", [P, 2, SEQ])
        act_ = s.sb("act", [P, FC, SEQ])
        int_in = s.sem("int_in")
        weights_ready = s.sem("weights_ready")
        gated_full = s.sem("gated_full")
        sg_ready = s.sem("sg_ready")
        swish_ready = s.sem("swish_ready")
        act_ready = s.sem("act_ready")
        out_full = s.sem("out_full")
        row_added = s.sem("row_added")
        stored = s.sem("stored")
        row = RowNorm(nc, core, s)

        with nc.Block() as block:
            @block.sync
            def _(sp):
                for W, W_d in ((Wg_int, Wg_d), (Wu_int, Wu_d), (Wd_int, Wd_d)):
                    sp.dma_start(W[:, :, :], W_d.rearrange("(c p) n -> p c n", p=P)).then_inc(int_in, 16)
                with sp.Fori(0, BATCH) as b:
                    sp.wait_ge(row_added, b + 2)
                    sp.dma_start(out_d[ds(b, 1), :, :].rearrange("b (t p) d -> p (b t) d", p=P),
                                 h[:, ds(b * TPB, TPB), :]).then_inc(stored, 16)
                sp.wait_ge(stored, 16 * BATCH)

            @block.tensor
            def _(pe):
                row.turn(pe, 0)
                pe.wait_ge(weights_ready, 3)
                with pe.Fori(0, BATCH) as b:
                    pe.wait_ge(row.xT_ready, b + 1)
                    for m in range(FC):
                        pe.wait_ge(act_ready, b * FC + (4 if m < 4 else m + 1))
                        for half, W in ((0, Wg), (1, Wu)):
                            for c in range(DC):
                                last = pe.matmul(ps[:, m % 4, half * SEQ:(half + 1) * SEQ], W[:, c, m * P:(m + 1) * P],
                                                 xT[:, c, :], start=(c == 0), stop=(c == DC - 1))
                        last.then_inc(gated_full, 1)
                    row.turn(pe, b + 1)
                    pe.wait_ge(row_added, b + 1)
                    pe.wait_ge(act_ready, b * FC + FC + 4)
                    for t in range(TPB):
                        for m in range(FC):
                            last = pe.matmul(ps[:, 5, t * D:(t + 1) * D], act_[:, m, t * P:(t + 1) * P], Wd[:, m, :],
                                             start=(m == 0), stop=(m == FC - 1))
                    last.then_inc(out_full, 1)

            @block.scalar
            def _(act):
                row.evacuate(act, 0)
                with act.Fori(0, BATCH) as b:
                    for m in range(FC):
                        act.wait_ge(gated_full, b * FC + m + 1)
                        act.wait_ge(act_ready, b * FC + m + 3)
                        act.activation(sg[:, m % 2, :], ps[:, m % 4, 0:SEQ], ACT.Sigmoid).then_inc(sg_ready, 1)
                    row.evacuate(act, b + 1)

            @block.gpsimd
            def _(pool):
                row.root(pool, 0)
                with pool.Fori(0, BATCH) as b:
                    row.root(pool, b + 1)

            @block.vector
            def _(dve):
                dve.sem_inc(act_ready, 4)
                dve.sem_inc(row_added, 1)
                row.norm(dve, 0, first=True)
                dve.wait_ge(int_in, 48)
                for W, W_int in ((Wg, Wg_int), (Wu, Wu_int), (Wd, Wd_int)):
                    dve.tensor_scalar(W[:, :, :], W_int[:, :, :], SCALE, None, ALU.mult).then_inc(weights_ready, 1)
                with dve.Fori(0, BATCH) as b:
                    row.norm(dve, b + 1)
                    for m in range(FC):
                        dve.wait_ge(sg_ready, b * FC + m + 1)
                        dve.tensor_tensor(sg[:, m % 2, :], sg[:, m % 2, :], ps[:, m % 4, 0:SEQ],
                                          ALU.mult).then_inc(swish_ready, 1)
                        dve.wait_ge(swish_ready, b * FC + m + 1)
                        dve.tensor_tensor(act_[:, m, :], sg[:, m % 2, :], ps[:, m % 4, SEQ:2 * SEQ],
                                          ALU.mult).then_inc(act_ready, 1)
                    dve.wait_ge(out_full, b + 1)
                    dve.tensor_tensor(h[:, ds(b * TPB, TPB), :], ps[:, 5, :].rearrange("p (t d) -> p t d", t=TPB),
                                      h[:, ds(b * TPB, TPB), :], ALU.add).then_inc(row_added, 1)


def tower(nc, a, out_d):
    with ExitStack() as ctx:
        core = Core(nc, ctx)
        constants(nc, core)
        embed(nc, core, a["ids"], a["L0_tok_E1"], a["L0_tok_W2T"], a["L0_tok_b2"], a["L0_tok_pos_emb"])
        linear_attention(nc, core, a["L0_attn_Wqkv"], a["L0_attn_bq"], a["L0_attn_bkv"], a["L0_attn_Wout"],
                         a["L0_attn_bout"])
        sign_ffn(nc, core, a["L0_ffn_k0"], a["L0_ffn_k1"], a["L0_ffn_k2"], a["L0_ffn_s"])
        min_gru(nc, core, *(a[f"L1_attn_{k}"] for k in ("W1", "b1", "W2", "b2", "Wz", "bz", "Wh", "bh", "Wo", "bo")))
        E = a["L1_ffn_w_gate"].shape[0]
        C = capacity(E)
        rows = nc.dram_tensor("moe_rows", (spare_rows(E, C) + 2 * N, D), F32, kind="Internal").ap()
        outs = nc.dram_tensor("moe_outs", (E * C, D), F32, kind="Internal").ap()
        capacity_moe(nc, core, *(a[f"L1_ffn_{k}"] for k in ("router_w", "router_b", "w_gate", "w_up", "w_down",
                                                            "sw_gate", "sw_up", "sw_down")), rows, outs)
        column_attention(nc, core, a["L2_attn_ln"], a["L2_attn_qkv_kernel"], a["L2_attn_out_kernel"])
        E2 = a["L2_ffn_w1"].shape[0]
        rows = nc.dram_tensor("top1_rows", ((top1_blocks(E2) + 1) * BLOCK, D), F32, kind="Internal").ap()
        outs = nc.dram_tensor("top1_outs", (top1_blocks(E2) * BLOCK, D), F32, kind="Internal").ap()
        top1_moe(nc, core, a["L2_ffn_router_w"], a["L2_ffn_router_b"], a["L2_ffn_w1"], a["L2_ffn_w2"], rows, outs)
        row_attention(nc, core, *(a[f"L3_attn_{k}"] for k in ("w_qkv", "bq", "bk", "bv", "w_proj", "b_proj")))
        swiglu(nc, core, a["L3_ffn_w_gateT"], a["L3_ffn_w_upT"], a["L3_ffn_w_downT"], out_d)


def columns(v):
    return np.ascontiguousarray(v.reshape(-1, P).T)


def pad_rows(v):
    pad = [(0, 0)] * v.ndim
    pad[-2] = (0, -v.shape[-2] % P)
    return np.pad(v, pad)


def lay_out(x, w):
    a = {"ids": np.ascontiguousarray(x.reshape(TILES, P).T)}
    for k in ("L0_tok_E1", "L0_tok_b2", "L0_tok_pos_emb", "L0_attn_Wqkv", "L0_attn_Wout", "L0_attn_bout"):
        a[k] = w[k]
    a["L0_tok_W2T"] = w["L0_tok_W2"].T
    a["L0_attn_bq"] = columns(w["L0_attn_bqkv"][:D])
    a["L0_attn_bkv"] = w["L0_attn_bqkv"][D:]
    for k in ("L0_ffn_k0", "L0_ffn_k1", "L0_ffn_k2"):
        a[k] = w[k].view(np.int32)
    a["L0_ffn_s"] = np.stack([w["L0_ffn_s0"], w["L0_ffn_s1"], w["L0_ffn_s2"]])
    for k in ("W1", "W2", "Wz", "Wh", "Wo", "bo"):
        a[f"L1_attn_{k}"] = w[f"L1_attn_{k}"]
    for k in ("b1", "b2", "bz", "bh"):
        a[f"L1_attn_{k}"] = columns(w[f"L1_attn_{k}"])
    for k in ("router_w", "router_b", "w_gate", "w_up", "sw_gate", "sw_up"):
        a[f"L1_ffn_{k}"] = w[f"L1_ffn_{k}"]
    a["L1_ffn_w_down"] = pad_rows(w["L1_ffn_w_down"])
    a["L1_ffn_sw_down"] = pad_rows(w["L1_ffn_sw_down"])
    a["L2_attn_ln"] = np.stack([columns(w["L2_attn_ln_scale"]), columns(w["L2_attn_ln_bias"])], axis=1)
    a["L2_attn_qkv_kernel"] = w["L2_attn_qkv_kernel"].reshape(D, -1)
    a["L2_attn_out_kernel"] = w["L2_attn_out_kernel"]
    for k in ("L2_ffn_router_w", "L2_ffn_router_b", "L2_ffn_w1", "L2_ffn_w2", "L3_attn_w_qkv", "L3_attn_w_proj",
              "L3_attn_b_proj"):
        a[k] = w[k]
    a["L3_attn_bq"], a["L3_attn_bk"] = columns(w["L3_attn_b_qkv"][:D]), columns(w["L3_attn_b_qkv"][D:2 * D])
    a["L3_attn_bv"] = w["L3_attn_b_qkv"][2 * D:]
    for k in ("w_gate", "w_up", "w_down"):
        a[f"L3_ffn_{k}T"] = w[f"L3_ffn_{k}"].T
    return {k: np.ascontiguousarray(v) for k, v in a.items()}


def kernel(**inputs):
    import concourse.bacc as bacc
    from concourse.bass_utils import run_bass_kernel_spmd

    w = {k: np.asarray(v) for k, v in inputs.items()}
    arrays = lay_out(w.pop("x"), w)
    nc = bacc.Bacc("TRN2", target_bir_lowering=False, num_devices=1)
    aps = {k: nc.dram_tensor(f"in_{k}", v.shape, mybir.dt.from_np(v.dtype), kind="ExternalInput").ap()
           for k, v in arrays.items()}
    out = nc.dram_tensor("out_h", (BATCH, SEQ, D), F32, kind="ExternalOutput").ap()
    tower(nc, aps, out)
    r = run_bass_kernel_spmd(nc, [{f"in_{k}": v for k, v in arrays.items()}], core_ids=[0])
    return r.results[0]["out_h"]
```

```python
from contextlib import ExitStack

import numpy as np

import concourse.bass as bass
from concourse import mybir

ALU = mybir.AluOpType
ACT = mybir.ActivationFunctionType
AX_X = mybir.AxisListType.X
F32 = mybir.dt.float32
BF16 = mybir.dt.bfloat16
F32R = mybir.dt.float32r
I32 = mybir.dt.int32
U8 = mybir.dt.uint8
ds = bass.ds

P = 128
BATCH, SEQ, D = 8, 256, 256
N = BATCH * SEQ
TILES = N // P
TPB = SEQ // P
DC = D // P
RANK = 32
LN_EPS = 1e-5


PASSES = [(0, 0), (0, 1), (1, 0)]


class Scope:

    def __init__(self, nc, ctx, prefix, stage=None):
        self.nc, self.ctx, self.prefix = nc, ctx, prefix
        self.sems = [] if stage is None else stage.sems

    def sb(self, name, shape, dt=F32):
        return self.ctx.enter_context(self.nc.sbuf_tensor(f"{self.prefix}_{name}", shape, dt))

    def sem(self, name):
        self.sems.append(self.ctx.enter_context(self.nc.semaphore(f"{self.prefix}_{name}")))
        return self.sems[-1]

    def clear(self):
        with self.nc.Block() as block:
            @block.gpsimd
            def _(pool):
                for sem in self.sems:
                    pool.sem_clear(sem)


class Chain:

    def __init__(self, eng, sem, base=0):
        self.eng, self.sem, self.base, self.steps = eng, sem, base, 0

    def __call__(self, ins):
        self.steps += 1
        ins.then_inc(self.sem, 1)
        self.eng.wait_ge(self.sem, self.base + self.steps)


class Core:

    def __init__(self, nc, ctx):
        s = Scope(nc, ctx, "core")
        self.pool_dma = Scope(nc, ctx, "pool_dma")
        self.h = s.sb("h", [P, TILES + TPB, D])
        self.xr = s.sb("xr", [P, TPB, D])
        self.xT = s.sb("xT", [P, DC, SEQ])
        self.ident = s.sb("ident", [P, P])
        self.ones = s.sb("ones", [P, P])
        self.neg_half = s.sb("neg_half", [P, TILES])
        self.ps = ctx.enter_context(nc.psum_tensor("ps", [P, 8, 512], F32))


class RowNorm:

    BANK = 7
    STEPS = 8

    def __init__(self, nc, core, s):
        self.core = core
        self.stats = s.sb("norm_stats", [P, TPB, 6])
        self.mean = s.sb("norm_mean", [P, TPB])
        self.diff = s.sb("norm_diff", [P, TPB])
        self.var_eps = s.sb("norm_var_eps", [P, TPB])
        self.rstd = s.sb("norm_rstd", [P, TPB])
        self.step = s.sem("norm_step")
        self.var_ready = s.sem("norm_var_ready")
        self.rstd_ready = s.sem("norm_rstd_ready")
        self.row_normed = s.sem("norm_row_normed")
        self.turned = s.sem("norm_turned")
        self.xT_ready = s.sem("norm_xT_ready")
        self.low_ready = s.sem("norm_low_ready")

    def norm(self, dve, r, first=False):
        xr = self.core.xr
        stats, mean, diff, var = self.stats, self.mean, self.diff, self.var_eps
        step = Chain(dve, self.step, r * self.STEPS)
        src = self.core.h[:, ds(r * TPB, TPB), :]
        for t in range(TPB):
            ins = dve.bn_stats(stats[:, t, :], src[:, t, :])
            if t == 0:
                ins.then_inc(self.step, 1)
        step.steps += 1
        step(ins)
        dve.tensor_tensor(mean[:, :], stats[:, :, 1], stats[:, :, 4], ALU.add).then_inc(self.step, 1)
        dve.tensor_tensor(var[:, :], stats[:, :, 2], stats[:, :, 5], ALU.add).then_inc(self.step, 1)
        step.steps += 2
        step(dve.tensor_tensor(diff[:, :], stats[:, :, 1], stats[:, :, 4], ALU.subtract))
        dve.tensor_scalar(mean[:, :], mean[:, :], 0.5, None, ALU.mult).then_inc(self.step, 1)
        step.steps += 1
        step(dve.scalar_tensor_tensor(out=diff[:, :], in0=diff[:, :], scalar=D / 4.0, in1=diff[:, :],
                                      op0=ALU.mult, op1=ALU.mult))
        step(dve.tensor_tensor(var[:, :], var[:, :], diff[:, :], ALU.add))
        dve.tensor_scalar(var[:, :], var[:, :], 1.0 / D, LN_EPS, ALU.mult, ALU.add).then_inc(self.var_ready, 1)
        dve.wait_ge(self.rstd_ready, r + 1)
        if not first:
            dve.wait_ge(self.turned, r)
        for t in range(TPB):
            dve.tensor_scalar(xr[:, t, :], src[:, t, :], mean[:, t:t + 1], self.rstd[:, t:t + 1],
                              ALU.subtract, ALU.mult).then_inc(self.row_normed, 1)
        assert step.steps == self.STEPS

    def root(self, pool, r):
        pool.wait_ge(self.var_ready, r + 1)
        pool.tensor_tensor(self.rstd[:, :], self.var_eps[:, :], self.core.neg_half[:, 0:TPB],
                           ALU.pow).then_inc(self.rstd_ready, 1)

    def turn(self, pe, r):
        pe.wait_ge(self.row_normed, r * TPB + TPB)
        for c in range(DC):
            for t in range(TPB):
                last = pe.transpose(self.core.ps[:, self.BANK, c * SEQ + t * P:c * SEQ + (t + 1) * P],
                                    self.core.xr[:, t, c * P:(c + 1) * P], self.core.ident[:, :])
        last.then_inc(self.turned, 1)

    def evacuate(self, act, r, out=None):
        out = self.core.xT[:, :, :] if out is None else out
        act.wait_ge(self.turned, r + 1)
        act.activation(out, self.core.ps[:, self.BANK, :].rearrange("p (c n) -> p c n", c=DC),
                       ACT.Copy).then_inc(self.xT_ready, 1)

    def low(self, dve, r, high, low):
        dve.wait_ge(self.xT_ready, r + 1)
        dve.tensor_tensor(low[:, :, :], self.core.ps[:, self.BANK, :].rearrange("p (c n) -> p c n", c=DC),
                          high[:, :, :].bitcast(F32), ALU.subtract).then_inc(self.low_ready, 1)


class StreamNorm:

    def __init__(self, nc, core, s, out, outT, eps=(LN_EPS,), affine=None):
        self.core, self.out, self.outT, self.eps, self.affine = core, out, outT, eps, affine
        self.stats = s.sb("snorm_stats", [P, TILES, 6])
        self.mean = s.sb("snorm_mean", [P, TILES])
        self.diff = s.sb("snorm_diff", [P, TILES])
        self.var_eps = s.sb("snorm_var_eps", [P, TILES])
        self.rstd = s.sb("snorm_rstd", [P, TILES])
        self.measured = s.sem("snorm_measured")
        self.step = s.sem("snorm_step")
        self.var_ready = s.sem("snorm_var_ready")
        self.rstd_ready = s.sem("snorm_rstd_ready")
        self.normed = s.sem("snorm_normed")
        self.turned = s.sem("snorm_turned")
        self.outT_ready = s.sem("snorm_outT_ready")

    def norm(self, dve):
        stats, mean, diff, var = self.stats, self.mean, self.diff, self.var_eps
        step = Chain(dve, self.step)
        for k, eps in enumerate(self.eps):
            src = self.core.h if k == 0 else self.out
            for t in range(TILES):
                if k > 0:
                    dve.wait_ge(self.normed, k * TILES - TILES + t + 1)
                dve.bn_stats(stats[:, t, :], src[:, t, :]).then_inc(self.measured, 1)
            dve.wait_ge(self.measured, (k + 1) * TILES)
            step(dve.tensor_tensor(mean[:, :], stats[:, :, 1], stats[:, :, 4], ALU.add))
            step(dve.tensor_tensor(var[:, :], stats[:, :, 2], stats[:, :, 5], ALU.add))
            step(dve.tensor_tensor(diff[:, :], stats[:, :, 1], stats[:, :, 4], ALU.subtract))
            step(dve.tensor_scalar(mean[:, :], mean[:, :], 0.5, None, ALU.mult))
            step(dve.scalar_tensor_tensor(out=diff[:, :], in0=diff[:, :], scalar=D / 4.0, in1=diff[:, :],
                                          op0=ALU.mult, op1=ALU.mult))
            step(dve.tensor_tensor(var[:, :], var[:, :], diff[:, :], ALU.add))
            dve.tensor_scalar(var[:, :], var[:, :], 1.0 / D, eps, ALU.mult, ALU.add).then_inc(self.var_ready, 1)
            dve.wait_ge(self.rstd_ready, k + 1)
            for t in range(TILES):
                dve.tensor_scalar(self.out[:, t, :], src[:, t, :], mean[:, t:t + 1], self.rstd[:, t:t + 1],
                                  ALU.subtract, ALU.mult).then_inc(self.normed, 1)

    def root(self, pool):
        for k in range(len(self.eps)):
            pool.wait_ge(self.var_ready, k + 1)
            pool.tensor_tensor(self.rstd[:, :], self.var_eps[:, :], self.core.neg_half[:, :],
                               ALU.pow).then_inc(self.rstd_ready, 1)

    def turn(self, pe):
        for b in range(BATCH):
            pe.wait_ge(self.normed, len(self.eps) * TILES - TILES + (b + 1) * TPB)
            if b >= 2:
                pe.wait_ge(self.outT_ready, b - 1)
            for c in range(DC):
                for t in range(TPB):
                    last = pe.transpose(self.core.ps[:, 6 + b % 2, c * SEQ + t * P:c * SEQ + (t + 1) * P],
                                        self.out[:, b * TPB + t, c * P:(c + 1) * P], self.core.ident[:, :])
            last.then_inc(self.turned, 1)

    def evacuate(self, act):
        for b in range(BATCH):
            turned = self.core.ps[:, 6 + b % 2, :].rearrange("p (c n) -> p c n", c=DC)
            out = self.outT[:, :, b * SEQ:(b + 1) * SEQ]
            act.wait_ge(self.turned, b + 1)
            if self.affine is None:
                act.activation(out, turned, ACT.Copy).then_inc(self.outT_ready, 1)
            else:
                gain, shift = self.affine
                for c in range(DC):
                    ins = act.activation(out[:, c, :], turned[:, c, :], ACT.Identity, bias=shift[:, c:c + 1],
                                         scale=gain[:, c:c + 1])
                ins.then_inc(self.outT_ready, 1)


def constants(nc, core):
    with ExitStack() as ctx:
        s = Scope(nc, ctx, "const")
        ident_zero = s.sem("ident_zero")
        made = s.sem("made")
        with nc.Block() as block:
            @block.gpsimd
            def _(pool):
                pool.memset(core.ident[:, :], 0.0).then_inc(ident_zero, 1)
                pool.memset(core.ones[:, :], 1.0).then_inc(made, 1)
                pool.memset(core.neg_half[:, :], -0.5).then_inc(made, 1)
                pool.memset(core.h[:, TILES:TILES + TPB, :], 0.0).then_inc(made, 1)
                pool.wait_ge(ident_zero, 1)
                pool.affine_select(out=core.ident[:, :], in_=core.ident[:, :], compare_op=ALU.not_equal,
                                   fill=1.0, base=0, pattern=[[-1, P]], channel_multiplier=1).then_inc(made, 1)
                pool.wait_ge(made, 4)
        s.clear()


def embed(nc, core, ids_d, E1_d, W2T_d, b2_d, pos_d):
    ps = core.ps
    with ExitStack() as ctx:
        s = Scope(nc, ctx, "tok")
        ids = s.sb("ids", [P, TILES], I32)
        rows = s.sb("rows", [P, TILES, RANK])
        rowsT = s.sb("rowsT", [RANK, N])
        W2T = s.sb("W2T", [RANK, D])
        b2 = s.sb("b2", [P, D])
        pos = s.sb("pos", [P, TPB, D])
        ids_in = s.sem("ids_in")
        params_in = s.sem("params_in")
        rows_in = core.pool_dma.sem("table_rows_in")
        rows_turned = s.sem("rows_turned")
        rowsT_ready = s.sem("rowsT_ready")
        pos_ready = s.sem("pos_ready")
        bank_full = s.sem("bank_full")
        bank_free = s.sem("bank_free")

        with nc.Block() as block:
            @block.sync
            def _(sp):
                sp.dma_start(ids[:, :], ids_d).then_inc(ids_in, 16)
                sp.dma_start(W2T[:, :], W2T_d).then_inc(params_in, 16)
                sp.dma_start(pos[:, :, :], pos_d[0, 0:SEQ, :].rearrange("(t p) d -> p t d",
                             p=P)).then_inc(params_in, 16)
                sp.dma_start(b2[:, :], b2_d.partition_broadcast(P)).then_inc(params_in, 16)

            @block.gpsimd
            def _(pool):
                pool.wait_ge(ids_in, 16)
                for t in range(TILES):
                    pool.indirect_dma_start(rows[:, t, :], None, E1_d,
                                            bass.IndirectOffsetOnAxis(ap=ids[:, t:t + 1], axis=0)).then_inc(rows_in, 16)

            @block.tensor
            def _(pe):
                pe.wait_ge(rows_in, 16 * TILES)
                for t in range(TILES):
                    last = pe.transpose(ps[0:RANK, t // 4, t % 4 * P:(t % 4 + 1) * P], rows[:, t, :], core.ident[:, :])
                last.then_inc(rows_turned, 1)
                pe.wait_ge(params_in, 48)
                pe.wait_ge(rowsT_ready, 1)
                for b in range(BATCH):
                    if b >= 4:
                        pe.wait_ge(bank_free, b - 3)
                    for t in range(TPB):
                        last = pe.matmul(ps[:, 4 + b % 4, t * D:(t + 1) * D],
                                         rowsT[:, (b * TPB + t) * P:(b * TPB + t + 1) * P], W2T[:, :],
                                         start=True, stop=True)
                    last.then_inc(bank_full, 1)

            @block.scalar
            def _(act):
                act.wait_ge(rows_turned, 1)
                act.activation(rowsT[:, :].rearrange("r (k n) -> r k n", k=4), ps[0:RANK, 0:4, :],
                               ACT.Copy).then_inc(rowsT_ready, 1)

            @block.vector
            def _(dve):
                dve.wait_ge(params_in, 48)
                dve.tensor_tensor(pos[:, :, :], pos[:, :, :], b2[:, :].unsqueeze(1).broadcast_to([P, TPB, D]),
                                  ALU.add).then_inc(pos_ready, 1)
                dve.wait_ge(pos_ready, 1)
                for b in range(BATCH):
                    dve.wait_ge(bank_full, b + 1)
                    dve.tensor_tensor(core.h[:, b * TPB:(b + 1) * TPB, :],
                                      ps[:, 4 + b % 4, :].rearrange("p (t d) -> p t d", t=TPB),
                                      pos[:, :, :], ALU.add).then_inc(bank_free, 1)
        s.clear()


def linear_attention(nc, core, Wqkv_d, bq_d, bkv_d, Wout_d, bout_d):
    ps, xT, h = core.ps, core.xT, core.h
    with ExitStack() as ctx:
        s = Scope(nc, ctx, "lattn")
        Wqkv = s.sb("Wqkv", [P, DC, 3 * D])
        Wout = s.sb("Wout", [P, DC, D])
        bq = s.sb("bq", [P, DC])
        bkv = s.sb("bkv", [P, 2 * D])
        bout = s.sb("bout", [P, D])
        qT = s.sb("qT", [P, 2, DC, SEQ])
        q_sq = s.sb("q_sq", [P, 2, DC, SEQ])
        kv = s.sb("kv", [P, TPB, 2 * D])
        k_sq = s.sb("k_sq", [P, D])
        k_ss = s.sb("k_ss", [P, TPB])
        rk = s.sb("rk", [P, TPB])
        k_by_v = s.sb("k_by_v", [P, TPB, D])
        sums = s.sb("sums", [P, DC + TPB])
        rq = s.sb("rq", [P, TPB])
        W_row = s.sb("W_row", [P, DC, D])
        weights_in = s.sem("weights_in")
        q_full = s.sem("q_full")
        kv_full = s.sem("kv_full")
        qT_ready = s.sem("qT_ready")
        kv_ready = s.sem("kv_ready")
        k_ss_ready = s.sem("k_ss_ready")
        k_by_v_ready = s.sem("k_by_v_ready")
        rk_ready = s.sem("rk_ready")
        sums_full = s.sem("sums_full")
        sums_ready = s.sem("sums_ready")
        rq_ready = s.sem("rq_ready")
        W_row_ready = s.sem("W_row_ready")
        out_full = s.sem("out_full")
        scaled = s.sem("scaled")
        row_added = s.sem("row_added")
        row = RowNorm(nc, core, s)

        with nc.Block() as block:
            @block.sync
            def _(sp):
                sp.dma_start(Wqkv[:, :, :], Wqkv_d.rearrange("(c p) n -> p c n", p=P)).then_inc(weights_in, 16)
                sp.dma_start(bq[:, :], bq_d).then_inc(weights_in, 16)
                sp.dma_start(bkv[:, :], bkv_d.partition_broadcast(P)).then_inc(weights_in, 16)
                sp.dma_start(Wout[:, :, :], Wout_d.rearrange("(c p) n -> p c n", p=P)).then_inc(weights_in, 16)
                sp.dma_start(bout[:, :], bout_d.partition_broadcast(P)).then_inc(weights_in, 16)

            PAIRS = BATCH // 2 - 1

            @block.tensor
            def _(pe):
                def project(b):
                    pe.wait_ge(row.xT_ready, b + 1)
                    pe.wait_ge(qT_ready, b * 2 + 2)
                    for m in range(DC):
                        for c in range(DC):
                            last = pe.matmul(ps[:, 0, m * SEQ:(m + 1) * SEQ], Wqkv[:, c, m * P:(m + 1) * P],
                                             xT[:, c, :], start=(c == 0), stop=(c == DC - 1))
                    last.then_inc(q_full, 1)
                    pe.wait_ge(kv_ready, b * 2 + 2)
                    for t in range(TPB):
                        for c in range(DC):
                            last = pe.matmul(ps[:, 1 + t, :], xT[:, c, t * P:(t + 1) * P],
                                             Wqkv[:, c, D:3 * D], start=(c == 0), stop=(c == DC - 1))
                        last.then_inc(kv_full, 1)

                def sum_up(b, u):
                    pe.wait_ge(k_by_v_ready, b * 2 + 2)
                    pe.wait_ge(rk_ready, b + 1)
                    pe.wait_ge(sums_ready, b + 1)
                    for c in range(DC):
                        for t in range(TPB):
                            pe.matmul(ps[:, 3, c:c + 1], k_by_v[:, t, c * P:(c + 1) * P], rk[:, t:t + 1],
                                      start=(t == 0), stop=(t == TPB - 1))
                    pe.wait_ge(qT_ready, b * 2 + 4)
                    for t in range(TPB):
                        for c in range(DC):
                            last = pe.matmul(ps[:, 3, DC + t:DC + t + 1], q_sq[:, u, c, t * P:(t + 1) * P],
                                             core.ones[:, 0:1], start=(c == 0), stop=(c == DC - 1))
                    last.then_inc(sums_full, 1)

                def output(b, u):
                    pe.wait_ge(W_row_ready, b + 1)
                    pe.wait_ge(row_added, b + 1)
                    for t in range(TPB):
                        for c in range(DC):
                            last = pe.matmul(ps[:, 4, t * D:(t + 1) * D], qT[:, u, c, t * P:(t + 1) * P],
                                             W_row[:, c, :], start=(c == 0), stop=(c == DC - 1))
                    last.then_inc(out_full, 1)

                row.turn(pe, 0)
                pe.wait_ge(weights_in, 80)
                project(0)
                row.turn(pe, 1)
                with pe.Fori(0, PAIRS) as i:
                    for u in (1, 0):
                        b = i * 2 + (2 - u)
                        project(b)
                        row.turn(pe, b + 1)
                        sum_up(b - 1, 1 - u)
                        output(b - 1, 1 - u)
                project(BATCH - 1)
                for b in (BATCH - 2, BATCH - 1):
                    sum_up(b, b % 2)
                    output(b, b % 2)

            @block.scalar
            def _(act):
                def queries(b, u):
                    act.wait_ge(q_full, b + 1)
                    for m in range(DC):
                        act.activation(q_sq[:, u, m, :], ps[:, 0, m * SEQ:(m + 1) * SEQ], ACT.Square, bias=bq[:, m:m + 1])
                    for m in range(DC):
                        act.activation(qT[:, u, m, :], ps[:, 0, m * SEQ:(m + 1) * SEQ], ACT.Identity,
                                       bias=bq[:, m:m + 1]).then_inc(qT_ready, 1)

                act.sem_inc(qT_ready, 2)
                act.wait_ge(weights_in, 80)
                row.evacuate(act, 0)
                queries(0, 0)
                row.evacuate(act, 1)
                with act.Fori(0, PAIRS) as i:
                    for u in (1, 0):
                        queries(i * 2 + (2 - u), u)
                        row.evacuate(act, i * 2 + (3 - u))
                queries(BATCH - 1, 1)

            @block.gpsimd
            def _(pool):
                def inverse_k(b):
                    pool.wait_ge(k_ss_ready, b * 2 + 2)
                    pool.tensor_tensor(rk[:, :], k_ss[:, :], core.neg_half[:, 0:TPB], ALU.pow).then_inc(rk_ready, 1)

                def inverse_q(b):
                    pool.wait_ge(sums_ready, b + 2)
                    pool.tensor_tensor(rq[:, :], sums[:, DC:DC + TPB], core.neg_half[:, 0:TPB],
                                       ALU.pow).then_inc(rq_ready, 1)

                row.root(pool, 0)
                row.root(pool, 1)
                inverse_k(0)
                with pool.Fori(1, BATCH - 1) as b:
                    row.root(pool, b + 1)
                    inverse_q(b - 1)
                    inverse_k(b)
                inverse_q(BATCH - 2)
                inverse_k(BATCH - 1)
                inverse_q(BATCH - 1)

            @block.vector
            def _(dve):
                def keys_values(b):
                    for t in range(TPB):
                        dve.wait_ge(kv_full, b * 2 + t + 1)
                        dve.tensor_tensor(kv[:, t, :], ps[:, 1 + t, :], bkv[:, :], ALU.add).then_inc(kv_ready, 1)
                        dve.wait_ge(kv_ready, b * 2 + t + 3)
                        dve.tensor_tensor_reduce(out=k_sq[:, :], in0=kv[:, t, 0:D], in1=kv[:, t, 0:D], scale=1.0,
                                                 scalar=0.0, op0=ALU.mult, op1=ALU.add,
                                                 accum_out=k_ss[:, t:t + 1]).then_inc(k_ss_ready, 1)
                        dve.tensor_tensor(k_by_v[:, t, :], kv[:, t, 0:D], kv[:, t, D:2 * D],
                                          ALU.mult).then_inc(k_by_v_ready, 1)

                def scale_weights(b):
                    dve.wait_ge(sums_full, b + 1)
                    dve.tensor_copy(sums[:, :], ps[:, 3, 0:DC + TPB]).then_inc(sums_ready, 1)
                    dve.wait_ge(sums_ready, b + 2)
                    dve.tensor_scalar(W_row[:, 0, :], Wout[:, 0, :], sums[:, 0:1], None, ALU.mult)
                    dve.tensor_scalar(W_row[:, 1, :], Wout[:, 1, :], sums[:, 1:2], None,
                                      ALU.mult).then_inc(W_row_ready, 1)

                def add(b):
                    dve.wait_ge(out_full, b + 1)
                    dve.wait_ge(rq_ready, b + 1)
                    for t in range(TPB):
                        dve.scalar_tensor_tensor(out=h[:, ds(b * 2 + t, 1), :], in0=ps[:, 4, t * D:(t + 1) * D],
                                                 scalar=rq[:, t:t + 1], in1=h[:, ds(b * 2 + t, 1), :],
                                                 op0=ALU.mult, op1=ALU.add).then_inc(scaled, 1)
                    dve.wait_ge(scaled, b * 2 + 2)
                    dve.tensor_tensor(h[:, ds(b * 2, TPB), :], h[:, ds(b * 2, TPB), :],
                                      bout[:, :].unsqueeze(1).broadcast_to([P, TPB, D]), ALU.add).then_inc(row_added, 1)

                dve.sem_inc(kv_ready, 2)
                dve.sem_inc(sums_ready, 1)
                dve.sem_inc(row_added, 1)
                row.norm(dve, 0, first=True)
                dve.wait_ge(weights_in, 80)
                row.norm(dve, 1)
                keys_values(0)
                with dve.Fori(1, BATCH - 1) as b:
                    row.norm(dve, b + 1)
                    scale_weights(b - 1)
                    keys_values(b)
                    add(b - 1)
                scale_weights(BATCH - 2)
                keys_values(BATCH - 1)
                add(BATCH - 2)
                scale_weights(BATCH - 1)
                add(BATCH - 1)
        s.clear()


def sign_ffn(nc, core, k0_d, k1_d, k2_d, s_d, Wz_d, Wz_parts):
    ps, xT, h = core.ps, core.xT, core.h
    F = k1_d.shape[0]
    FC = F // P
    G1_BANKS, G2_BANKS = (0, 1, 2), (3, 4, 5)
    JOBS = FC // 2
    with ExitStack() as ctx:
        s = Scope(nc, ctx, "sffn")
        k0_words = s.sb("k0", [P, 2 * DC, F // 4], I32)
        k1_words = s.sb("k1", [P, FC, F // 4], I32)
        k2_words = s.sb("k2", [P, FC, D // 4], I32)
        k0, k1, k2 = (k[:, :, :].bitcast(U8) for k in (k0_words, k1_words, k2_words))
        W0 = s.sb("W0", [P, DC, F], F32R)
        W1 = s.sb("W1", [P, FC, F], F32R)
        W2 = s.sb("W2", [P, FC, D], F32R)
        x_parts = [s.sb(f"x_{n}", [P, DC, SEQ], F32R) for n in ("high", "low")]
        sc = s.sb("sc", [P, 3])
        gain = s.sb("gain", [P, 2])
        hidden = s.sb("hidden", [P, 2, 2, SEQ])
        h1_parts, h2_parts = ([s.sb(f"{h}_{n}", [P, FC, SEQ], F32R) for n in ("high", "low")] for h in ("h1", "h2"))
        Wz_raw = s.sb("Wz_raw", [P, F])
        Wz_raw_in = s.sem("Wz_raw_in")
        Wz_high_ready = s.sem("Wz_high_ready")
        Wz_ready = s.sem("Wz_ready")
        bits_in = s.sem("bits_in")
        W0_ready = s.sem("W0_ready")
        W1_ready = s.sem("W1_ready")
        W2_ready = s.sem("W2_ready")
        gain_ready = s.sem("gain_ready")
        hidden_full = s.sem("hidden_full")
        hidden_ready = s.sem("hidden_ready")
        high_ready = s.sem("high_ready")
        parts_ready = s.sem("parts_ready")
        out_full = s.sem("out_full")
        row_added = s.sem("row_added")
        row = RowNorm(nc, core, s)

        with nc.Block() as block:
            @block.sync
            def _(sp):
                sp.dma_start(k0_words[:, :, :], k0_d.rearrange("(c p) n -> p c n", p=P)).then_inc(bits_in, 16)
                sp.dma_start(sc[:, :], s_d.partition_broadcast(P)).then_inc(bits_in, 16)
                sp.dma_start(k1_words[:, :, :], k1_d.rearrange("(c p) n -> p c n", p=P)).then_inc(bits_in, 16)
                sp.dma_start(k2_words[:, :, :], k2_d.rearrange("(c p) n -> p c n", p=P)).then_inc(bits_in, 16)
                sp.dma_start(Wz_raw[:, :], Wz_d[0:P, :]).then_inc(Wz_raw_in, 16)
                with sp.Fori(1, BATCH) as b:
                    sp.wait_ge(Wz_ready, b)
                    sp.dma_start(Wz_raw[:, :], Wz_d[ds(b * P, P), :]).then_inc(Wz_raw_in, 16)

            @block.tensor
            def _(pe):
                row.turn(pe, 0)
                pe.wait_ge(W0_ready, 1)
                with pe.Fori(0, BATCH) as b:
                    done = b * (2 * JOBS)
                    pe.wait_ge(row.low_ready, b + 1)
                    for j in range(JOBS):
                        pe.wait_ge(hidden_ready, done + (JOBS if j < 3 else 2 * JOBS + j - 2))
                        for m in range(2):
                            for c in range(DC):
                                for i, x in enumerate(x_parts):
                                    last = pe.matmul(ps[:, G1_BANKS[j % 3], m * SEQ:(m + 1) * SEQ],
                                                     W0[:, c, (2 * j + m) * P:(2 * j + m + 1) * P], x[:, c, :],
                                                     start=(c + i == 0), stop=(c + i == DC))
                        last.then_inc(hidden_full, 1)
                    pe.wait_ge(W1_ready, 1)
                    for j in range(JOBS):
                        if j == 2:
                            row.turn(pe, b + 1)
                        if j >= 3:
                            pe.wait_ge(hidden_ready, done + 3 * JOBS + j - 2)
                        for m in range(2):
                            for c in range(FC):
                                if j == 0 and m == 0 and c % 2 == 0:
                                    pe.wait_ge(parts_ready, done + c // 2 + 3)
                                for i, h1 in enumerate(h1_parts):
                                    last = pe.matmul(ps[:, G2_BANKS[j % 3], m * SEQ:(m + 1) * SEQ],
                                                     W1[:, c, (2 * j + m) * P:(2 * j + m + 1) * P], h1[:, c, :],
                                                     start=(c + i == 0), stop=(c + i == FC))
                        last.then_inc(hidden_full, 1)
                    pe.wait_ge(W2_ready, 1)
                    pe.wait_ge(row_added, b + 1)
                    for t in range(TPB):
                        for c in range(FC):
                            if t == 0 and c % 2 == 0:
                                pe.wait_ge(parts_ready, done + JOBS + c // 2 + 3)
                            for i, h2 in enumerate(h2_parts):
                                last = pe.matmul(ps[:, 6, t * D:(t + 1) * D], h2[:, c, t * P:(t + 1) * P], W2[:, c, :],
                                                 start=(c + i == 0), stop=(c + i == FC))
                    last.then_inc(out_full, 1)

            @block.scalar
            def _(act):
                def relu(n, j, bank, k):
                    act.wait_ge(hidden_full, n + 1)
                    act.wait_ge(parts_ready, n + 1)
                    act.activation(hidden[:, j % 2, :, :], ps[:, bank, :].rearrange("p (m n) -> p m n", m=2),
                                   ACT.Relu, scale=gain[:, k:k + 1]).then_inc(hidden_ready, 1)

                act.sem_inc(hidden_ready, 2 * JOBS)
                row.evacuate(act, 0, x_parts[0][:, :, :])
                act.wait_ge(gain_ready, 2)
                with act.Fori(0, BATCH) as b:
                    for j in range(JOBS):
                        relu(b * (2 * JOBS) + j, j, G1_BANKS[j % 3], 0)
                    for j in range(JOBS):
                        if j == 2:
                            row.evacuate(act, b + 1, x_parts[0][:, :, :])
                        relu(b * (2 * JOBS) + JOBS + j, j, G2_BANKS[j % 3], 1)

            @block.gpsimd
            def _(pool):
                row.root(pool, 0)
                high, low = Wz_parts
                assert Wz_d.shape[0] == BATCH * P
                with pool.Fori(0, BATCH) as b:
                    row.root(pool, b + 1)
                    pool.wait_ge(Wz_raw_in, b * 16 + 16)
                    pool.tensor_copy(high[:, ds(b, 1), :], Wz_raw[:, :].unsqueeze(1)).then_inc(Wz_high_ready, 1)
                    pool.wait_ge(Wz_high_ready, b + 1)
                    pool.tensor_tensor(low[:, ds(b, 1), :], Wz_raw[:, :].unsqueeze(1),
                                       high[:, ds(b, 1), :].bitcast(F32), ALU.subtract).then_inc(Wz_ready, 1)
                pool.wait_ge(Wz_ready, BATCH)

            @block.vector
            def _(dve):
                def split(n, j, parts):
                    high, low = (p[:, 2 * j:2 * j + 2, :] for p in parts)
                    dve.wait_ge(hidden_ready, n + 2 * JOBS + 1)
                    dve.tensor_copy(high, hidden[:, j % 2, :, :]).then_inc(high_ready, 1)
                    dve.wait_ge(high_ready, n + 1)
                    dve.tensor_tensor(low, hidden[:, j % 2, :, :], high.bitcast(F32),
                                      ALU.subtract).then_inc(parts_ready, 1)

                row.norm(dve, 0, first=True)
                dve.sem_inc(row_added, 1)
                dve.sem_inc(parts_ready, 2)
                dve.wait_ge(bits_in, 64)
                dve.tensor_scalar(gain[:, 0:1], sc[:, 0:1], 4.0, None, ALU.mult).then_inc(gain_ready, 1)
                dve.tensor_scalar(gain[:, 1:2], sc[:, 1:2], 2.0, None, ALU.mult).then_inc(gain_ready, 1)
                dve.tensor_tensor(W0[:, :, :], k0[:, 0:DC, :], k0[:, DC:2 * DC, :], ALU.subtract).then_inc(W0_ready, 1)
                dve.tensor_scalar(W1[:, :, :], k1[:, :, :], 2.0, -1.0, ALU.mult, ALU.add).then_inc(W1_ready, 1)
                dve.tensor_scalar(W2[:, :, :], k2[:, :, :], 2.0, -1.0, ALU.mult, ALU.add).then_inc(W2_ready, 1)
                row.low(dve, 0, *x_parts)
                with dve.Fori(0, BATCH) as b:
                    for j in range(JOBS):
                        split(b * (2 * JOBS) + j, j, h1_parts)
                    row.norm(dve, b + 1)
                    for j in range(JOBS):
                        if j == 2:
                            row.low(dve, b + 1, *x_parts)
                        split(b * (2 * JOBS) + JOBS + j, j, h2_parts)
                    dve.wait_ge(out_full, b + 1)
                    dve.scalar_tensor_tensor(out=h[:, ds(b * TPB, TPB), :],
                                             in0=ps[:, 6, :].rearrange("p (t d) -> p t d", t=TPB), scalar=sc[:, 2:3],
                                             in1=h[:, ds(b * TPB, TPB), :], op0=ALU.mult,
                                             op1=ALU.add).then_inc(row_added, 1)
        s.clear()


def min_gru(nc, core, Wz_parts, W1_d, b1_d, W2_d, b2_d, bz_d, Wh_d, bh_d, Wo_d, bo_d):
    ps, xT, h = core.ps, core.xT, core.h
    F = Wh_d.shape[0]
    FC = F // P
    SILU_BANKS = 4
    with ExitStack() as ctx:
        s = Scope(nc, ctx, "gru")
        W1 = s.sb("W1", [P, DC, F])
        W2 = s.sb("W2", [P, DC, F])
        Wh = s.sb("Wh", [P, FC, F])
        Wo = s.sb("Wo", [P, FC, D])
        b1, b2, bz, bh = (s.sb(n, [P, FC]) for n in ("b1", "b2", "bz", "bh"))
        neg_bz = s.sb("neg_bz", [P, FC])
        bo = s.sb("bo", [P, D])
        sg = s.sb("sg", [P, SILU_BANKS, SEQ])
        u = s.sb("u", [P, FC, SEQ])
        u_parts = [s.sb(f"u_{n}", [P, FC, SEQ], F32R) for n in ("high", "low")]
        skip = s.sb("skip", [P, FC, SEQ])
        keep = s.sb("keep", [P, 2, SEQ])
        z = s.sb("z", [P, 2, SEQ])
        drive = s.sb("drive", [P, 2, SEQ])
        state = s.sb("state", [P, 2, SEQ])
        biases_in = s.sem("biases_in")
        u_high_ready = s.sem("u_high_ready")
        u_parts_ready = s.sem("u_parts_ready")
        W1_in, W2_in, gates_in, Wo_in = (s.sem(n) for n in ("W1_in", "W2_in", "gates_in", "Wo_in"))
        neg_bz_ready = s.sem("neg_bz_ready")
        silu_full = s.sem("silu_full")
        sg_ready = s.sem("sg_ready")
        silu_ready = s.sem("silu_ready")
        gate_full = s.sem("gate_full")
        gate_ready = s.sem("gate_ready")
        drive_ready = s.sem("drive_ready")
        state_ready = s.sem("state_ready")
        sum_ready = s.sem("sum_ready")
        out_full = s.sem("out_full")
        product_added = s.sem("product_added")
        row_added = s.sem("row_added")
        row = RowNorm(nc, core, s)

        with nc.Block() as block:
            @block.sync
            def _(sp):
                sp.dma_start(W1[:, :, :], W1_d.rearrange("(c p) n -> p c n", p=P)).then_inc(W1_in, 16)
                for bias, bias_d in ((b1, b1_d), (b2, b2_d), (bz, bz_d), (bh, bh_d)):
                    sp.dma_start(bias[:, :], bias_d).then_inc(biases_in, 16)
                sp.dma_start(bo[:, :], bo_d.partition_broadcast(P)).then_inc(biases_in, 16)
                sp.dma_start(W2[:, :, :], W2_d.rearrange("(c p) n -> p c n", p=P)).then_inc(W2_in, 16)
                sp.dma_start(Wh[:, :, :], Wh_d.rearrange("(c p) n -> p c n", p=P)).then_inc(gates_in, 16)
                sp.dma_start(Wo[:, :, :], Wo_d.rearrange("(c p) n -> p c n", p=P)).then_inc(Wo_in, 16)

            @block.tensor
            def _(pe):
                row.turn(pe, 0)
                pe.wait_ge(W1_in, 16)
                with pe.Fori(0, BATCH) as b:
                    pe.wait_ge(row.xT_ready, b + 1)
                    for j in range(2 * FC):
                        W, m = (W1, j) if j < FC else (W2, j - FC)
                        if j == FC:
                            pe.wait_ge(W2_in, 16)
                        pe.wait_ge(silu_ready, b * (2 * FC) + j + 1)
                        for c in range(DC):
                            last = pe.matmul(ps[:, j % SILU_BANKS, 0:SEQ], W[:, c, m * P:(m + 1) * P], xT[:, c, :],
                                             start=(c == 0), stop=(c == DC - 1))
                        last.then_inc(silu_full, 1)
                    pe.wait_ge(gates_in, 16)
                    for m in range(FC):
                        if m == 2:
                            row.turn(pe, b + 1)
                        pe.wait_ge(gate_ready, b * FC + m + 1)
                        pe.wait_ge(drive_ready, b * FC + m + 1)
                        for c in range(FC):
                            if m == 0:
                                pe.wait_ge(u_parts_ready, b * FC + c + 1)
                            pe.matmul(ps[:, 4 + m % 2, SEQ:2 * SEQ], Wh[:, c, m * P:(m + 1) * P], u[:, c, :],
                                      start=(c == 0), stop=(c == FC - 1))
                        for c in range(FC):
                            for n, (w, x) in enumerate(PASSES):
                                last = pe.matmul(ps[:, 4 + m % 2, 0:SEQ], Wz_parts[w][:, c, m * P:(m + 1) * P],
                                                 u_parts[x][:, c, :], start=(c + n == 0),
                                                 stop=(c == FC - 1 and n == 2))
                        last.then_inc(gate_full, 1)
                    pe.wait_ge(Wo_in, 16)
                    pe.wait_ge(product_added, b + 1)
                    for t in range(TPB):
                        for c in range(FC):
                            if t == 0:
                                pe.wait_ge(sum_ready, b * FC + c + 1)
                            last = pe.matmul(ps[:, 6, t * D:(t + 1) * D], skip[:, c, t * P:(t + 1) * P], Wo[:, c, :],
                                             start=(c == 0), stop=(c == FC - 1))
                    last.then_inc(out_full, 1)

            @block.scalar
            def _(act):
                row.evacuate(act, 0)
                act.sem_inc(gate_ready, 2)
                act.wait_ge(biases_in, 80)
                act.wait_ge(neg_bz_ready, 1)
                with act.Fori(0, BATCH) as b:
                    for j in range(2 * FC):
                        bias, m = (b1, j) if j < FC else (b2, j - FC)
                        act.wait_ge(silu_full, b * (2 * FC) + j + 1)
                        act.activation(sg[:, j % SILU_BANKS, :], ps[:, j % SILU_BANKS, 0:SEQ], ACT.Sigmoid,
                                       bias=bias[:, m:m + 1]).then_inc(sg_ready, 1)
                    for m in range(FC):
                        if m == 2:
                            row.evacuate(act, b + 1)
                        act.wait_ge(gate_full, b * FC + m + 1)
                        act.wait_ge(state_ready, b * FC + m + 1)
                        act.activation(keep[:, m % 2, :], ps[:, 4 + m % 2, 0:SEQ], ACT.Sigmoid,
                                       bias=neg_bz[:, m:m + 1], scale=-1.0)
                        act.activation(z[:, m % 2, :], ps[:, 4 + m % 2, 0:SEQ], ACT.Sigmoid,
                                       bias=bz[:, m:m + 1]).then_inc(gate_ready, 1)

            @block.gpsimd
            def _(pool):
                row.root(pool, 0)
                with pool.Fori(0, BATCH) as b:
                    row.root(pool, b + 1)

            @block.vector
            def _(dve):
                row.norm(dve, 0, first=True)
                dve.sem_inc(silu_ready, SILU_BANKS)
                dve.sem_inc(drive_ready, 2)
                dve.sem_inc(state_ready, 2)
                dve.sem_inc(product_added, 1)
                dve.wait_ge(biases_in, 80)
                dve.tensor_scalar(neg_bz[:, :], bz[:, :], -1.0, None, ALU.mult).then_inc(neg_bz_ready, 1)
                with dve.Fori(0, BATCH) as b:
                    for j in range(2 * FC):
                        bias, out, m = (b1, u, j) if j < FC else (b2, skip, j - FC)
                        dve.wait_ge(sg_ready, b * (2 * FC) + j + 1)
                        dve.scalar_tensor_tensor(out=out[:, m, :], in0=ps[:, j % SILU_BANKS, 0:SEQ], scalar=bias[:, m:m + 1],
                                                 in1=sg[:, j % SILU_BANKS, :], op0=ALU.add,
                                                 op1=ALU.mult).then_inc(silu_ready, 1)
                        if j < FC:
                            dve.wait_ge(silu_ready, b * (2 * FC) + j + SILU_BANKS + 1)
                            high, low = (p[:, j, :] for p in u_parts)
                            dve.tensor_copy(high, u[:, j, :]).then_inc(u_high_ready, 1)
                            dve.wait_ge(u_high_ready, b * FC + j + 1)
                            dve.tensor_tensor(low, u[:, j, :], high.bitcast(F32),
                                              ALU.subtract).then_inc(u_parts_ready, 1)
                    row.norm(dve, b + 1)
                    for m in range(FC):
                        dve.wait_ge(gate_ready, b * FC + m + 3)
                        dve.scalar_tensor_tensor(out=drive[:, m % 2, :], in0=ps[:, 4 + m % 2, SEQ:2 * SEQ],
                                                 scalar=bh[:, m:m + 1], in1=z[:, m % 2, :], op0=ALU.add,
                                                 op1=ALU.mult).then_inc(drive_ready, 1)
                        dve.wait_ge(drive_ready, b * FC + m + 3)
                        dve.tensor_tensor_scan(out=state[:, m % 2, :], data0=keep[:, m % 2, :],
                                               data1=drive[:, m % 2, :], initial=0.0, op0=ALU.mult,
                                               op1=ALU.add).then_inc(state_ready, 1)
                        dve.wait_ge(state_ready, b * FC + m + 3)
                        dve.tensor_tensor(skip[:, m, :], skip[:, m, :], state[:, m % 2, :],
                                          ALU.add).then_inc(sum_ready, 1)
                    dve.wait_ge(out_full, b + 1)
                    dve.tensor_tensor(h[:, ds(b * TPB, TPB), :], ps[:, 6, :].rearrange("p (t d) -> p t d", t=TPB),
                                      h[:, ds(b * TPB, TPB), :], ALU.add).then_inc(product_added, 1)
                    dve.wait_ge(product_added, b + 2)
                    dve.tensor_tensor(h[:, ds(b * TPB, TPB), :], h[:, ds(b * TPB, TPB), :],
                                      bo[:, :].unsqueeze(1).broadcast_to([P, TPB, D]), ALU.add).then_inc(row_added, 1)
        s.clear()


class Router:

    def __init__(self, nc, core, s, E, K):
        self.core, self.E, self.K = core, E, K
        T = TILES
        self.logits = s.sb("logits", [P, T, E])
        self.peak = s.sb("peak", [P, T])
        self.probs = s.sb("probs", [P, T, E])
        self.total = s.sb("total", [P, T])
        self.index = s.sb("index", [P, T, E])
        self.before = s.sb("before", [P, P])
        self.cand = s.sb("cand", [P, T, E])
        self.top = [s.sb(f"top{k}", [P, T]) for k in range(K)]
        self.best = [s.sb(f"best{k}", [P, T]) for k in range(K)]
        self.hot = [s.sb(f"hot{k}", [P, T, E]) for k in range(K)]
        self.chosen = s.sb("chosen", [P, T, E]) if K > 1 else self.hot[0]
        self.count = [s.sb(f"count{k}", [P, T, E]) for k in range(2)]
        self.pos = s.sb("pos", [P, T, E])
        self.made = s.sem("route_made")
        self.before_one = s.sem("route_before_one")
        self.shifted = s.sem("route_shifted")
        self.exped = s.sem("route_exped")
        self.chosen_ready = s.sem("route_chosen_ready")
        self.counted = s.sem("route_counted")
        self.step = s.sem("route_step")

    def wide(self, column):
        return column[:, :].unsqueeze(2).broadcast_to([P, TILES, self.E])

    def tables(self, pool):
        pool.iota(self.index[:, :, :], pattern=[[0, TILES], [1, self.E]], base=0, channel_multiplier=0,
                  allow_small_or_imprecise_dtypes=True).then_inc(self.made, 1)
        pool.memset(self.before[:, :], 1.0).then_inc(self.before_one, 1)
        pool.wait_ge(self.before_one, 1)
        pool.affine_select(out=self.before[:, :], in_=self.before[:, :], compare_op=ALU.is_ge, fill=0.0, base=-1,
                           pattern=[[1, P]], channel_multiplier=-1).then_inc(self.made, 1)

    def exp(self, act):
        act.wait_ge(self.shifted, 1)
        act.activation(self.probs[:, :, :], self.cand[:, :, :], ACT.Exp).then_inc(self.exped, 1)

    def count_before(self, pe):
        pe.wait_ge(self.made, 2)
        pe.wait_ge(self.chosen_ready, 1)
        n = TILES * self.E
        flat = self.chosen[:, :, :].rearrange("p t e -> p (t e)")
        pe.matmul(self.core.ps[:, 0, 0:n], self.before[:, :], flat, start=True, stop=True)
        pe.matmul(self.core.ps[:, 1, 0:n], self.core.ones[:, :], flat, start=True, stop=True).then_inc(self.counted, 1)

    def route(self, dve):
        T, E, n = TILES, self.E, TILES * self.E
        step = Chain(dve, self.step)
        step(dve.tensor_reduce(self.peak[:, :], self.logits[:, :, :], AX_X, ALU.max))
        dve.tensor_tensor(self.cand[:, :, :], self.logits[:, :, :], self.wide(self.peak),
                          ALU.subtract).then_inc(self.shifted, 1)
        dve.wait_ge(self.exped, 1)
        step(dve.tensor_reduce(self.total[:, :], self.probs[:, :, :], AX_X, ALU.add))
        step(dve.reciprocal(self.total[:, :], self.total[:, :]))
        step(dve.tensor_tensor(self.probs[:, :, :], self.probs[:, :, :], self.wide(self.total), ALU.mult))
        dve.wait_ge(self.made, 2)
        for k in range(self.K):
            step(dve.tensor_reduce(self.top[k][:, :], self.probs[:, :, :], AX_X, ALU.max))
            step(dve.tensor_tensor(self.cand[:, :, :], self.probs[:, :, :], self.wide(self.top[k]), ALU.is_equal))
            step(dve.scalar_tensor_tensor(out=self.cand[:, :, :], in0=self.cand[:, :, :], scalar=-float(E),
                                          in1=self.index[:, :, :], op0=ALU.mult, op1=ALU.add))
            step(dve.tensor_reduce(self.best[k][:, :], self.cand[:, :, :], AX_X, ALU.min))
            step(dve.tensor_tensor(self.hot[k][:, :, :], self.cand[:, :, :], self.wide(self.best[k]), ALU.is_equal))
            if k < self.K - 1:
                step(dve.scalar_tensor_tensor(out=self.probs[:, :, :], in0=self.hot[k][:, :, :], scalar=-2.0,
                                              in1=self.probs[:, :, :], op0=ALU.mult, op1=ALU.add))
        if self.K > 1:
            step(dve.tensor_tensor(self.chosen[:, :, :], self.hot[0][:, :, :], self.hot[1][:, :, :], ALU.add))
        dve.sem_inc(self.chosen_ready, 1)
        dve.wait_ge(self.counted, 1)
        in_tile = self.core.ps[:, 0, 0:n].rearrange("p (t e) -> p t e", e=E)
        of_tile = self.core.ps[:, 1, 0:n].rearrange("p (t e) -> p t e", e=E)
        a, b = self.count
        step(dve.tensor_copy(a[:, :, :], of_tile))
        d = 1
        while d < T:
            step(dve.tensor_copy(b[:, 0:d, :], a[:, 0:d, :]))
            step(dve.tensor_tensor(b[:, d:T, :], a[:, d:T, :], a[:, 0:T - d, :], ALU.add))
            a, b = b, a
            d *= 2
        step(dve.tensor_tensor(self.pos[:, :, :], a[:, :, :], of_tile, ALU.subtract))
        step(dve.tensor_tensor(self.pos[:, :, :], self.pos[:, :, :], in_tile, ALU.add))
        return step, a[:, T - 1, :], b


def capacity(E):
    return -(-N * 2 * 5 // 4 // E)


def spare_rows(E, C):
    return -(-(E + 1) * C // (4 * P)) * 4 * P


def capacity_moe(nc, core, router_w_d, router_b_d, gate_d, up_d, down_d, sgate_d, sup_d, sdown_d, ROWS, OUTS):
    ps, xT, xr, h = core.ps, core.xT, core.xr, core.h
    E, _, F = gate_d.shape
    C = capacity(E)
    SPARE = spare_rows(E, C)
    CHUNKS = [(c, min(P, F - c * P)) for c in range(-(-F // P))]
    SLOTS = [(t, min(P, C - t * P)) for t in range(-(-C // P))]
    NF, NS = len(CHUNKS), len(SLOTS)
    ZERO = SPARE * D // P // 4
    with ExitStack() as ctx:
        s = Scope(nc, ctx, "cmoe")
        xn = s.sb("xn", [P, TILES, D])
        r = Router(nc, core, s, E, 2)
        slot = [s.sb(f"slot{k}", [P, TILES]) for k in range(2)]
        place = [s.sb(f"place{k}", [P, TILES]) for k in range(2)]
        kept = [s.sb(f"kept{k}", [P, TILES]) for k in range(2)]
        spare = [s.sb(f"spare{k}", [P, TILES]) for k in range(2)]
        weight = [s.sb(f"weight{k}", [P, TILES]) for k in range(2)]
        to_row = [s.sb(f"to_row{k}", [P, TILES], I32) for k in range(2)]
        from_row = [s.sb(f"from_row{k}", [P, TILES], I32) for k in range(2)]
        zeros_done = s.sem("zeros_done")

        with ExitStack() as ctx_a:
            sa = Scope(nc, ctx_a, "cmoe_shared", s)
            Wr = sa.sb("Wr", [P, DC, E])
            br = sa.sb("br", [P, E])
            Wg = sa.sb("Wg", [P, DC, F])
            Wu = sa.sb("Wu", [P, DC, F])
            Wd = sa.sb("Wd", [P, NF, D])
            xnT = sa.sb("xnT", [P, DC, N])
            zeros = sa.sb("zeros", [P, ZERO])
            sg = sa.sb("sg", [P, 2, SEQ])
            act_ = sa.sb("act", [P, NF, SEQ])
            zeros_made = sa.sem("zeros_made")
            router_in = sa.sem("router_in")
            weights_in = sa.sem("weights_in")
            logits_full = sa.sem("logits_full")
            logits_ready = sa.sem("logits_ready")
            rows_ready = sa.sem("rows_ready")
            scattered = core.pool_dma.sem("cmoe_scattered")
            gated_full = sa.sem("gated_full")
            sg_ready = sa.sem("sg_ready")
            swish_ready = sa.sem("swish_ready")
            act_ready = sa.sem("act_ready")
            out_full = sa.sem("out_full")
            product_added = sa.sem("product_added")
            row_added = sa.sem("row_added")
            norm = StreamNorm(nc, core, sa, xn, xnT)

            with nc.Block() as block:
                @block.sync
                def _(sp):
                    sp.dma_start(Wr[:, :, :], router_w_d.rearrange("(c p) n -> p c n", p=P)).then_inc(router_in, 16)
                    sp.dma_start(br[:, :], router_b_d.partition_broadcast(P)).then_inc(router_in, 16)
                    sp.dma_start(Wg[:, :, :], sgate_d.rearrange("(c p) n -> p c n", p=P)).then_inc(weights_in, 16)
                    sp.dma_start(Wu[:, :, :], sup_d.rearrange("(c p) n -> p c n", p=P)).then_inc(weights_in, 16)
                    sp.dma_start(Wd[:, :, :], sdown_d.rearrange("(c p) n -> p c n", p=P)).then_inc(weights_in, 16)
                    sp.wait_ge(zeros_made, 1)
                    rows = ROWS[0:SPARE, :].rearrange("(q a) d -> q (a d)", q=4 * P)
                    for q in range(4):
                        sp.dma_start(rows[q * P:(q + 1) * P, :], zeros[:, :]).then_inc(zeros_done, 16)

                @block.tensor
                def _(pe):
                    norm.turn(pe)
                    pe.wait_ge(router_in, 32)
                    for t in range(TILES):
                        if t % TPB == 0:
                            pe.wait_ge(norm.outT_ready, t // TPB + 1)
                        for c in range(DC):
                            last = pe.matmul(ps[:, 4, t * E:(t + 1) * E], xnT[:, c, t * P:(t + 1) * P], Wr[:, c, :],
                                             start=(c == 0), stop=(c == DC - 1))
                    last.then_inc(logits_full, 1)
                    r.count_before(pe)
                    pe.wait_ge(weights_in, 48)
                    with pe.Fori(0, BATCH) as b:
                        for m, w in CHUNKS:
                            pe.wait_ge(act_ready, b * NF + m + 1)
                            for half, W in ((0, Wg), (1, Wu)):
                                for c in range(DC):
                                    last = pe.matmul(ps[0:w, m, half * SEQ:(half + 1) * SEQ],
                                                     W[:, c, m * P:m * P + w], xnT[:, c, ds(b * SEQ, SEQ)],
                                                     start=(c == 0), stop=(c == DC - 1))
                            last.then_inc(gated_full, 1)
                        pe.wait_ge(product_added, b + 1)
                        for t in range(TPB):
                            for m, w in CHUNKS:
                                pe.wait_ge(act_ready, b * NF + NF + m + 1)
                                last = pe.matmul(ps[:, 3, t * D:(t + 1) * D], act_[0:w, m, t * P:(t + 1) * P],
                                                 Wd[0:w, m, :], start=(m == 0), stop=(m == NF - 1))
                        last.then_inc(out_full, 1)

                @block.scalar
                def _(act):
                    norm.evacuate(act)
                    r.exp(act)
                    with act.Fori(0, BATCH) as b:
                        for m, w in CHUNKS:
                            act.wait_ge(gated_full, b * NF + m + 1)
                            act.wait_ge(act_ready, b * NF + NF + m // 2)
                            act.activation(sg[0:w, m % 2, :], ps[0:w, m, 0:SEQ], ACT.Sigmoid).then_inc(sg_ready, 1)

                @block.gpsimd
                def _(pool):
                    pool.memset(zeros[:, :], 0.0).then_inc(zeros_made, 1)
                    norm.root(pool)
                    r.tables(pool)
                    for k in range(2):
                        pool.iota(spare[k][:, :], pattern=[[P, TILES]], base=SPARE + k * N, channel_multiplier=1,
                                  allow_small_or_imprecise_dtypes=True).then_inc(r.made, 1)
                    pool.wait_ge(zeros_done, 64)
                    for k in range(2):
                        pool.wait_ge(rows_ready, k + 1)
                        for t in range(TILES):
                            pool.indirect_dma_start(ROWS, bass.IndirectOffsetOnAxis(ap=to_row[k][:, t:t + 1], axis=0),
                                                    xn[:, t, :], None).then_inc(scattered, 16)
                    pool.wait_ge(scattered, 16 * 2 * TILES)

                @block.vector
                def _(dve):
                    norm.norm(dve)
                    dve.wait_ge(router_in, 32)
                    dve.wait_ge(logits_full, 1)
                    dve.tensor_tensor(r.logits[:, :, :], ps[:, 4, 0:TILES * E].rearrange("p (t e) -> p t e", e=E),
                                      br[:, :].unsqueeze(1).broadcast_to([P, TILES, E]),
                                      ALU.add).then_inc(logits_ready, 1)
                    dve.wait_ge(logits_ready, 1)
                    step, _, tmp = r.route(dve)
                    dve.wait_ge(r.made, 4)
                    for k in range(2):
                        step(dve.tensor_tensor(tmp[:, :, :], r.hot[k][:, :, :], r.pos[:, :, :], ALU.mult))
                        step(dve.tensor_reduce(place[k][:, :], tmp[:, :, :], AX_X, ALU.add))
                        step(dve.tensor_scalar(kept[k][:, :], place[k][:, :], float(C), None, ALU.is_lt))
                        step(dve.tensor_scalar(place[k][:, :], place[k][:, :], float(C - 1), None, ALU.min))
                        step(dve.tensor_scalar(slot[k][:, :], r.best[k][:, :], float(E), float(C), ALU.add, ALU.mult))
                        step(dve.tensor_tensor(slot[k][:, :], slot[k][:, :], place[k][:, :], ALU.add))
                        step(dve.tensor_copy(from_row[k][:, :], slot[k][:, :]))
                        step(dve.tensor_tensor(slot[k][:, :], slot[k][:, :], spare[k][:, :], ALU.subtract))
                        step(dve.tensor_tensor(slot[k][:, :], slot[k][:, :], kept[k][:, :], ALU.mult))
                        step(dve.tensor_tensor(slot[k][:, :], slot[k][:, :], spare[k][:, :], ALU.add))
                        dve.tensor_copy(to_row[k][:, :], slot[k][:, :]).then_inc(rows_ready, 1)
                    total = r.total
                    step(dve.tensor_tensor(total[:, :], r.top[0][:, :], r.top[1][:, :], ALU.add))
                    step(dve.tensor_scalar(total[:, :], total[:, :], 1e-9, None, ALU.add))
                    step(dve.reciprocal(total[:, :], total[:, :]))
                    for k in range(2):
                        step(dve.tensor_tensor(weight[k][:, :], r.top[k][:, :], total[:, :], ALU.mult))
                        step(dve.tensor_tensor(weight[k][:, :], weight[k][:, :], kept[k][:, :], ALU.mult))
                    dve.sem_inc(act_ready, NF)
                    dve.sem_inc(product_added, 1)
                    with dve.Fori(0, BATCH) as b:
                        for m, w in CHUNKS:
                            dve.wait_ge(sg_ready, b * NF + m + 1)
                            dve.tensor_tensor(sg[0:w, m % 2, :], sg[0:w, m % 2, :], ps[0:w, m, 0:SEQ],
                                              ALU.mult).then_inc(swish_ready, 1)
                            dve.wait_ge(swish_ready, b * NF + m + 1)
                            dve.tensor_tensor(act_[0:w, m, :], sg[0:w, m % 2, :], ps[0:w, m, SEQ:2 * SEQ],
                                              ALU.mult).then_inc(act_ready, 1)
                        dve.wait_ge(out_full, b + 1)
                        dve.tensor_tensor(h[:, ds(b * TPB, TPB), :], ps[:, 3, :].rearrange("p (t d) -> p t d", t=TPB),
                                          h[:, ds(b * TPB, TPB), :], ALU.add).then_inc(product_added, 1)
                        dve.wait_ge(product_added, b + 2)
                        dve.tensor_tensor(h[:, ds(b * TPB, TPB), :], h[:, ds(b * TPB, TPB), :],
                                          xn[:, ds(b * TPB, TPB), :], ALU.add).then_inc(row_added, 1)
                    dve.wait_ge(row_added, BATCH)

        with ExitStack() as ctx_c:
            sc = Scope(nc, ctx_c, "cmoe_experts", s)
            GATE, UP, DOWN, PIECES = 0, 1, 2, 3
            raw = sc.sb("raw", [P, PIECES, NF * D])
            W_parts = [sc.sb(f"W_{n}", [P, 2, PIECES, NF * D], F32R) for n in ("high", "low")]
            WIDTHS = (DC * F, DC * F, NF * D)
            assert DC * F <= NF * D
            xe = sc.sb("xe", [P, 2, NS, D])
            xeT_parts = [sc.sb(f"xeT_{n}", [P, DC, C], F32R) for n in ("high", "low")]
            sg = sc.sb("sg", [P, 2, C])
            act_ = sc.sb("act", [P, 2, C])
            act_parts = [sc.sb(f"act_{n}", [P, 2, NF, NS * P], F32R) for n in ("high", "low")]
            ye = sc.sb("ye", [P, 2, NS, D])
            raw_in = [sc.sem(f"raw_in{p}") for p in range(PIECES)]
            W_high_ready = sc.sem("W_high_ready")
            W_low_ready = sc.sem("W_low_ready")
            pad_zero = sc.sem("pad_zero")
            rows_in = [sc.sem(f"rows_in{u}") for u in range(2)]
            turned = sc.sem("turned")
            xeT_high_ready = sc.sem("xeT_high_ready")
            xeT_ready = sc.sem("xeT_ready")
            gated_full = sc.sem("gated_full")
            sg_ready = sc.sem("sg_ready")
            swish_ready = sc.sem("swish_ready")
            product_ready = sc.sem("product_ready")
            act_high_ready = sc.sem("act_high_ready")
            act_ready = sc.sem("act_ready")
            out_full = sc.sem("out_full")
            ye_ready = sc.sem("ye_ready")
            stored = [sc.sem(f"stored{u}") for u in range(2)]

            with nc.Block() as block:
                @block.sync
                def _(sp):
                    def rows(e, u, first):
                        if not first:
                            sp.wait_ge(turned, e - 1)
                        sp.dma_start(xe[:, u, 0:NS - 1, :],
                                     ROWS[ds(e * C, (NS - 1) * P), :].rearrange("(t p) d -> p t d", p=P)
                                     ).then_inc(rows_in[u], 16)
                        sp.dma_start(xe[0:SLOTS[-1][1], u, NS - 1, :],
                                     ROWS[ds(e * C + (NS - 1) * P, SLOTS[-1][1]), :]).then_inc(rows_in[u], 16)

                    def weights(e, p, first=False):
                        if not first:
                            split = e * PIECES + 2 if p == DOWN else e * PIECES - PIECES + p + 1
                            sp.wait_ge(W_low_ready, split)
                        W_d, n = ((gate_d, F), (up_d, F), (down_d, D))[p]
                        sp.dma_start(raw[:, p, 0:WIDTHS[p]].rearrange("p (c n) -> p c n", n=n),
                                     W_d[ds(e, 1), :, :].rearrange("e (c p) n -> p (e c) n", p=P)
                                     ).then_inc(raw_in[p], 16)

                    def store(e, u):
                        n = SLOTS[-1][1]
                        sp.wait_ge(ye_ready, e + 2)
                        sp.dma_start(OUTS[ds(e * C, 2 * P), :].rearrange("(t p) d -> p t d", p=P),
                                     ye[:, u, 0:2, :]).then_inc(stored[u], 16)
                        sp.dma_start(OUTS[ds(e * C + 2 * P, n), :], ye[0:n, u, 2, :]).then_inc(stored[u], 16)

                    rows(0, 0, True)
                    weights(0, GATE, True)
                    weights(0, UP, True)
                    rows(1, 1, True)
                    weights(0, DOWN, True)
                    weights(1, GATE)
                    weights(1, UP)
                    rows(2, 0, False)
                    weights(2, GATE)
                    weights(2, UP)
                    weights(1, DOWN)
                    with sp.Fori(1, E // 2 - 1) as i:
                        for u in range(2):
                            e = i * 2 + u
                            rows(e + 1, 1 - u, False)
                            weights(e + 1, GATE)
                            weights(e + 1, UP)
                            store(e - 2, u)
                            weights(e, DOWN)
                    rows(E - 1, 1, False)
                    weights(E - 1, GATE)
                    weights(E - 1, UP)
                    store(E - 4, 0)
                    weights(E - 2, DOWN)
                    store(E - 3, 1)
                    weights(E - 1, DOWN)
                    store(E - 2, 0)
                    store(E - 1, 1)
                    for u in range(2):
                        sp.wait_ge(stored[u], 32 + E // 2 * 32)

                @block.gpsimd
                def _(pool):
                    for parts in act_parts:
                        pool.memset(parts[:, :, :, C:NS * P].bitcast(F32), 0.0).then_inc(pad_zero, 1)

                    def weights_low(n, p, u):
                        pool.wait_ge(W_high_ready, n + 1)
                        pool.tensor_tensor(W_parts[1][:, u, p, 0:WIDTHS[p]], raw[:, p, 0:WIDTHS[p]],
                                           W_parts[0][:, u, p, 0:WIDTHS[p]].bitcast(F32),
                                           ALU.subtract).then_inc(W_low_ready, 1)

                    def after(e, u):
                        weights_low(e * PIECES + 2, GATE, 1 - u)
                        weights_low(e * PIECES + 3, UP, 1 - u)
                        weights_low(e * PIECES + 4, DOWN, u)

                    weights_low(0, GATE, 0)
                    weights_low(1, UP, 0)
                    after(0, 0)
                    with pool.Fori(0, E // 2 - 1) as i:
                        for u in (1, 0):
                            after(i * 2 + (2 - u), u)
                    weights_low(E * PIECES - 1, DOWN, 1)

                @block.tensor
                def _(pe):
                    def turn(e, i, u):
                        pe.wait_ge(rows_in[u], i * 32 + 32)
                        for c in range(DC):
                            for t, n in SLOTS:
                                last = pe.transpose(ps[:, 6 + c, t * P:t * P + n], xe[0:n, u, t, c * P:(c + 1) * P],
                                                    core.ident[0:n, 0:n])
                        last.then_inc(turned, 1)

                    def gate_up(e, u):
                        pe.wait_ge(xeT_ready, e + 1)
                        pe.wait_ge(W_low_ready, e * PIECES + 2)
                        for m, w in CHUNKS:
                            pe.wait_ge(act_ready, e * NF + m + 1)
                            for half, piece in ((0, GATE), (1, UP)):
                                terms = [(c, y, x) for c in range(DC) for y, x in PASSES]
                                for n, (c, y, x) in enumerate(terms):
                                    last = pe.matmul(ps[0:w, 2 * ((u + m) % 2) + half, 0:C],
                                                     W_parts[y][:, u, piece, c * F + m * P:c * F + m * P + w],
                                                     xeT_parts[x][:, c, :], start=(n == 0),
                                                     stop=(n == len(terms) - 1))
                            last.then_inc(gated_full, 1)

                    def down(e, u):
                        pe.wait_ge(ye_ready, e + 1)
                        for t in range(NS):
                            for m, w in CHUNKS:
                                if t == 0:
                                    pe.wait_ge(act_ready, e * NF + m + 3)
                                for n, (y, x) in enumerate(PASSES):
                                    last = pe.matmul(ps[:, 4 + t // 2, t % 2 * D:(t % 2 + 1) * D],
                                                     act_parts[x][0:w, u, m, t * P:(t + 1) * P],
                                                     W_parts[y][0:w, u, DOWN, m * D:(m + 1) * D],
                                                     start=(m + n == 0), stop=(m == NF - 1 and n == 2))
                        last.then_inc(out_full, 1)

                    pe.wait_ge(pad_zero, 2)
                    turn(0, 0, 0)
                    gate_up(0, 0)
                    turn(1, 0, 1)
                    with pe.Fori(0, E // 2 - 1) as i:
                        for u in (1, 0):
                            e = i * 2 + (2 - u)
                            gate_up(e, u)
                            turn(e + 1, i + 1, 1 - u)
                            down(e - 1, 1 - u)
                    gate_up(E - 1, 1)
                    down(E - 2, 0)
                    pe.wait_ge(W_low_ready, E * PIECES)
                    down(E - 1, 1)

                @block.scalar
                def _(act):
                    def evacuate(e):
                        act.wait_ge(turned, e + 1)
                        act.activation(xeT_parts[0][:, :, :], ps[:, 6:8, 0:C], ACT.Copy).then_inc(xeT_high_ready, 1)

                    def weights_high(e, p, u):
                        act.wait_ge(raw_in[p], e * 16 + 16)
                        act.activation(W_parts[0][:, u, p, 0:WIDTHS[p]], raw[:, p, 0:WIDTHS[p]],
                                       ACT.Copy).then_inc(W_high_ready, 1)

                    def sigmoids(e, u, last=False):
                        for m, w in CHUNKS:
                            x = (u + m) % 2
                            act.wait_ge(gated_full, e * NF + m + 1)
                            act.wait_ge(act_ready, e * NF + m + 1)
                            act.activation(sg[0:w, x, :], ps[0:w, 2 * x, 0:C], ACT.Sigmoid).then_inc(sg_ready, 1)
                            if m == DOWN:
                                weights_high(e, DOWN, u)
                            elif not last:
                                weights_high(e + 1, m, 1 - u)
                        if not last:
                            evacuate(e + 1)

                    def output(e, i, u):
                        act.wait_ge(out_full, e + 1)
                        act.wait_ge(stored[u], i * 32 + 32)
                        act.activation(ye[:, u, 0:2, :], ps[:, 4, :].rearrange("p (t d) -> p t d", t=2), ACT.Copy)
                        n = SLOTS[-1][1]
                        act.activation(ye[0:n, u, 2, :], ps[0:n, 5, 0:D], ACT.Copy).then_inc(ye_ready, 1)

                    act.sem_inc(ye_ready, 1)
                    for u in range(2):
                        act.sem_inc(stored[u], 32)
                    assert NF == PIECES
                    evacuate(0)
                    weights_high(0, GATE, 0)
                    weights_high(0, UP, 0)
                    sigmoids(0, 0)
                    with act.Fori(0, E // 2 - 1) as i:
                        for u in (1, 0):
                            sigmoids(i * 2 + (2 - u), u)
                            output(i * 2 + (1 - u), i, 1 - u)
                    sigmoids(E - 1, 1, last=True)
                    output(E - 2, E // 2 - 1, 0)
                    output(E - 1, E // 2 - 1, 1)

                @block.vector
                def _(dve):
                    def low(e):
                        dve.wait_ge(xeT_high_ready, e + 1)
                        dve.tensor_tensor(xeT_parts[1][:, :, :], ps[:, 6:8, 0:C], xeT_parts[0][:, :, :].bitcast(F32),
                                          ALU.subtract).then_inc(xeT_ready, 1)

                    def activations(e, u):
                        for m, w in CHUNKS:
                            x = (u + m) % 2
                            dve.wait_ge(sg_ready, e * NF + m + 1)
                            dve.tensor_tensor(sg[0:w, x, :], sg[0:w, x, :], ps[0:w, 2 * x, 0:C],
                                              ALU.mult).then_inc(swish_ready, 1)
                            dve.wait_ge(swish_ready, e * NF + m + 1)
                            dve.tensor_tensor(act_[0:w, x, :], sg[0:w, x, :], ps[0:w, 2 * x + 1, 0:C],
                                              ALU.mult).then_inc(product_ready, 1)
                            dve.wait_ge(product_ready, e * NF + m + 1)
                            high, low = (p[0:w, u, m, 0:C] for p in act_parts)
                            dve.tensor_copy(high, act_[0:w, x, :]).then_inc(act_high_ready, 1)
                            dve.wait_ge(act_high_ready, e * NF + m + 1)
                            dve.tensor_tensor(low, act_[0:w, x, :], high.bitcast(F32),
                                              ALU.subtract).then_inc(act_ready, 1)

                    dve.sem_inc(act_ready, 2)
                    low(0)
                    activations(0, 0)
                    low(1)
                    with dve.Fori(0, E // 2 - 1) as i:
                        for u in (1, 0):
                            activations(i * 2 + (2 - u), u)
                            low(i * 2 + (3 - u))
                    activations(E - 1, 1)

        with ExitStack() as ctx_d:
            sd = Scope(nc, ctx_d, "cmoe_combine", s)
            y = [sd.sb(f"y{k}", [P, TILES, D]) for k in range(2)]
            y_in = [core.pool_dma.sem(f"cmoe_y_in{t}") for t in range(4)]
            added = sd.sem("added")
            with nc.Block() as block:
                @block.gpsimd
                def _(pool):
                    for t in range(TILES):
                        for k in range(2):
                            pool.indirect_dma_start(y[k][:, t, :], None, OUTS,
                                                    bass.IndirectOffsetOnAxis(ap=from_row[k][:, t:t + 1], axis=0)
                                                    ).then_inc(y_in[t // 4], 16)

                @block.vector
                def _(dve):
                    for g in range(4):
                        dve.wait_ge(y_in[g], 16 * 8)
                        for k in range(2):
                            for t in range(4 * g, 4 * g + 4):
                                dve.scalar_tensor_tensor(out=h[:, t, :], in0=y[k][:, t, :],
                                                         scalar=weight[k][:, t:t + 1], in1=h[:, t, :],
                                                         op0=ALU.mult, op1=ALU.add).then_inc(added, 1)
                            dve.wait_ge(added, 8 * g + 4 * k + 4)
        s.clear()


def column_attention(nc, core, ln_d, Wqkv_d, Wout_d):
    ps, h = core.ps, core.h
    HD = 64
    H = Wqkv_d.shape[1] // 3 // HD
    HC = H * HD // P
    GROUP, HALF = 32, 16
    GROUPS = SEQ // GROUP
    UH = 8
    UNITS = 2 * H // UH
    MASKED = -1e30
    SCALE = 1.0 / float(np.sqrt(HD))
    with ExitStack() as ctx:
        s = Scope(nc, ctx, "cattn")
        xT_all = s.sb("xT_all", [P, DC, N + GROUP])
        ctxT = s.sb("ctxT", [P, HC, N])
        Wout = s.sb("Wout", [P, HC, D])
        Wqkv = s.sb("Wqkv", [P, DC, 3 * H * HD])
        weights_in = s.sem("weights_in")
        Wout_in = s.sem("Wout_in")

        with ExitStack() as ctx_a:
            sa = Scope(nc, ctx_a, "cattn_norm", s)
            affine = sa.sb("affine", [P, 2, DC])
            affine_in = sa.sem("affine_in")
            pad_zero = sa.sem("pad_zero")
            xn = sa.sb("xn", [P, TILES, D])
            norm = StreamNorm(nc, core, sa, xn, xT_all, eps=(LN_EPS, 1e-6),
                              affine=(affine[:, 0, :], affine[:, 1, :]))
            with nc.Block() as block:
                @block.sync
                def _(sp):
                    sp.dma_start(affine[:, :, :], ln_d).then_inc(affine_in, 16)
                    sp.dma_start(Wqkv[:, :, :], Wqkv_d.rearrange("(c p) n -> p c n", p=P)).then_inc(weights_in, 16)
                    sp.dma_start(Wout[:, :, :], Wout_d.rearrange("(c p) n -> p c n", p=P)).then_inc(Wout_in, 16)

                @block.tensor
                def _(pe):
                    norm.turn(pe)

                @block.scalar
                def _(act):
                    act.wait_ge(affine_in, 16)
                    norm.evacuate(act)

                @block.gpsimd
                def _(pool):
                    pool.memset(xT_all[:, :, N:N + GROUP], 0.0).then_inc(pad_zero, 1)
                    norm.root(pool)
                    pool.wait_ge(pad_zero, 1)

                @block.vector
                def _(dve):
                    norm.norm(dve)

        with ExitStack() as ctx_b:
            sb_ = Scope(nc, ctx_b, "cattn_heads", s)
            ident16 = sb_.sb("ident16", [P, P], BF16)
            mask = sb_.sb("mask", [P, 4, P], BF16)
            xg = sb_.sb("xg", [P, DC, 2 * P])
            qkT = sb_.sb("qkT", [P, 2 * HC, 2 * P])
            v = sb_.sb("v", [P, 2, H * HD])
            probs = sb_.sb("probs", [P, 4, UH, P])
            probsT = sb_.sb("probsT", [P, 2, UH, P])
            peak = sb_.sb("peak", [P, 2, UH])
            total = sb_.sb("total", [P, 2, UH])
            mask_step = sb_.sem("mask_step")
            xg_ready = sb_.sem("xg_ready")
            scores_full = sb_.sem("scores_full")
            peak_ready = sb_.sem("peak_ready")
            shifted = sb_.sem("shifted")
            exped = sb_.sem("exped")
            total_ready = sb_.sem("total_ready")
            inverse_ready = sb_.sem("inverse_ready")
            probs_ready = sb_.sem("probs_ready")
            turned = sb_.sem("turned")
            probsT_ready = sb_.sem("probsT_ready")
            job_full = sb_.sem("job_full")
            job_read = sb_.sem("job_read")
            JOBS = ["ctx0", "qk0", "qk1", "ctx1", "qk2", "qk3", "ctx2", "qk4", "qk5", "qk6", "qk7", "ctx3",
                    "v0", "v1", "v2", "v3"]
            NJ = len(JOBS)

            with nc.Block() as block:
                @block.gpsimd
                def _(pool):
                    step = Chain(pool, mask_step)
                    step(pool.memset(mask[:, :, :], MASKED))
                    for b in range(BATCH):
                        step(pool.affine_select(out=mask[:, :, :], in_=mask[:, :, :], compare_op=ALU.not_equal,
                                                fill=0.0, base=-b * HALF, pattern=[[0, 4], [-1, P]],
                                                channel_multiplier=1))
                    step(pool.tensor_copy(ident16[:, :], core.ident[:, :]))

                @block.tensor
                def _(pe):
                    def job(name, base):
                        q = JOBS.index(name)
                        pe.wait_ge(job_read, base + q + 1)
                        return 6 + q % 2

                    def qk(j, base):
                        bank = job(f"qk{j}", base)
                        for half in range(2):
                            col = (2 * j + half) * P
                            for c in range(DC):
                                last = pe.matmul(ps[:, bank, half * 2 * P:(half + 1) * 2 * P],
                                                 Wqkv[:, c, col:col + P], xg[:, c, :],
                                                 start=(c == 0), stop=(c == DC - 1))
                        last.then_inc(job_full, 1)

                    def values(i, base):
                        u, half = i // 2, i % 2
                        bank = job(f"v{i}", base)
                        col = (2 * H * HD) + half * 512
                        for c in range(DC):
                            last = pe.matmul(ps[:, bank, :], xg[:, c, u * P:(u + 1) * P],
                                             Wqkv[:, c, col:col + 512], start=(c == 0), stop=(c == DC - 1))
                        last.then_inc(job_full, 1)

                    def scores(k, g):
                        u, m0, bank = k // 2, k % 2 * 4, 2 * (k % 2)
                        pe.wait_ge(shifted, g * UNITS + k + 1)
                        for odd in range(2):
                            pe.matmul(ps[:, bank + odd, :], ident16[:, :], mask[:, :, :].rearrange("p r k -> p (r k)"),
                                      start=True, stop=False, skip_group_check=True)
                        for j in range(4):
                            for odd in range(2):
                                rows = slice(odd * HD, (odd + 1) * HD)
                                last = pe.matmul(ps[:, bank + odd, j * P:(j + 1) * P],
                                                 qkT[rows, m0 + j, u * P:(u + 1) * P],
                                                 qkT[rows, HC + m0 + j, u * P:(u + 1) * P],
                                                 start=False, stop=(j == 3), skip_group_check=True)
                        last.then_inc(scores_full, 1)

                    def turn(k, g):
                        pe.wait_ge(probs_ready, g * UNITS + k + 1)
                        pe.wait_ge(probsT_ready, g * UNITS + k + 1)
                        for i in range(UH):
                            last = pe.transpose(ps[:, 4 + i // 4, i % 4 * P:(i % 4 + 1) * P], probs[:, k, i, :],
                                                core.ident[:, :])
                        last.then_inc(turned, 1)

                    def mix(k, base, g):
                        u, m0 = k // 2, k % 2 * 4
                        bank = job(f"ctx{k}", base)
                        pe.wait_ge(probsT_ready, g * UNITS + k + 2)
                        for j in range(4):
                            for odd in range(2):
                                head = 2 * (m0 + j) + odd
                                last = pe.matmul(ps[odd * HD:(odd + 1) * HD, bank, j * P:(j + 1) * P],
                                                 v[:, u, head * HD:(head + 1) * HD], probsT[:, k % 2, odd * 4 + j, :],
                                                 start=True, stop=True, skip_group_check=True)
                        last.then_inc(job_full, 1)

                    pe.wait_ge(weights_in, 16)
                    pe.wait_ge(mask_step, BATCH + 2)
                    pe.wait_ge(xg_ready, 1)
                    first = 0
                    for j in range(HC):
                        if first >= 2:
                            pe.wait_ge(job_read, 2 + first - 1)
                        for half in range(2):
                            col = (2 * j + half) * P
                            for c in range(DC):
                                last = pe.matmul(ps[:, 6 + first % 2, half * 2 * P:(half + 1) * 2 * P],
                                                 Wqkv[:, c, col:col + P], xg[:, c, :],
                                                 start=(c == 0), stop=(c == DC - 1))
                        last.then_inc(job_full, 1)
                        first += 1
                    for u in range(2):
                        for half in range(2):
                            pe.wait_ge(job_read, 2 + first - 1)
                            col = (2 * H * HD) + half * 512
                            for c in range(DC):
                                last = pe.matmul(ps[:, 6 + first % 2, :], xg[:, c, u * P:(u + 1) * P],
                                                 Wqkv[:, c, col:col + 512], start=(c == 0), stop=(c == DC - 1))
                            last.then_inc(job_full, 1)
                            first += 1
                    assert first == HC + 4 and first % 2 == 0

                    pe.wait_ge(job_read, 2 + HC)
                    scores(0, 0)
                    scores(1, 0)
                    with pe.Fori(0, GROUPS) as g:
                        base = g * NJ + first
                        scores(2, g)
                        turn(0, g)
                        scores(3, g)
                        turn(1, g)
                        pe.wait_ge(job_read, base + 2)
                        mix(0, base, g)
                        pe.wait_ge(xg_ready, g + 2)
                        qk(0, base)
                        qk(1, base)
                        turn(2, g)
                        mix(1, base, g)
                        qk(2, base)
                        qk(3, base)
                        turn(3, g)
                        mix(2, base, g)
                        for j in range(4, HC):
                            qk(j, base)
                        mix(3, base, g)
                        values(0, base)
                        pe.wait_ge(job_read, base + 2 + JOBS.index("qk7") + 1)
                        scores(0, g + 1)
                        values(1, base)
                        scores(1, g + 1)
                        values(2, base)
                        values(3, base)

                @block.scalar
                def _(act):
                    def read(n, out, src):
                        act.wait_ge(job_full, n + 1)
                        act.activation(out, src, ACT.Copy).then_inc(job_read, 1)

                    def read_qk(n, j, bank):
                        read(n, qkT[:, 2 * j:2 * j + 2, :], ps[:, bank, :].rearrange("p (m n) -> p m n", m=2))

                    def read_v(n, u, half, bank):
                        read(n, v[:, u, half * 512:(half + 1) * 512], ps[:, bank, :])

                    def read_ctx(n, k, g, bank):
                        u, m0 = k // 2, k % 2 * 4
                        out = ctxT[:, m0:m0 + 4, :].rearrange("p m (b s) -> p m b s", s=SEQ)
                        act.wait_ge(job_full, n + 1)
                        for j in range(4):
                            ins = act.activation(out[:, j, :, ds(g * GROUP + u * HALF, HALF)],
                                                 ps[:, bank, j * P:(j + 1) * P].rearrange("p (b s) -> p b s", s=HALF),
                                                 ACT.Copy)
                        ins.then_inc(job_read, 1)

                    def exp(k, g):
                        act.wait_ge(shifted, g * UNITS + k + 3)
                        act.activation(probs[:, k, :, :], probs[:, k, :, :], ACT.Exp,
                                       scale=SCALE).then_inc(exped, 1)

                    def read_probsT(k, g):
                        act.wait_ge(turned, g * UNITS + k + 1)
                        act.activation(probsT[:, k % 2, :, :].rearrange("p (x i) n -> p x (i n)", x=2), ps[:, 4:6, :],
                                       ACT.Copy).then_inc(probsT_ready, 1)

                    act.sem_inc(job_read, 2)
                    act.sem_inc(probsT_ready, 1)
                    for j in range(HC):
                        read_qk(j, j, 6 + j % 2)
                    for i in range(4):
                        read_v(HC + i, i // 2, i % 2, 6 + (HC + i) % 2)
                    first = HC + 4
                    exp(0, 0)
                    exp(1, 0)
                    with act.Fori(0, GROUPS) as g:
                        base = g * NJ + first

                        def next_qk(j):
                            q = JOBS.index(f"qk{j}")
                            read_qk(base + q, j, 6 + q % 2)

                        def next_v(i):
                            q = JOBS.index(f"v{i}")
                            read_v(base + q, i // 2, i % 2, 6 + q % 2)

                        def mixed(k):
                            q = JOBS.index(f"ctx{k}")
                            read_ctx(base + q, k, g, 6 + q % 2)

                        read_probsT(0, g)
                        exp(2, g)
                        read_probsT(1, g)
                        mixed(0)
                        exp(3, g)
                        next_qk(0)
                        next_qk(1)
                        read_probsT(2, g)
                        mixed(1)
                        next_qk(2)
                        next_qk(3)
                        read_probsT(3, g)
                        mixed(2)
                        for j in range(4, HC):
                            next_qk(j)
                        mixed(3)
                        next_v(0)
                        exp(0, g + 1)
                        next_v(1)
                        exp(1, g + 1)
                        next_v(2)
                        next_v(3)

                @block.vector
                def _(dve):
                    columns_of = xT_all[:, :, 0:N].rearrange("p c (b s) -> p c b s", s=SEQ)
                    tail = xT_all[:, :, GROUP:N + GROUP].rearrange("p c (b s) -> p c b s", s=SEQ)

                    def group_columns(first):
                        for u in range(2):
                            for c in range(DC):
                                if first is None:
                                    src = columns_of[:, c, :, u * HALF:(u + 1) * HALF]
                                else:
                                    src = tail[:, c, :, ds(first * GROUP + u * HALF, HALF)]
                                ins = dve.tensor_copy(xg[:, c, u * P:(u + 1) * P].rearrange("p (b s) -> p b s", s=HALF),
                                                      src)
                        ins.then_inc(xg_ready, 1)

                    def softmax(k, g):
                        n = g * UNITS + k
                        bank, x = 2 * (k % 2), k % 2
                        scores = ps[:, bank:bank + 2, :].rearrange("p x (i n) -> p (x i) n", i=4)
                        dve.wait_ge(scores_full, n + 1)
                        dve.tensor_reduce(peak[:, x, :], scores, AX_X, ALU.max).then_inc(peak_ready, 1)
                        dve.wait_ge(peak_ready, n + 1)
                        dve.tensor_tensor(probs[:, k, :, :], scores,
                                          peak[:, x, :].unsqueeze(2).broadcast_to([P, UH, P]),
                                          ALU.subtract).then_inc(shifted, 1)

                    def normalise(k, g):
                        n = g * UNITS + k
                        x = k % 2
                        dve.wait_ge(exped, n + 1)
                        dve.tensor_reduce(total[:, x, :], probs[:, k, :, :], AX_X, ALU.add).then_inc(total_ready, 1)
                        dve.wait_ge(total_ready, n + 1)
                        dve.reciprocal(total[:, x, :], total[:, x, :]).then_inc(inverse_ready, 1)
                        dve.wait_ge(inverse_ready, n + 1)
                        dve.tensor_tensor(probs[:, k, :, :], probs[:, k, :, :],
                                          total[:, x, :].unsqueeze(2).broadcast_to([P, UH, P]),
                                          ALU.mult).then_inc(probs_ready, 1)

                    dve.sem_inc(shifted, 2)
                    group_columns(None)
                    softmax(0, 0)
                    softmax(1, 0)
                    normalise(0, 0)
                    normalise(1, 0)
                    with dve.Fori(0, GROUPS) as g:
                        softmax(2, g)
                        dve.wait_ge(job_full, g * NJ + HC + 4)
                        group_columns(g)
                        softmax(3, g)
                        normalise(2, g)
                        normalise(3, g)
                        softmax(0, g + 1)
                        softmax(1, g + 1)
                        normalise(0, g + 1)
                        normalise(1, g + 1)

        with ExitStack() as ctx_c:
            sc = Scope(nc, ctx_c, "cattn_out", s)
            rowT = sc.sb("rowT", [P, 2, HC, SEQ])
            rowT_ready = sc.sem("rowT_ready")
            out_full = sc.sem("out_full")
            row_added = sc.sem("row_added")
            with nc.Block() as block:
                @block.tensor
                def _(pe):
                    pe.wait_ge(Wout_in, 16)
                    with pe.Fori(0, BATCH // 2) as i:
                        for u in range(2):
                            pe.wait_ge(rowT_ready, i * 2 + u + 1)
                            pe.wait_ge(row_added, i * 2 + u + 1)
                            for t in range(TPB):
                                for c in range(HC):
                                    last = pe.matmul(ps[:, u, t * D:(t + 1) * D], rowT[:, u, c, t * P:(t + 1) * P],
                                                     Wout[:, c, :], start=(c == 0), stop=(c == HC - 1))
                            last.then_inc(out_full, 1)

                @block.scalar
                def _(act):
                    for u in range(2):
                        act.activation(rowT[:, u, :, :], ctxT[:, :, u * SEQ:(u + 1) * SEQ],
                                       ACT.Copy).then_inc(rowT_ready, 1)
                    with act.Fori(1, BATCH // 2) as i:
                        for u in range(2):
                            act.wait_ge(out_full, i * 2 + u - 1)
                            act.activation(rowT[:, u, :, :], ctxT[:, :, ds(i * (2 * SEQ) + u * SEQ, SEQ)],
                                           ACT.Copy).then_inc(rowT_ready, 1)

                @block.vector
                def _(dve):
                    dve.sem_inc(row_added, 2)
                    with dve.Fori(0, BATCH // 2) as i:
                        for u in range(2):
                            dve.wait_ge(out_full, i * 2 + u + 1)
                            dve.tensor_tensor(h[:, ds(i * 4 + 2 * u, TPB), :],
                                              ps[:, u, :].rearrange("p (t d) -> p t d", t=TPB),
                                              h[:, ds(i * 4 + 2 * u, TPB), :], ALU.add).then_inc(row_added, 1)
        s.clear()


def top1_blocks(E):
    return (N - E) // BLOCK + E


BLOCK = 256


def top1_moe(nc, core, router_w_d, router_b_d, w1_d, w2_d, ROWS, OUTS):
    ps, xT, xr, h = core.ps, core.xT, core.xr, core.h
    E, _, F2 = w1_d.shape
    F = F2 // 2
    FC = F // P
    NB = top1_blocks(E)
    TB = BLOCK // P
    ZERO = (NB + 1) * BLOCK * D // P // 4
    with ExitStack() as ctx:
        s = Scope(nc, ctx, "tmoe")
        xn = s.sb("xn", [P, TILES, D])
        r = Router(nc, core, s, E, 1)
        blocks = s.sb("blocks", [P, E])
        ends = [s.sb(f"ends{k}", [P, E]) for k in range(2)]
        block_no = s.sb("block_no", [P, NB, E])
        passed = s.sb("passed", [P, NB, E])
        block_expert_f = s.sb("block_expert_f", [P, NB])
        block_expert = s.sb("block_expert", [P, NB], I32)
        slot = s.sb("slot", [P, TILES])
        row_of = s.sb("row_of", [P, TILES], I32)
        zeros_done = s.sem("zeros_done")

        with ExitStack() as ctx_a:
            sa = Scope(nc, ctx_a, "tmoe_norm", s)
            Wr = sa.sb("Wr", [P, DC, E])
            br = sa.sb("br", [P, E])
            zeros = sa.sb("zeros", [P, ZERO])
            zeros_made = sa.sem("zeros_made")
            weights_in = sa.sem("weights_in")
            logits_full = sa.sem("logits_full")
            logits_ready = sa.sem("logits_ready")
            xnT = sa.sb("xnT", [P, DC, N])
            norm = StreamNorm(nc, core, sa, xn, xnT)

            with nc.Block() as block:
                @block.sync
                def _(sp):
                    sp.dma_start(Wr[:, :, :], router_w_d.rearrange("(c p) n -> p c n", p=P)).then_inc(weights_in, 16)
                    sp.dma_start(br[:, :], router_b_d.partition_broadcast(P)).then_inc(weights_in, 16)
                    sp.wait_ge(zeros_made, 1)
                    rows = ROWS.rearrange("(q a) d -> q (a d)", q=4 * P)
                    for q in range(4):
                        sp.dma_start(rows[q * P:(q + 1) * P, :], zeros[:, :]).then_inc(zeros_done, 16)
                    sp.wait_ge(zeros_done, 64)

                @block.tensor
                def _(pe):
                    norm.turn(pe)
                    pe.wait_ge(weights_in, 32)
                    for t in range(TILES):
                        if t % TPB == 0:
                            pe.wait_ge(norm.outT_ready, t // TPB + 1)
                        for c in range(DC):
                            last = pe.matmul(ps[:, 4, t * E:(t + 1) * E], xnT[:, c, t * P:(t + 1) * P], Wr[:, c, :],
                                             start=(c == 0), stop=(c == DC - 1))
                    last.then_inc(logits_full, 1)

                @block.scalar
                def _(act):
                    norm.evacuate(act)

                @block.gpsimd
                def _(pool):
                    pool.memset(zeros[:, :], 0.0).then_inc(zeros_made, 1)
                    norm.root(pool)
                    r.tables(pool)
                    pool.iota(block_no[:, :, :], pattern=[[1, NB], [0, E]], base=0, channel_multiplier=0,
                              allow_small_or_imprecise_dtypes=True).then_inc(r.made, 1)
                    pool.wait_ge(r.made, 3)

                @block.vector
                def _(dve):
                    norm.norm(dve)
                    dve.wait_ge(weights_in, 32)
                    dve.wait_ge(logits_full, 1)
                    dve.tensor_tensor(r.logits[:, :, :], ps[:, 4, 0:TILES * E].rearrange("p (t e) -> p t e", e=E),
                                      br[:, :].unsqueeze(1).broadcast_to([P, TILES, E]),
                                      ALU.add).then_inc(logits_ready, 1)
                    dve.wait_ge(logits_ready, 1)

        with ExitStack() as ctx_b:
            sb_ = Scope(nc, ctx_b, "tmoe_route", s)
            rows_ready = sb_.sem("rows_ready")
            scattered = core.pool_dma.sem("tmoe_scattered")
            with nc.Block() as block:
                @block.scalar
                def _(act):
                    r.exp(act)

                @block.tensor
                def _(pe):
                    r.count_before(pe)

                @block.vector
                def _(dve):
                    step, count, tmp = r.route(dve)
                    step(dve.tensor_scalar(blocks[:, :], count, 0.0, None, ALU.is_gt))
                    for k in range(1, N // BLOCK):
                        step(dve.scalar_tensor_tensor(out=blocks[:, :], in0=count, scalar=float(k * BLOCK),
                                                      in1=blocks[:, :], op0=ALU.is_gt, op1=ALU.add))
                    a, b = ends
                    step(dve.tensor_copy(a[:, :], blocks[:, :]))
                    d = 1
                    while d < E:
                        step(dve.tensor_copy(b[:, 0:d], a[:, 0:d]))
                        step(dve.tensor_tensor(b[:, d:E], a[:, d:E], a[:, 0:E - d], ALU.add))
                        a, b = b, a
                        d *= 2
                    step(dve.tensor_tensor(b[:, :], a[:, :], blocks[:, :], ALU.subtract))
                    step(dve.tensor_scalar(b[:, :], b[:, :], float(BLOCK), None, ALU.mult))
                    step(dve.tensor_tensor(r.pos[:, :, :], r.pos[:, :, :],
                                           b[:, :].unsqueeze(1).broadcast_to([P, TILES, E]), ALU.add))
                    step(dve.tensor_tensor(tmp[:, :, :], r.hot[0][:, :, :], r.pos[:, :, :], ALU.mult))
                    step(dve.tensor_reduce(slot[:, :], tmp[:, :, :], AX_X, ALU.add))
                    dve.tensor_copy(row_of[:, :], slot[:, :]).then_inc(rows_ready, 1)
                    step(dve.tensor_tensor(passed[:, :, :], block_no[:, :, :],
                                           a[:, :].unsqueeze(1).broadcast_to([P, NB, E]), ALU.is_ge))
                    step(dve.tensor_reduce(block_expert_f[:, :], passed[:, :, :], AX_X, ALU.add))
                    step(dve.tensor_scalar(block_expert_f[:, :], block_expert_f[:, :], float(E - 1), None, ALU.min))
                    step(dve.tensor_copy(block_expert[:, :], block_expert_f[:, :]))

                @block.gpsimd
                def _(pool):
                    pool.wait_ge(rows_ready, 1)
                    for t in range(TILES):
                        pool.indirect_dma_start(ROWS, bass.IndirectOffsetOnAxis(ap=row_of[:, t:t + 1], axis=0),
                                                xn[:, t, :], None).then_inc(scattered, 16)
                    pool.wait_ge(scattered, 16 * TILES)

        with ExitStack() as ctx_c:
            sc = Scope(nc, ctx_c, "tmoe_blocks", s)
            PIECES = DC + 1
            assert FC * D == F2
            raw = sc.sb("raw", [P, PIECES, F2])
            W_parts = [sc.sb(f"W_{n}", [P, 2, PIECES, F2], F32R) for n in ("high", "low")]
            xe = sc.sb("xe", [P, 2, TB, D])
            xeT_parts = [sc.sb(f"xeT_{n}", [P, DC, BLOCK], F32R) for n in ("high", "low")]
            sg = sc.sb("sg", [P, 2, BLOCK])
            act_ = sc.sb("act", [P, 2, BLOCK])
            act_parts = [sc.sb(f"act_{n}", [P, FC, BLOCK], F32R) for n in ("high", "low")]
            ye = sc.sb("ye", [P, 2, TB, D])
            raw_in = [sc.sem(f"raw_in{p}") for p in range(PIECES)]
            W_high_ready = sc.sem("W_high_ready")
            W_low_ready = sc.sem("W_low_ready")
            rows_in = [sc.sem(f"rows_in{u}") for u in range(2)]
            turned = sc.sem("turned")
            xeT_high_ready = sc.sem("xeT_high_ready")
            xeT_ready = sc.sem("xeT_ready")
            gated_full = sc.sem("gated_full")
            sg_ready = sc.sem("sg_ready")
            swish_ready = sc.sem("swish_ready")
            product_ready = sc.sem("product_ready")
            act_high_ready = sc.sem("act_high_ready")
            act_ready = sc.sem("act_ready")
            out_full = sc.sem("out_full")
            ye_ready = sc.sem("ye_ready")
            stored = [sc.sem(f"stored{u}") for u in range(2)]
            PAIRS = NB // 2
            assert NB % 2 == 1

            with nc.Block() as block:
                @block.sync
                def _(sp):
                    def rows(j, u, first):
                        if not first:
                            sp.wait_ge(turned, j - 1)
                        sp.dma_start(xe[:, u, :, :], ROWS[ds(j * BLOCK, BLOCK), :].rearrange("(t p) d -> p t d", p=P)
                                     ).then_inc(rows_in[u], 16)

                    def weights(j, first):
                        e = sp.value_load(block_expert[0:1, ds(j, 1)], min_val=0, max_val=E - 1)
                        w1 = w1_d[ds(e, 1), :, :].rearrange("e (c p) n -> p (e c) n", p=P)
                        w2 = w2_d[ds(e, 1), :, :].rearrange("e (m p) n -> p (e m) n", p=P)
                        for p in range(PIECES):
                            if not first:
                                sp.wait_ge(W_low_ready, j * PIECES - PIECES + p + 1)
                            if p < DC:
                                sp.dma_start(raw[:, p, :], w1[:, p, :]).then_inc(raw_in[p], 16)
                            else:
                                sp.dma_start(raw[:, p, :].rearrange("p (m n) -> p m n", n=D),
                                             w2).then_inc(raw_in[p], 16)

                    def store(j, u):
                        sp.wait_ge(ye_ready, j + 2)
                        sp.dma_start(OUTS[ds(j * BLOCK, BLOCK), :].rearrange("(t p) d -> p t d", p=P),
                                     ye[:, u, :, :]).then_inc(stored[u], 16)

                    rows(0, 0, True)
                    weights(0, True)
                    rows(1, 1, True)
                    weights(1, False)
                    with sp.Fori(1, PAIRS) as i:
                        for u in range(2):
                            rows(i * 2 + u, u, False)
                            weights(i * 2 + u, False)
                            store(i * 2 + u - 2, u)
                    rows(NB - 1, 0, False)
                    weights(NB - 1, False)
                    store(NB - 3, 0)
                    rows(NB, 1, False)
                    store(NB - 2, 1)
                    store(NB - 1, 0)
                    sp.wait_ge(rows_in[1], 16 * (NB + 1) // 2)
                    sp.wait_ge(stored[0], 16 + 16 * (PAIRS + 1))
                    sp.wait_ge(stored[1], 16 + 16 * PAIRS)

                @block.gpsimd
                def _(pool):
                    with pool.Fori(0, PAIRS) as i:
                        for u in range(2):
                            for p in range(PIECES):
                                pool.wait_ge(W_high_ready, i * (2 * PIECES) + u * PIECES + p + 1)
                                pool.tensor_tensor(W_parts[1][:, u, p, :], raw[:, p, :],
                                                   W_parts[0][:, u, p, :].bitcast(F32),
                                                   ALU.subtract).then_inc(W_low_ready, 1)
                    for p in range(PIECES):
                        pool.wait_ge(W_high_ready, (NB - 1) * PIECES + p + 1)
                        pool.tensor_tensor(W_parts[1][:, 0, p, :], raw[:, p, :], W_parts[0][:, 0, p, :].bitcast(F32),
                                           ALU.subtract).then_inc(W_low_ready, 1)

                @block.tensor
                def _(pe):
                    def turn(j, i, u):
                        pe.wait_ge(rows_in[u], i * 16 + 16)
                        for c in range(DC):
                            for t in range(TB):
                                last = pe.transpose(ps[:, 7, c * BLOCK + t * P:c * BLOCK + (t + 1) * P],
                                                    xe[:, u, t, c * P:(c + 1) * P], core.ident[:, :])
                        last.then_inc(turned, 1)

                    def mlp(j, i, u):
                        pe.wait_ge(xeT_ready, j + 1)
                        pe.wait_ge(W_low_ready, j * PIECES + DC)
                        for m in range(FC):
                            pe.wait_ge(act_ready, j * FC + m + 1)
                            for half in range(2):
                                terms = [(c, w, x) for c in range(DC) for w, x in PASSES]
                                for n, (c, w, x) in enumerate(terms):
                                    last = pe.matmul(ps[:, m % 4, half * BLOCK:(half + 1) * BLOCK],
                                                     W_parts[w][:, u, c, half * F + m * P:half * F + (m + 1) * P],
                                                     xeT_parts[x][:, c, :], start=(n == 0), stop=(n == len(terms) - 1))
                            last.then_inc(gated_full, 1)
                        turn(j + 1, i + u, 1 - u)
                        pe.wait_ge(ye_ready, j + 1)
                        pe.wait_ge(W_low_ready, j * PIECES + PIECES)
                        for t in range(TB):
                            for m in range(FC):
                                if t == 0:
                                    pe.wait_ge(act_ready, j * FC + m + 5)
                                for n, (w, x) in enumerate(PASSES):
                                    last = pe.matmul(ps[:, 5, t * D:(t + 1) * D],
                                                     act_parts[x][:, m, t * P:(t + 1) * P],
                                                     W_parts[w][:, u, DC, m * D:(m + 1) * D],
                                                     start=(m + n == 0), stop=(m == FC - 1 and n == 2))
                        last.then_inc(out_full, 1)

                    turn(0, 0, 0)
                    with pe.Fori(0, PAIRS) as i:
                        for u in range(2):
                            mlp(i * 2 + u, i, u)
                    mlp(NB - 1, PAIRS, 0)

                @block.scalar
                def _(act):
                    def evacuate(j):
                        act.wait_ge(turned, j + 1)
                        act.activation(xeT_parts[0][:, :, :], ps[:, 7, :].rearrange("p (c n) -> p c n", c=DC),
                                       ACT.Copy).then_inc(xeT_high_ready, 1)

                    def weights_high(j, p, u):
                        act.wait_ge(raw_in[p], j * 16 + 16)
                        act.activation(W_parts[0][:, u, p, :], raw[:, p, :], ACT.Copy).then_inc(W_high_ready, 1)

                    def mlp(j, i, u, last=False):
                        for m in range(FC):
                            if m in (2, 4, 6) and not last:
                                weights_high(j + 1, m // 2 - 1, 1 - u)
                            act.wait_ge(gated_full, j * FC + m + 1)
                            act.wait_ge(act_ready, j * FC + m + 3)
                            act.activation(sg[:, m % 2, :], ps[:, m % 4, 0:BLOCK], ACT.Sigmoid).then_inc(sg_ready, 1)
                        evacuate(j + 1)
                        act.wait_ge(out_full, j + 1)
                        act.wait_ge(stored[u], i * 16 + 16)
                        act.activation(ye[:, u, :, :], ps[:, 5, :].rearrange("p (t d) -> p t d", t=TB),
                                       ACT.Copy).then_inc(ye_ready, 1)

                    act.sem_inc(ye_ready, 1)
                    for u in range(2):
                        act.sem_inc(stored[u], 16)
                    evacuate(0)
                    for p in range(PIECES):
                        weights_high(0, p, 0)
                    with act.Fori(0, PAIRS) as i:
                        for u in range(2):
                            mlp(i * 2 + u, i, u)
                    mlp(NB - 1, PAIRS, 0, last=True)

                @block.vector
                def _(dve):
                    def low(j):
                        dve.wait_ge(xeT_high_ready, j + 1)
                        dve.tensor_tensor(xeT_parts[1][:, :, :], ps[:, 7, :].rearrange("p (c n) -> p c n", c=DC),
                                          xeT_parts[0][:, :, :].bitcast(F32), ALU.subtract).then_inc(xeT_ready, 1)

                    def mlp(j):
                        for m in range(FC):
                            dve.wait_ge(sg_ready, j * FC + m + 1)
                            dve.tensor_tensor(sg[:, m % 2, :], sg[:, m % 2, :], ps[:, m % 4, 0:BLOCK],
                                              ALU.mult).then_inc(swish_ready, 1)
                            dve.wait_ge(swish_ready, j * FC + m + 1)
                            dve.tensor_tensor(act_[:, m % 2, :], sg[:, m % 2, :], ps[:, m % 4, BLOCK:2 * BLOCK],
                                              ALU.mult).then_inc(product_ready, 1)
                            dve.wait_ge(product_ready, j * FC + m + 1)
                            dve.tensor_copy(act_parts[0][:, m, :], act_[:, m % 2, :]).then_inc(act_high_ready, 1)
                            dve.wait_ge(act_high_ready, j * FC + m + 1)
                            dve.tensor_tensor(act_parts[1][:, m, :], act_[:, m % 2, :],
                                              act_parts[0][:, m, :].bitcast(F32), ALU.subtract).then_inc(act_ready, 1)

                    dve.sem_inc(act_ready, 4)
                    low(0)
                    with dve.Fori(0, NB) as j:
                        mlp(j)
                        low(j + 1)

        with ExitStack() as ctx_d:
            sd = Scope(nc, ctx_d, "tmoe_combine", s)
            y = sd.sb("y", [P, TILES, D])
            y_in = [core.pool_dma.sem(f"tmoe_y_in{t}") for t in range(4)]
            added = sd.sem("added")
            with nc.Block() as block:
                @block.gpsimd
                def _(pool):
                    for t in range(TILES):
                        pool.indirect_dma_start(y[:, t, :], None, OUTS,
                                                bass.IndirectOffsetOnAxis(ap=row_of[:, t:t + 1], axis=0)
                                                ).then_inc(y_in[t // 4], 16)

                @block.vector
                def _(dve):
                    for g in range(4):
                        dve.wait_ge(y_in[g], 16 * 4)
                        for t in range(4 * g, 4 * g + 4):
                            dve.scalar_tensor_tensor(out=h[:, t, :], in0=y[:, t, :], scalar=r.top[0][:, t:t + 1],
                                                     in1=h[:, t, :], op0=ALU.mult, op1=ALU.add).then_inc(added, 1)
        s.clear()


def row_attention(nc, core, Wqkv_d, bq_d, bk_d, bv_d, Wproj_d, bproj_d):
    ps, xT, h = core.ps, core.xT, core.h
    H, HD = 16, 16
    UH = 4
    UNITS = TPB * H // UH
    PER_CHUNK = P // HD
    SCALE = 1.0 / float(np.sqrt(HD))
    JOBS = ["mix0", "mix1", "k0", "mix2", "k1", "mix3", "q", "mix4", "outT0", "mix5", "proj0", "mix6", "mix7", "v",
            "outT1", "proj1"]
    BY_ACT = [j for j in JOBS if j[0] in "okq"]
    BY_DVE = [j for j in JOBS if j not in BY_ACT]
    with ExitStack() as ctx:
        s = Scope(nc, ctx, "rattn")
        Wqkv = s.sb("Wqkv", [P, DC, 3 * D])
        Wproj = s.sb("Wproj", [P, DC, D])
        bq = s.sb("bq", [P, DC])
        bk = s.sb("bk", [P, DC])
        bv = s.sb("bv", [P, D])
        bproj = s.sb("bproj", [P, D])
        mask = s.sb("mask", [P, PER_CHUNK])
        qT = s.sb("qT", [P, 2, DC, SEQ])
        kT = s.sb("kT", [P, DC, SEQ])
        keys = s.sb("keys", [P, 2, H, SEQ])
        v = s.sb("v", [P, TPB, H, HD + 1])
        probs = s.sb("probs", [P, 4, UH, SEQ])
        probsT = s.sb("probsT", [P, 2, UH * TPB, P])
        peak = s.sb("peak", [P, 2, UH])
        inverse = s.sb("inverse", [P, 2, UH])
        out = s.sb("out", [P, TPB, D])
        outT = s.sb("outT", [P, TPB, DC, P])
        weights_in = s.sem("weights_in")
        mask_step = s.sem("mask_step")
        keys_ready = s.sem("keys_ready")
        ones_set = s.sem("ones_set")
        scores_full = s.sem("scores_full")
        peak_ready = s.sem("peak_ready")
        shifted = s.sem("shifted")
        exped = s.sem("exped")
        turned = s.sem("turned")
        probsT_ready = s.sem("probsT_ready")
        inverse_ready = s.sem("inverse_ready")
        job_full = s.sem("job_full")
        act_read = s.sem("act_read")
        dve_read = s.sem("dve_read")
        product_added = s.sem("product_added")
        row = RowNorm(nc, core, s)

        def bank(name):
            return 6 + JOBS.index(name) % 2

        def full(name, b):
            return b * len(JOBS) + (4 + JOBS.index(name) + 1)

        def act_count(name, b):
            return b * len(BY_ACT) + (len(BY_ACT) + BY_ACT.index(name) + 1)

        def dve_count(name, b):
            return b * len(BY_DVE) + (len(BY_DVE) + BY_DVE.index(name) + 1)

        with nc.Block() as block:
            @block.sync
            def _(sp):
                sp.dma_start(Wqkv[:, :, :], Wqkv_d.rearrange("(c p) n -> p c n", p=P)).then_inc(weights_in, 16)
                sp.dma_start(bq[:, :], bq_d).then_inc(weights_in, 16)
                sp.dma_start(bk[:, :], bk_d).then_inc(weights_in, 16)
                sp.dma_start(bv[:, :], bv_d.partition_broadcast(P)).then_inc(weights_in, 16)
                sp.dma_start(bproj[:, :], bproj_d.partition_broadcast(P)).then_inc(weights_in, 16)
                sp.dma_start(Wproj[:, :, :], Wproj_d.rearrange("(c p) n -> p c n", p=P)).then_inc(weights_in, 16)

            @block.gpsimd
            def _(pool):
                step = Chain(pool, mask_step)
                step(pool.memset(mask[:, :], 1.0))
                step(pool.affine_select(out=mask[:, :], in_=mask[:, :], compare_op=ALU.is_ge, fill=0.0, base=0,
                                        pattern=[[-HD, PER_CHUNK]], channel_multiplier=1))
                step(pool.affine_select(out=mask[:, :], in_=mask[:, :], compare_op=ALU.is_ge, fill=0.0, base=HD - 1,
                                        pattern=[[HD, PER_CHUNK]], channel_multiplier=-1))
                pool.memset(v[:, :, :, HD:HD + 1], 1.0).then_inc(ones_set, 1)

                def spread_keys(b, u):
                    for m in range(DC):
                        pool.wait_ge(act_read, act_count(f"k{m}", b))
                        pool.tensor_tensor(keys[:, u, m * PER_CHUNK:(m + 1) * PER_CHUNK, :],
                                           kT[:, m, :].unsqueeze(1).broadcast_to([P, PER_CHUNK, SEQ]),
                                           mask[:, :].unsqueeze(2).broadcast_to([P, PER_CHUNK, SEQ]),
                                           ALU.mult).then_inc(keys_ready, 1)

                row.root(pool, 0)
                pool.wait_ge(mask_step, 3)
                spread_keys(-1, 0)
                with pool.Fori(0, BATCH // 2) as i:
                    for u in range(2):
                        row.root(pool, i * 2 + u + 1)
                        spread_keys(i * 2 + u, 1 - u)

            @block.tensor
            def _(pe):
                def bank_free(name, b):
                    q = JOBS.index(name)
                    before = JOBS[q - 2]
                    if q < 2:
                        b = b - 1
                    if before in BY_ACT:
                        pe.wait_ge(act_read, act_count(before, b))
                    else:
                        pe.wait_ge(dve_read, dve_count(before, b))

                def scores(k, b, w):
                    u, c, x = k // (H // UH), k % (H // UH) // 2, 2 * (k % 2)
                    pe.wait_ge(shifted, b * UNITS + k + 1)
                    for i in range(2):
                        head = k % (H // UH) * UH + 2 * i
                        last = pe.matmul(ps[:, x + i, :], qT[:, w, c, u * P:(u + 1) * P],
                                         keys[:, w, head:head + 2, :].rearrange("p h n -> p (h n)"),
                                         start=True, stop=True)
                    last.then_inc(scores_full, 1)

                def turn_probs(k, b):
                    pe.wait_ge(exped, b * UNITS + k + 1)
                    pe.wait_ge(probsT_ready, b * UNITS + k + 1)
                    for i in range(UH):
                        for t in range(TPB):
                            n = i * TPB + t
                            last = pe.transpose(ps[:, 4 + n // 4, n % 4 * P:(n % 4 + 1) * P],
                                                probs[:, k % 4, i, t * P:(t + 1) * P], core.ident[:, :])
                    last.then_inc(turned, 1)

                def mix(k, b):
                    bank_free(f"mix{k}", b)
                    pe.wait_ge(probsT_ready, b * UNITS + k + 2)
                    for i in range(UH):
                        head = k % (H // UH) * UH + i
                        for t in range(TPB):
                            last = pe.matmul(ps[:, bank(f"mix{k}"), i * (HD + 1):(i + 1) * (HD + 1)],
                                             probsT[:, k % 2, i * TPB + t, :], v[:, t, head, :],
                                             start=(t == 0), stop=(t == TPB - 1))
                    last.then_inc(job_full, 1)

                def out_turn(u, b):
                    pe.wait_ge(dve_read, dve_count(f"mix{4 * u + 3}", b))
                    bank_free(f"outT{u}", b)
                    for c in range(DC):
                        last = pe.transpose(ps[:, bank(f"outT{u}"), c * P:(c + 1) * P], out[:, u, c * P:(c + 1) * P],
                                            core.ident[:, :])
                    last.then_inc(job_full, 1)

                def project(u, b):
                    pe.wait_ge(act_read, act_count(f"outT{u}", b))
                    bank_free(f"proj{u}", b)
                    for c in range(DC):
                        last = pe.matmul(ps[:, bank(f"proj{u}"), 0:D], outT[:, u, c, :], Wproj[:, c, :],
                                         start=(c == 0), stop=(c == DC - 1))
                    last.then_inc(job_full, 1)

                def queries():
                    for m in range(DC):
                        for c in range(DC):
                            last = pe.matmul(ps[:, bank("q"), m * SEQ:(m + 1) * SEQ], Wqkv[:, c, m * P:(m + 1) * P],
                                             xT[:, c, :], start=(c == 0), stop=(c == DC - 1))
                    last.then_inc(job_full, 1)

                def key_chunk(m):
                    for c in range(DC):
                        last = pe.matmul(ps[:, bank(f"k{m}"), 0:SEQ], Wqkv[:, c, D + m * P:D + (m + 1) * P],
                                         xT[:, c, :], start=(c == 0), stop=(c == DC - 1))
                    last.then_inc(job_full, 1)

                def values():
                    for t in range(TPB):
                        for c in range(DC):
                            last = pe.matmul(ps[:, bank("v"), t * D:(t + 1) * D], xT[:, c, t * P:(t + 1) * P],
                                             Wqkv[:, c, 2 * D:3 * D], start=(c == 0), stop=(c == DC - 1))
                    last.then_inc(job_full, 1)

                row.turn(pe, 0)
                pe.wait_ge(weights_in, 96)
                pe.wait_ge(row.xT_ready, 1)
                key_chunk(0)
                pe.wait_ge(act_read, act_count("k0", -1))
                key_chunk(1)
                pe.wait_ge(act_read, act_count("k1", -1))
                queries()
                values()
                pe.wait_ge(ones_set, 1)
                pe.wait_ge(act_read, act_count("q", -1))
                pe.wait_ge(keys_ready, DC)
                scores(0, 0, 0)
                scores(1, 0, 0)
                with pe.Fori(0, BATCH // 2) as i:
                    for u in range(2):
                        b = i * 2 + u
                        scores(2, b, u)
                        turn_probs(0, b)
                        scores(3, b, u)
                        turn_probs(1, b)
                        pe.wait_ge(dve_read, dve_count("v", b - 1))
                        mix(0, b)
                        row.turn(pe, b + 1)
                        scores(4, b, u)
                        turn_probs(2, b)
                        pe.wait_ge(row.xT_ready, b + 2)
                        mix(1, b)
                        for m in range(DC):
                            bank_free(f"k{m}", b)
                            key_chunk(m)
                            scores(5 + m, b, u)
                            turn_probs(3 + m, b)
                            mix(2 + m, b)
                        bank_free("q", b)
                        queries()
                        scores(7, b, u)
                        turn_probs(5, b)
                        mix(4, b)
                        out_turn(0, b)
                        pe.wait_ge(act_read, act_count("q", b))
                        pe.wait_ge(keys_ready, (b + 2) * DC)
                        scores(0, b + 1, 1 - u)
                        turn_probs(6, b)
                        mix(5, b)
                        project(0, b)
                        scores(1, b + 1, 1 - u)
                        turn_probs(7, b)
                        mix(6, b)
                        mix(7, b)
                        bank_free("v", b)
                        values()
                        out_turn(1, b)
                        project(1, b)

            @block.scalar
            def _(act):
                def read_q(b, w):
                    act.wait_ge(job_full, full("q", b))
                    for m in range(DC):
                        ins = act.activation(qT[:, w, m, :], ps[:, bank("q"), m * SEQ:(m + 1) * SEQ], ACT.Identity,
                                             bias=bq[:, m:m + 1])
                    ins.then_inc(act_read, 1)

                def read_k(m, b):
                    act.wait_ge(job_full, full(f"k{m}", b))
                    act.activation(kT[:, m, :], ps[:, bank(f"k{m}"), 0:SEQ], ACT.Identity,
                                   bias=bk[:, m:m + 1]).then_inc(act_read, 1)

                def exp(k, b):
                    act.wait_ge(shifted, b * UNITS + k + 3)
                    act.activation(probs[:, k % 4, :, :], probs[:, k % 4, :, :], ACT.Exp,
                                   scale=SCALE).then_inc(exped, 1)

                def read_probsT(k, b):
                    act.wait_ge(turned, b * UNITS + k + 1)
                    act.activation(probsT[:, k % 2, :, :].rearrange("p (x i) n -> p x (i n)", x=2), ps[:, 4:6, :],
                                   ACT.Copy).then_inc(probsT_ready, 1)

                def read_outT(u, b):
                    act.wait_ge(job_full, full(f"outT{u}", b))
                    act.activation(outT[:, u, :, :], ps[:, bank(f"outT{u}"), 0:D].rearrange("p (c n) -> p c n", c=DC),
                                   ACT.Copy).then_inc(act_read, 1)

                act.sem_inc(probsT_ready, 1)
                row.evacuate(act, 0)
                act.wait_ge(weights_in, 96)
                for m in range(DC):
                    act.wait_ge(job_full, 1 + m)
                    act.activation(kT[:, m, :], ps[:, bank(f"k{m}"), 0:SEQ], ACT.Identity,
                                   bias=bk[:, m:m + 1]).then_inc(act_read, 1)
                act.wait_ge(job_full, 3)
                for m in range(DC):
                    ins = act.activation(qT[:, 0, m, :], ps[:, bank("q"), m * SEQ:(m + 1) * SEQ], ACT.Identity,
                                         bias=bq[:, m:m + 1])
                ins.then_inc(act_read, 1)
                act.wait_ge(act_read, act_count("q", -1))
                act.sem_inc(act_read, 2)
                exp(0, 0)
                exp(1, 0)
                with act.Fori(0, BATCH // 2) as i:
                    for u in range(2):
                        b = i * 2 + u
                        for k in range(2):
                            read_probsT(k, b)
                            exp(k + 2, b)
                        row.evacuate(act, b + 1)
                        for m in range(DC):
                            read_probsT(2 + m, b)
                            read_k(m, b)
                            exp(4 + m, b)
                        read_probsT(4, b)
                        read_q(b, 1 - u)
                        exp(6, b)
                        read_probsT(5, b)
                        exp(7, b)
                        read_outT(0, b)
                        read_probsT(6, b)
                        exp(0, b + 1)
                        read_probsT(7, b)
                        exp(1, b + 1)
                        read_outT(1, b)

            @block.vector
            def _(dve):
                def shift(k, b):
                    n = b * UNITS + k
                    x = k % 2
                    scores = ps[:, 2 * x:2 * x + 2, :].rearrange("p x (i n) -> p (x i) n", i=2)
                    dve.wait_ge(scores_full, n + 1)
                    dve.tensor_reduce(peak[:, x, :], scores, AX_X, ALU.max).then_inc(peak_ready, 1)
                    dve.wait_ge(peak_ready, n + 1)
                    dve.tensor_tensor(probs[:, k % 4, :, :], scores, peak[:, x, :].unsqueeze(2).broadcast_to([P, UH, SEQ]),
                                      ALU.subtract).then_inc(shifted, 1)

                def read_mix(k, b):
                    u, first = k // (H // UH), k % (H // UH) * UH
                    dve.wait_ge(job_full, full(f"mix{k}", b))
                    mixed = ps[:, bank(f"mix{k}"), 0:UH * (HD + 1)].rearrange("p (h d) -> p h d", d=HD + 1)
                    dve.reciprocal(inverse[:, k % 2, :], mixed[:, :, HD]).then_inc(inverse_ready, 1)
                    dve.wait_ge(inverse_ready, b * UNITS + k + 1)
                    dve.tensor_tensor(out[:, u, first * HD:(first + UH) * HD].rearrange("p (h d) -> p h d", d=HD),
                                      mixed[:, :, 0:HD], inverse[:, k % 2, :].unsqueeze(2).broadcast_to([P, UH, HD]),
                                      ALU.mult).then_inc(dve_read, 1)

                def read_v(ready):
                    dve.wait_ge(job_full, ready)
                    for t in range(TPB):
                        ins = dve.tensor_tensor(v[:, t, :, 0:HD],
                                                ps[:, bank("v"), t * D:(t + 1) * D].rearrange("p (h d) -> p h d", d=HD),
                                                bv[:, :].rearrange("p (h d) -> p h d", d=HD), ALU.add)
                    ins.then_inc(dve_read, 1)

                def add(u, b):
                    dve.wait_ge(job_full, full(f"proj{u}", b))
                    dve.tensor_tensor(h[:, ds(b * TPB + u, 1), :], ps[:, bank(f"proj{u}"), 0:D],
                                      h[:, ds(b * TPB + u, 1), :], ALU.add).then_inc(dve_read, 1)
                    dve.wait_ge(dve_read, dve_count(f"proj{u}", b))
                    dve.tensor_tensor(h[:, ds(b * TPB + u, 1), :], h[:, ds(b * TPB + u, 1), :], bproj[:, :],
                                      ALU.add).then_inc(product_added, 1)

                dve.sem_inc(shifted, 2)
                dve.sem_inc(dve_read, BY_DVE.index("v"))
                row.norm(dve, 0, first=True)
                dve.wait_ge(weights_in, 96)
                read_v(4)
                dve.wait_ge(dve_read, dve_count("v", -1))
                dve.sem_inc(dve_read, 1)
                shift(0, 0)
                shift(1, 0)
                with dve.Fori(0, BATCH // 2) as i:
                    for u in range(2):
                        b = i * 2 + u
                        shift(2, b)
                        row.norm(dve, b + 1)
                        shift(3, b)
                        for k in range(4):
                            read_mix(k, b)
                            shift(k + 4, b)
                        read_mix(4, b)
                        shift(0, b + 1)
                        read_mix(5, b)
                        add(0, b)
                        shift(1, b + 1)
                        read_mix(6, b)
                        read_mix(7, b)
                        read_v(full("v", b))
                        add(1, b)
        s.clear()


def swiglu(nc, core, Wg_d, Wu_d, Wd_d, out_d):
    ps, h = core.ps, core.h
    F = Wg_d.shape[1]
    FC = F // P
    SCALE = float(np.float32(1.0 / 127.0))
    with ExitStack() as ctx:
        s = Scope(nc, ctx, "swi")
        Wg_int = s.sb("Wg_int", [P, DC, F], I32)
        Wu_int = s.sb("Wu_int", [P, DC, F], I32)
        Wd_int = s.sb("Wd_int", [P, FC, D], I32)
        W = s.sb("W", [P, DC * F])
        GATE, UP, DOWN = 0, 1, 2
        assert DC * F == FC * D
        W_parts = [s.sb(f"W_{n}", [P, 3, DC * F], F32R) for n in ("high", "low")]
        x_parts = [s.sb(f"x_{n}", [P, DC, SEQ], F32R) for n in ("high", "low")]
        sg = s.sb("sg", [P, 2, SEQ])
        act_ = s.sb("act", [P, 3, SEQ])
        act_parts = [s.sb(f"act_{n}", [P, FC, SEQ], F32R) for n in ("high", "low")]
        int_in = s.sem("int_in")
        W_ready = s.sem("W_ready")
        W_high_ready = s.sem("W_high_ready")
        weights_ready = s.sem("weights_ready")
        gated_full = s.sem("gated_full")
        sg_ready = s.sem("sg_ready")
        swish_ready = s.sem("swish_ready")
        product_ready = s.sem("product_ready")
        act_high_ready = s.sem("act_high_ready")
        act_ready = s.sem("act_ready")
        out_full = s.sem("out_full")
        row_added = s.sem("row_added")
        stored = s.sem("stored")
        row = RowNorm(nc, core, s)

        with nc.Block() as block:
            @block.sync
            def _(sp):
                for W_int, W_d in ((Wg_int, Wg_d), (Wu_int, Wu_d), (Wd_int, Wd_d)):
                    sp.dma_start(W_int[:, :, :], W_d.rearrange("(c p) n -> p c n", p=P)).then_inc(int_in, 16)
                with sp.Fori(0, BATCH) as b:
                    sp.wait_ge(row_added, b + 2)
                    sp.dma_start(out_d[ds(b, 1), :, :].rearrange("b (t p) d -> p (b t) d", p=P),
                                 h[:, ds(b * TPB, TPB), :]).then_inc(stored, 16)
                sp.wait_ge(stored, 16 * BATCH)

            @block.tensor
            def _(pe):
                row.turn(pe, 0)
                pe.wait_ge(weights_ready, 3)
                with pe.Fori(0, BATCH) as b:
                    pe.wait_ge(row.low_ready, b + 1)
                    for m in range(FC):
                        pe.wait_ge(product_ready, b * FC + (4 if m < 4 else m + 1))
                        for half, piece in ((0, GATE), (1, UP)):
                            terms = [(c, w, x) for c in range(DC) for w, x in PASSES]
                            for n, (c, w, x) in enumerate(terms):
                                last = pe.matmul(ps[:, m % 4, half * SEQ:(half + 1) * SEQ],
                                                 W_parts[w][:, piece, c * F + m * P:c * F + (m + 1) * P],
                                                 x_parts[x][:, c, :], start=(n == 0), stop=(n == len(terms) - 1))
                        last.then_inc(gated_full, 1)
                    row.turn(pe, b + 1)
                    pe.wait_ge(row_added, b + 1)
                    for t in range(TPB):
                        for m in range(FC):
                            if t == 0:
                                pe.wait_ge(act_ready, b * FC + m + 1)
                            for n, (w, x) in enumerate(PASSES):
                                last = pe.matmul(ps[:, 5, t * D:(t + 1) * D], act_parts[x][:, m, t * P:(t + 1) * P],
                                                 W_parts[w][:, DOWN, m * D:(m + 1) * D],
                                                 start=(m + n == 0), stop=(m == FC - 1 and n == 2))
                    last.then_inc(out_full, 1)

            @block.scalar
            def _(act):
                row.evacuate(act, 0, x_parts[0][:, :, :])

                def high(b, m):
                    act.wait_ge(product_ready, b * FC + m + 5)
                    act.activation(act_parts[0][:, m, :], act_[:, m % 3, :], ACT.Copy).then_inc(act_high_ready, 1)

                with act.Fori(0, BATCH) as b:
                    for m in range(FC):
                        act.wait_ge(gated_full, b * FC + m + 1)
                        act.wait_ge(product_ready, b * FC + m + 3)
                        act.activation(sg[:, m % 2, :], ps[:, m % 4, 0:SEQ], ACT.Sigmoid).then_inc(sg_ready, 1)
                        if m > 0:
                            high(b, m - 1)
                    high(b, FC - 1)
                    row.evacuate(act, b + 1, x_parts[0][:, :, :])

            @block.gpsimd
            def _(pool):
                row.root(pool, 0)
                with pool.Fori(0, BATCH) as b:
                    row.root(pool, b + 1)

            @block.vector
            def _(dve):
                dve.sem_inc(product_ready, 4)
                dve.sem_inc(row_added, 1)
                row.norm(dve, 0, first=True)
                dve.wait_ge(int_in, 48)
                row.low(dve, 0, *x_parts)
                for p, W_int in enumerate((Wg_int, Wu_int, Wd_int)):
                    high, low = (part[:, p, :] for part in W_parts)
                    dve.tensor_scalar(W[:, :], W_int[:, :, :].rearrange("p c n -> p (c n)"), SCALE, None,
                                      ALU.mult).then_inc(W_ready, 1)
                    dve.wait_ge(W_ready, p + 1)
                    dve.tensor_copy(high, W[:, :]).then_inc(W_high_ready, 1)
                    dve.wait_ge(W_high_ready, p + 1)
                    dve.tensor_tensor(low, W[:, :], high.bitcast(F32), ALU.subtract).then_inc(weights_ready, 1)
                    dve.wait_ge(weights_ready, p + 1)

                def low(b, m):
                    dve.wait_ge(act_high_ready, b * FC + m + 1)
                    dve.tensor_tensor(act_parts[1][:, m, :], act_[:, m % 3, :], act_parts[0][:, m, :].bitcast(F32),
                                      ALU.subtract).then_inc(act_ready, 1)

                with dve.Fori(0, BATCH) as b:
                    for m in range(FC):
                        if m == 1:
                            row.norm(dve, b + 1)
                        dve.wait_ge(sg_ready, b * FC + m + 1)
                        dve.tensor_tensor(sg[:, m % 2, :], sg[:, m % 2, :], ps[:, m % 4, 0:SEQ],
                                          ALU.mult).then_inc(swish_ready, 1)
                        dve.wait_ge(swish_ready, b * FC + m + 1)
                        dve.tensor_tensor(act_[:, m % 3, :], sg[:, m % 2, :], ps[:, m % 4, SEQ:2 * SEQ],
                                          ALU.mult).then_inc(product_ready, 1)
                        if m > 0:
                            low(b, m - 1)
                    low(b, FC - 1)
                    row.low(dve, b + 1, *x_parts)
                    dve.wait_ge(out_full, b + 1)
                    dve.tensor_tensor(h[:, ds(b * TPB, TPB), :], ps[:, 5, :].rearrange("p (t d) -> p t d", t=TPB),
                                      h[:, ds(b * TPB, TPB), :], ALU.add).then_inc(row_added, 1)


def tower(nc, a, out_d):
    with ExitStack() as ctx:
        core = Core(nc, ctx)
        constants(nc, core)
        embed(nc, core, a["ids"], a["L0_tok_E1"], a["L0_tok_W2T"], a["L0_tok_b2"], a["L0_tok_pos_emb"])
        linear_attention(nc, core, a["L0_attn_Wqkv"], a["L0_attn_bq"], a["L0_attn_bkv"], a["L0_attn_Wout"],
                         a["L0_attn_bout"])
        with ExitStack() as ctx_z:
            F = a["L1_attn_Wz"].shape[0]
            gates = Scope(nc, ctx_z, "gates")
            Wz_parts = [gates.sb(f"Wz_{n}", [P, F // P, F], F32R) for n in ("high", "low")]
            sign_ffn(nc, core, a["L0_ffn_k0"], a["L0_ffn_k1"], a["L0_ffn_k2"], a["L0_ffn_s"], a["L1_attn_Wz"],
                     Wz_parts)
            min_gru(nc, core, Wz_parts, *(a[f"L1_attn_{k}"] for k in ("W1", "b1", "W2", "b2", "bz", "Wh", "bh",
                                                                      "Wo", "bo")))
        E = a["L1_ffn_w_gate"].shape[0]
        C = capacity(E)
        rows = nc.dram_tensor("moe_rows", (spare_rows(E, C) + 2 * N, D), F32, kind="Internal").ap()
        outs = nc.dram_tensor("moe_outs", (E * C, D), F32, kind="Internal").ap()
        capacity_moe(nc, core, *(a[f"L1_ffn_{k}"] for k in ("router_w", "router_b", "w_gate", "w_up", "w_down",
                                                            "sw_gate", "sw_up", "sw_down")), rows, outs)
        column_attention(nc, core, a["L2_attn_ln"], a["L2_attn_qkv_kernel"], a["L2_attn_out_kernel"])
        E2 = a["L2_ffn_w1"].shape[0]
        rows = nc.dram_tensor("top1_rows", ((top1_blocks(E2) + 1) * BLOCK, D), F32, kind="Internal").ap()
        outs = nc.dram_tensor("top1_outs", (top1_blocks(E2) * BLOCK, D), F32, kind="Internal").ap()
        top1_moe(nc, core, a["L2_ffn_router_w"], a["L2_ffn_router_b"], a["L2_ffn_w1"], a["L2_ffn_w2"], rows, outs)
        row_attention(nc, core, *(a[f"L3_attn_{k}"] for k in ("w_qkv", "bq", "bk", "bv", "w_proj", "b_proj")))
        swiglu(nc, core, a["L3_ffn_w_gateT"], a["L3_ffn_w_upT"], a["L3_ffn_w_downT"], out_d)


def columns(v):
    return np.ascontiguousarray(v.reshape(-1, P).T)


def pad_rows(v):
    pad = [(0, 0)] * v.ndim
    pad[-2] = (0, -v.shape[-2] % P)
    return np.pad(v, pad)


def lay_out(x, w):
    a = {"ids": np.ascontiguousarray(x.reshape(TILES, P).T)}
    for k in ("L0_tok_E1", "L0_tok_b2", "L0_tok_pos_emb", "L0_attn_Wqkv", "L0_attn_Wout", "L0_attn_bout"):
        a[k] = w[k]
    a["L0_tok_W2T"] = w["L0_tok_W2"].T
    a["L0_attn_bq"] = columns(w["L0_attn_bqkv"][:D])
    a["L0_attn_bkv"] = w["L0_attn_bqkv"][D:]
    for k in ("L0_ffn_k0", "L0_ffn_k1", "L0_ffn_k2"):
        a[k] = w[k].view(np.int32)
    a["L0_ffn_s"] = np.stack([w["L0_ffn_s0"], w["L0_ffn_s1"], w["L0_ffn_s2"]])
    for k in ("W1", "W2", "Wz", "Wh", "Wo", "bo"):
        a[f"L1_attn_{k}"] = w[f"L1_attn_{k}"]
    for k in ("b1", "b2", "bz", "bh"):
        a[f"L1_attn_{k}"] = columns(w[f"L1_attn_{k}"])
    for k in ("router_w", "router_b", "w_gate", "w_up", "sw_gate", "sw_up"):
        a[f"L1_ffn_{k}"] = w[f"L1_ffn_{k}"]
    a["L1_ffn_w_down"] = pad_rows(w["L1_ffn_w_down"])
    a["L1_ffn_sw_down"] = pad_rows(w["L1_ffn_sw_down"])
    a["L2_attn_ln"] = np.stack([columns(w["L2_attn_ln_scale"]), columns(w["L2_attn_ln_bias"])], axis=1)
    a["L2_attn_qkv_kernel"] = w["L2_attn_qkv_kernel"].reshape(D, -1)
    a["L2_attn_out_kernel"] = w["L2_attn_out_kernel"]
    for k in ("L2_ffn_router_w", "L2_ffn_router_b", "L2_ffn_w1", "L2_ffn_w2", "L3_attn_w_qkv", "L3_attn_w_proj",
              "L3_attn_b_proj"):
        a[k] = w[k]
    a["L3_attn_bq"], a["L3_attn_bk"] = columns(w["L3_attn_b_qkv"][:D]), columns(w["L3_attn_b_qkv"][D:2 * D])
    a["L3_attn_bv"] = w["L3_attn_b_qkv"][2 * D:]
    for k in ("w_gate", "w_up", "w_down"):
        a[f"L3_ffn_{k}T"] = w[f"L3_ffn_{k}"].T
    return {k: np.ascontiguousarray(v) for k, v in a.items()}


def kernel(**inputs):
    import concourse.bacc as bacc
    from concourse.bass_utils import run_bass_kernel_spmd

    w = {k: np.asarray(v) for k, v in inputs.items()}
    arrays = lay_out(w.pop("x"), w)
    nc = bacc.Bacc("TRN2", target_bir_lowering=False, num_devices=1)
    aps = {k: nc.dram_tensor(f"in_{k}", v.shape, mybir.dt.from_np(v.dtype), kind="ExternalInput").ap()
           for k, v in arrays.items()}
    out = nc.dram_tensor("out_h", (BATCH, SEQ, D), F32, kind="ExternalOutput").ap()
    tower(nc, aps, out)
    r = run_bass_kernel_spmd(nc, [{f"in_{k}": v for k, v in arrays.items()}], core_ids=[0])
    return r.results[0]["out_h"]
```
